# Optimizing a Trainium2 kernel written in Bass

```python
import numpy as np
import jax
import jax.numpy as jnp

def _softmax(x, axis=-1):
    return jax.nn.softmax(x, axis=axis)

def _gelu(x):
    return jax.nn.gelu(x, approximate=True)

def _silu(x):
    return jax.nn.silu(x)

def _sigmoid(x):
    return jax.nn.sigmoid(x)

def _layernorm(x, axis=-1, eps=1e-05):
    m = jnp.mean(x, axis=axis, keepdims=True)
    v = jnp.var(x, axis=axis, keepdims=True)
    return (x - m) / jnp.sqrt(v + eps)

def _scatter_add(tgt, idx, src, axis=0):
    return tgt.at[idx].add(src)

def _segment_sum(src, seg, n):
    return jax.ops.segment_sum(src, seg, n)
kernel_name = 'mk_seq_preln_d1_jaxref_r8_d3a063'

def setup_inputs(seed: int=0):
    np.random.seed(seed)
    _w = jnp.asarray

    def _L0_attn_setup():
        import jax, jax.numpy as jnp
        import numpy as np
        EPS = 1e-06
        CHUNK = 64
        GATE_LOGIT_NORMALIZER = 16.0
        NUM_HEADS = 4

        def _rms(x, w):
            return x * jax.lax.rsqrt(jnp.mean(x * x, axis=-1, keepdims=True) + EPS) * w

        def _gla_chunk(q, k, v, glog, num_heads):
            B, T, Dk = q.shape
            Dv = v.shape[-1]
            dk, dv = (Dk // num_heads, Dv // num_heads)
            Nc = T // CHUNK

            def split(x, d):
                return x.reshape(B, T, num_heads, d).transpose(0, 2, 1, 3).reshape(B, num_heads, Nc, CHUNK, d)
            q, k, v, g = (split(q, dk), split(k, dk), split(v, dv), split(glog, dk))
            b = jnp.cumsum(g, axis=3)
            scale = dk ** (-0.5)
            qe = q * jnp.exp(b) * scale
            mask = jnp.tril(jnp.ones((CHUNK, CHUNK), dtype=bool))
            A = jnp.einsum('bhncd,bhnsd->bhncs', qe, k * jnp.exp(-b))
            A = jnp.where(mask, A, 0.0)
            o_intra = jnp.einsum('bhncs,bhnsd->bhncd', A, v)

            def step(S, xs):
                qe_c, k_c, v_c, b_c = xs
                blast = b_c[:, :, -1, :]
                o_inter = jnp.einsum('bhcd,bhde->bhce', qe_c, S)
                kd = k_c * jnp.exp(blast[:, :, None, :] - b_c)
                S_new = S * jnp.exp(blast)[..., None] + jnp.einsum('bhcd,bhce->bhde', kd, v_c)
                return (S_new, o_inter)
            S0 = jnp.zeros((B, num_heads, dk, dv), q.dtype)
            xs = tuple((jnp.moveaxis(t, 2, 0) for t in (qe, k, v, b)))
            _, o_inter = jax.lax.scan(step, S0, xs)
            o = o_intra + jnp.moveaxis(o_inter, 0, 2)
            return o.reshape(B, num_heads, T, dv).transpose(0, 2, 1, 3)
        key = jax.random.key(seed)
        ks = jax.random.split(key, 12)
        B, T, Hs = (4, 256, 128)
        Dk, Dv, I, R = (64, 128, 352, 16)
        p = lambda k, s: jax.random.normal(k, s, jnp.float32) * 0.02
        return {'hidden_states': jax.random.normal(ks[0], (B, T, Hs), jnp.float32), 'attn_norm_w': jnp.ones((Hs,), jnp.float32), 'Wq': p(ks[1], (Hs, Dk)), 'Wk': p(ks[2], (Hs, Dk)), 'Wv': p(ks[3], (Hs, Dv)), 'Wg': p(ks[4], (Hs, Dv)), 'Wgk1': p(ks[5], (Hs, R)), 'Wgk2': p(ks[6], (R, Dk)), 'bgk2': jnp.zeros((Dk,), jnp.float32), 'gnorm_w': jnp.ones((Dv // NUM_HEADS,), jnp.float32), 'Wo': p(ks[7], (Dv, Hs)), 'mlp_norm_w': jnp.ones((Hs,), jnp.float32), 'W_gate': p(ks[8], (Hs, I)), 'W_up': p(ks[9], (Hs, I)), 'W_down': p(ks[10], (I, Hs))}
    _L0_attn_in = _L0_attn_setup()

    def _L0_ffn_setup():
        import jax, jax.numpy as jnp
        import numpy as np
        NUM_NOD = 6
        MAX_PREV = 5
        NUM_EDGE = 20
        D = 128
        H = 8
        LN_EPS = 1e-06

        def _layernorm(x, g, b):
            mu = jnp.mean(x, axis=-1, keepdims=True)
            var = jnp.mean(jnp.square(x - mu), axis=-1, keepdims=True)
            return (x - mu) * jax.lax.rsqrt(var + LN_EPS) * g + b

        def _mha(q, k, v, wq, wk, wv, wo):
            B, S, d = q.shape
            dh = d // H
            qh = (q @ wq).reshape(B, S, H, dh)
            kh = (k @ wk).reshape(B, S, H, dh)
            vh = (v @ wv).reshape(B, S, H, dh)
            scores = jnp.einsum('bqhd,bkhd->bhqk', qh, kh) / jnp.sqrt(jnp.asarray(dh, q.dtype))
            attn = jax.nn.softmax(scores, axis=-1)
            ctx = jnp.einsum('bhqk,bkhd->bqhd', attn, vh).reshape(B, S, d)
            return ctx @ wo
        key = jax.random.key(seed)
        ks = jax.random.split(key, 12)
        B, S = (8, 128)
        scale = 1.0 / np.sqrt(D)
        return {'inputs': jax.random.normal(ks[0], (B, S, D), jnp.float32), 'ew': jax.random.uniform(ks[1], (NUM_NOD, 3), jnp.float32), 'act_w': jax.random.uniform(ks[2], (NUM_NOD,), jnp.float32), 'We': jax.random.normal(ks[3], (NUM_EDGE, D, D), jnp.float32) * scale, 'be': jnp.zeros((NUM_EDGE, D), jnp.float32), 'Wq': jax.random.normal(ks[4], (NUM_NOD, D, D), jnp.float32) * scale, 'Wk': jax.random.normal(ks[5], (NUM_NOD, D, D), jnp.float32) * scale, 'Wv': jax.random.normal(ks[6], (NUM_NOD, D, D), jnp.float32) * scale, 'Wo': jax.random.normal(ks[7], (NUM_NOD, D, D), jnp.float32) * scale, 'ln_g': jnp.ones((D,), jnp.float32), 'ln_b': jnp.zeros((D,), jnp.float32)}
    _L0_ffn_in = _L0_ffn_setup()
    _d = {'L0_attn_hidden_states': _L0_attn_in['hidden_states'], 'L0_attn_attn_norm_w': _L0_attn_in['attn_norm_w'], 'L0_attn_Wq': _L0_attn_in['Wq'], 'L0_attn_Wk': _L0_attn_in['Wk'], 'L0_attn_Wv': _L0_attn_in['Wv'], 'L0_attn_Wg': _L0_attn_in['Wg'], 'L0_attn_Wgk1': _L0_attn_in['Wgk1'], 'L0_attn_Wgk2': _L0_attn_in['Wgk2'], 'L0_attn_bgk2': _L0_attn_in['bgk2'], 'L0_attn_gnorm_w': _L0_attn_in['gnorm_w'], 'L0_attn_Wo': _L0_attn_in['Wo'], 'L0_attn_mlp_norm_w': _L0_attn_in['mlp_norm_w'], 'L0_attn_W_gate': _L0_attn_in['W_gate'], 'L0_attn_W_up': _L0_attn_in['W_up'], 'L0_attn_W_down': _L0_attn_in['W_down'], 'L0_ffn_ew': _L0_ffn_in['ew'], 'L0_ffn_act_w': _L0_ffn_in['act_w'], 'L0_ffn_We': _L0_ffn_in['We'], 'L0_ffn_be': _L0_ffn_in['be'], 'L0_ffn_Wq': _L0_ffn_in['Wq'], 'L0_ffn_Wk': _L0_ffn_in['Wk'], 'L0_ffn_Wv': _L0_ffn_in['Wv'], 'L0_ffn_Wo': _L0_ffn_in['Wo'], 'L0_ffn_ln_g': _L0_ffn_in['ln_g'], 'L0_ffn_ln_b': _L0_ffn_in['ln_b']}
    _x0 = _d['L0_attn_hidden_states']
    _d['L0_attn_hidden_states'] = jax.random.normal(jax.random.fold_in(jax.random.key(seed), 1), (16, 256, 128), dtype=_x0.dtype)
    del _x0
    return _d

def reference(L0_attn_hidden_states, L0_attn_attn_norm_w, L0_attn_Wq, L0_attn_Wk, L0_attn_Wv, L0_attn_Wg, L0_attn_Wgk1, L0_attn_Wgk2, L0_attn_bgk2, L0_attn_gnorm_w, L0_attn_Wo, L0_attn_mlp_norm_w, L0_attn_W_gate, L0_attn_W_up, L0_attn_W_down, L0_ffn_ew, L0_ffn_act_w, L0_ffn_We, L0_ffn_be, L0_ffn_Wq, L0_ffn_Wk, L0_ffn_Wv, L0_ffn_Wo, L0_ffn_ln_g, L0_ffn_ln_b):

    def _L0_attn_ref(hidden_states, attn_norm_w, Wq, Wk, Wv, Wg, Wgk1, Wgk2, bgk2, gnorm_w, Wo, mlp_norm_w, W_gate, W_up, W_down):
        import jax, jax.numpy as jnp
        import numpy as np
        EPS = 1e-06
        CHUNK = 64
        GATE_LOGIT_NORMALIZER = 16.0
        NUM_HEADS = 4

        def _rms(x, w):
            return x * jax.lax.rsqrt(jnp.mean(x * x, axis=-1, keepdims=True) + EPS) * w

        def _gla_chunk(q, k, v, glog, num_heads):
            B, T, Dk = q.shape
            Dv = v.shape[-1]
            dk, dv = (Dk // num_heads, Dv // num_heads)
            Nc = T // CHUNK

            def split(x, d):
                return x.reshape(B, T, num_heads, d).transpose(0, 2, 1, 3).reshape(B, num_heads, Nc, CHUNK, d)
            q, k, v, g = (split(q, dk), split(k, dk), split(v, dv), split(glog, dk))
            b = jnp.cumsum(g, axis=3)
            scale = dk ** (-0.5)
            qe = q * jnp.exp(b) * scale
            mask = jnp.tril(jnp.ones((CHUNK, CHUNK), dtype=bool))
            A = jnp.einsum('bhncd,bhnsd->bhncs', qe, k * jnp.exp(-b))
            A = jnp.where(mask, A, 0.0)
            o_intra = jnp.einsum('bhncs,bhnsd->bhncd', A, v)

            def step(S, xs):
                qe_c, k_c, v_c, b_c = xs
                blast = b_c[:, :, -1, :]
                o_inter = jnp.einsum('bhcd,bhde->bhce', qe_c, S)
                kd = k_c * jnp.exp(blast[:, :, None, :] - b_c)
                S_new = S * jnp.exp(blast)[..., None] + jnp.einsum('bhcd,bhce->bhde', kd, v_c)
                return (S_new, o_inter)
            S0 = jnp.zeros((B, num_heads, dk, dv), q.dtype)
            xs = tuple((jnp.moveaxis(t, 2, 0) for t in (qe, k, v, b)))
            _, o_inter = jax.lax.scan(step, S0, xs)
            o = o_intra + jnp.moveaxis(o_inter, 0, 2)
            return o.reshape(B, num_heads, T, dv).transpose(0, 2, 1, 3)
        x = hidden_states
        h = _rms(x, attn_norm_w)
        q, k, v = (h @ Wq, h @ Wk, h @ Wv)
        glog = jax.nn.log_sigmoid(h @ Wgk1 @ Wgk2 + bgk2) / GATE_LOGIT_NORMALIZER
        o = _gla_chunk(q, k, v, glog, NUM_HEADS)
        g_out = (h @ Wg).reshape(o.shape)
        o = _rms(o, gnorm_w) * (g_out * jax.nn.sigmoid(g_out))
        attn_out = o.reshape(x.shape[0], x.shape[1], -1) @ Wo
        x2 = attn_out + x
        n = _rms(x2, mlp_norm_w)
        mlp = jax.nn.silu(n @ W_gate) * (n @ W_up) @ W_down
        return x2 + mlp

    def _L0_ffn_ref(inputs, ew, act_w, We, be, Wq, Wk, Wv, Wo, ln_g, ln_b):
        import jax, jax.numpy as jnp
        import numpy as np
        NUM_NOD = 6
        MAX_PREV = 5
        NUM_EDGE = 20
        D = 128
        H = 8
        LN_EPS = 1e-06

        def _layernorm(x, g, b):
            mu = jnp.mean(x, axis=-1, keepdims=True)
            var = jnp.mean(jnp.square(x - mu), axis=-1, keepdims=True)
            return (x - mu) * jax.lax.rsqrt(var + LN_EPS) * g + b

        def _mha(q, k, v, wq, wk, wv, wo):
            B, S, d = q.shape
            dh = d // H
            qh = (q @ wq).reshape(B, S, H, dh)
            kh = (k @ wk).reshape(B, S, H, dh)
            vh = (v @ wv).reshape(B, S, H, dh)
            scores = jnp.einsum('bqhd,bkhd->bhqk', qh, kh) / jnp.sqrt(jnp.asarray(dh, q.dtype))
            attn = jax.nn.softmax(scores, axis=-1)
            ctx = jnp.einsum('bhqk,bkhd->bqhd', attn, vh).reshape(B, S, d)
            return ctx @ wo
        nodes = {-1: inputs}
        lind = 0
        for c in range(NUM_NOD):
            nsrc = min(c + 1, MAX_PREV)
            snode = c - nsrc
            eq, ek, ev = (lind + nsrc - 1, lind, lind + nsrc // 2)
            in_q, in_k, in_v = (c - 1, snode, snode + nsrc // 2)
            q = ew[c, 0] * (nodes[in_q] @ We[eq] + be[eq])
            k = ew[c, 1] * (nodes[in_k] @ We[ek] + be[ek])
            v = ew[c, 2] * (nodes[in_v] @ We[ev] + be[ev])
            o = _mha(q, k, v, Wq[c], Wk[c], Wv[c], Wo[c])
            nodes[c] = act_w[c] * o + q
            lind += nsrc
        out = nodes[NUM_NOD - 1]
        return _layernorm(out, ln_g, ln_b)
    x = L0_attn_hidden_states
    x = x + _L0_attn_ref(_layernorm(x, axis=-1), L0_attn_attn_norm_w, L0_attn_Wq, L0_attn_Wk, L0_attn_Wv, L0_attn_Wg, L0_attn_Wgk1, L0_attn_Wgk2, L0_attn_bgk2, L0_attn_gnorm_w, L0_attn_Wo, L0_attn_mlp_norm_w, L0_attn_W_gate, L0_attn_W_up, L0_attn_W_down)
    x = x + _L0_ffn_ref(_layernorm(x, axis=-1), L0_ffn_ew, L0_ffn_act_w, L0_ffn_We, L0_ffn_be, L0_ffn_Wq, L0_ffn_Wk, L0_ffn_Wv, L0_ffn_Wo, L0_ffn_ln_g, L0_ffn_ln_b)
    return x

_drawn_inputs = setup_inputs


def setup_inputs(seed=0):
    import zlib

    import numpy as np

    out = dict(_drawn_inputs(seed))
    spreads = {'L0_attn_attn_norm_w': (1.0, 0.6),
     'L0_attn_bgk2': (0.0, 0.8),
     'L0_attn_gnorm_w': (1.0, 0.6),
     'L0_attn_mlp_norm_w': (1.0, 0.6),
     'L0_ffn_be': (0.0, 0.1),
     'L0_ffn_ln_g': (1.0, 0.6),
     'L0_ffn_ln_b': (0.0, 0.8)}
    factors = {'L0_attn_Wq': 4.473,
     'L0_attn_Wk': 4.467,
     'L0_attn_Wv': 4.431,
     'L0_attn_Wg': 4.49,
     'L0_attn_Wgk1': 8.0,
     'L0_attn_Wgk2': 8.0,
     'L0_attn_Wo': 4.426,
     'L0_attn_W_gate': 8.0,
     'L0_attn_W_up': 8.0,
     'L0_attn_W_down': 8.0,
     'L0_ffn_Wq': 64.0,
     'L0_ffn_Wk': 64.0,
     'L0_ffn_act_w': 8.0,
     'L0_ffn_We': 5.14,
     'L0_ffn_Wv': 3.099,
     'L0_ffn_Wo': 3.154}
    for name, (base, spread) in spreads.items():
        noise = np.random.default_rng([zlib.crc32(name.encode()), seed]).standard_normal(out[name].shape)
        drawn = base * np.exp(spread * noise) if base else spread * noise
        out[name] = jnp.asarray(drawn.astype(out[name].dtype))
    for name, factor in factors.items():
        out[name] = (out[name] * factor).astype(out[name].dtype)
    return out
```

```python
from contextlib import ExitStack

import numpy as np

import concourse.bass as bass
from concourse import mybir

ALU = mybir.AluOpType
ACT = mybir.ActivationFunctionType
AX_X = mybir.AxisListType.X
F32 = mybir.dt.float32
F32R = mybir.dt.float32r
U32 = mybir.dt.uint32

P = 128
D = 128
BATCH, T = 16, 256
TILES = BATCH * T // P
LN_EPS, RMS_EPS, FFN_LN_EPS = 1e-5, 1e-6, 1e-6

GH, DK, DV, CHUNK = 4, 16, 32, 64
QK = GH * DK
GATE_NORM = 16.0
RANK = 16
MLP = 352
MT = 3
MROWS = [128, 128, MLP - 256]
TPI = 4
TOK = TPI * P
ITERS = TILES // TPI
BPI = TOK // T

NODES, MAX_PREV, EDGES = 6, 5, 20
H, DH = 8, 16
PAIRS = H // 2
KT = T // P
LIVE = 4
STEPS = NODES * LIVE
GROUPS = BATCH // LIVE
GCOL = 4
VW = 32
PARTS = 3
ROWS = PARTS * 32
UNITS = PAIRS * KT
SBANK = (0, 1, 7)
ACT_UNITS = (1, 3, 6)
STACK_DMAS = PARTS * 3


def graph():
    out, at = [], 0
    for c in range(NODES):
        n = min(c + 1, MAX_PREV)
        s = c - n
        out.append(dict(e=(at + n - 1, at, at + n // 2), src=(c - 1, s, s + n // 2)))
        at += n
    return out


GRAPH = graph()


class Event:

    def __init__(self, sem, place, events):
        self.sem, self.place, self.events = sem, place, events

    def at(self, n):
        return n * self.events + self.place

C_ID, C_CUM, C_MASK, C_MEAN, C_HEAD, C_STATE, C_END = 0, 128, 256, 768, 896, 900, 1028


def constants():
    c = np.zeros((P, C_END), np.float32)
    i = np.arange(P)
    c[:, C_ID:C_ID + P] = np.eye(P)
    causal = (i[:, None] <= i[None, :]) & (i[:, None] // CHUNK == i[None, :] // CHUNK)
    c[:, C_CUM:C_CUM + P] = causal
    c[:, C_MASK:C_MASK + GH * P] = np.tile(causal, (1, GH))
    c[:, C_MEAN:C_MEAN + P] = (i[:, None] // DV == i[None, :] // DV) / DV
    r = np.arange(QK)
    c[:QK, C_HEAD:C_HEAD + GH] = r[:, None] // DK == np.arange(GH)[None, :]
    c[:QK, C_STATE:C_STATE + P] = r[:, None] // DK == i[None, :] // DV
    return c


def build(nc, a, consts, out):
    ds = bass.ds
    with ExitStack() as ctx:
        def sb(name, shape, dt=F32):
            return ctx.enter_context(nc.sbuf_tensor(name, shape, dt))

        def sem(name):
            return ctx.enter_context(nc.semaphore(name))

        bank = [ctx.enter_context(nc.psum_tensor(f"bank{n}", [P, 512], F32)) for n in range(8)]

        def quads(n):
            return bank[n][:, :].rearrange("p (t d) -> p t d", t=4)

        cst = sb("cst", [P, C_END])
        ident = cst[:, C_ID:C_ID + P]
        cum = cst[:, C_CUM:C_CUM + P]
        causal = cst[:, C_MASK:C_MASK + GH * P].bitcast(U32)
        mean_dv = cst[:, C_MEAN:C_MEAN + P]
        head_mask = cst[0:QK, C_HEAD:C_HEAD + GH]
        state_mask = cst[0:QK, C_STATE:C_STATE + P]
        xall = sb("xall", [P, TILES, D])
        xT = sb("xT", [P, TILES * P])
        wa = sb("wa", [P, 2 * QK + 2 * D])
        wz = sb("wz", [P, QK])
        wo = sb("wo", [P, D])
        wgu = sb("wgu", [P, 2, MLP])
        wd = sb("wd", [P, MT, D])
        bgk = sb("bgk", [P, QK])
        eps_col = sb("eps_col", [P, 1])
        cols = sb("cols", [P, 3])
        w_res = sb("w_res", [P, NODES, D])
        w_fold = sb("w_fold", [P, NODES, 3, D])
        w_out = sb("w_out", [P, NODES, D])
        bcol = sb("bcol", [P, NODES, 3])
        nb5 = sb("nb5", [P, D])
        lng = sb("lng", [P, 2, D])
        scal = sb("scal", [P, NODES * 4])
        kz = [sb(f"kz{b}", [ROWS, H, T], F32R) for b in range(LIVE)]
        qs = [sb(f"qs{b}", [ROWS, PAIRS, T], F32R) for b in range(LIVE)]
        hl = [sb(f"hl{n}", [P, 2, 2 * T], F32R) for n in range(2)]
        parts = nc.dram_tensor("parts", (LIVE, P, 2, 2 * T), F32, kind="Internal").ap()

        UW = 16400
        region = sb("region", [P, UW])

        def carver():
            at = [0]

            def carve(*dims, rows=P):
                n = int(np.prod(dims))
                v = region[0:rows, at[0]:at[0] + n]
                at[0] += n
                assert at[0] <= UW, at[0]
                if len(dims) == 2:
                    v = v.rearrange("p (a b) -> p a b", a=dims[0])
                elif len(dims) == 3:
                    v = v.rearrange("p (a b c) -> p a b c", a=dims[0], b=dims[1])
                return v
            return carve, at

        carve, _ = carver()
        xn = carve(TPI, D)
        hh = carve(TPI, D)
        hT = carve(TOK)
        zb = carve(TPI, QK)
        za = carve(TPI, QK)
        gl = carve(TPI, QK)
        ebq = carve(TOK, rows=QK)
        ebk = carve(TOK, rows=QK)
        qe = carve(TOK, rows=QK)
        ke = carve(TOK, rows=QK)
        qbd = carve(GH, TOK, rows=QK)
        vsb = carve(TPI, D)
        sg = carve(TOK)
        keT = carve(TPI, QK)
        am = carve(TPI, GH * P)
        kvs = carve(BPI, 3, D, rows=QK)
        sq = carve(TOK)
        uu = carve(TOK)
        x2 = carve(TPI, D)
        nn = carve(TPI, D)
        nT = carve(TOK)
        eg = carve(2, TOK)
        hid = carve(MT, TOK)
        st = carve(TPI, 6)
        mv = carve(2, TPI)
        sm = carve(3, TPI)
        ve = carve(2, TPI)
        rr = carve(2, TPI)
        rt = carve(2, TPI)
        st2 = carve(TPI, 6)
        mv2 = carve(2, TPI)
        sm2 = carve(3, TPI)
        ss = carve(TPI)
        ve2 = carve(TPI)
        rr2 = carve(TPI)
        rt2 = carve(TPI)
        ve3 = carve(TPI)
        rr3 = carve(TPI)
        rt3 = carve(TPI)
        carve, at = carver()
        at[0] = 0
        we_raw = carve(EDGES, D)
        wqkv_raw = carve(3, NODES * D)
        wo_raw = carve(NODES, D)
        weT = carve(2, 3 * D)
        be_rows = carve(D, rows=EDGES)
        beT = carve(EDGES)
        bprod = carve(NODES, 4)
        wgk1 = carve(RANK)
        wgk1T = carve(P, rows=RANK)
        wgk2 = carve(QK, rows=RANK)
        nb5w = carve(D)
        carve, _ = carver()
        x0T = carve(LIVE, T)
        node = carve(LIVE, NODES - 1, T)
        vaug = [carve(KT, H * VW) for _ in range(LIVE)]
        prob = [carve(2, T) for _ in range(2)]
        probT = carve(H, KT * T)
        raw = carve(2 * T)
        rec = carve(KT * H)
        ctxc = carve(KT, D)
        ctxT = [carve(T) for _ in range(2)]
        mx = [carve(UNITS, 2) for _ in range(2)]
        fy = carve(KT, D)
        fst = carve(KT, 6)
        fmv = carve(2, KT)
        fsm = carve(3, KT)
        fve = carve(KT)
        fr = carve(KT)
        frt = carve(KT)

        def names(text):
            return {n: sem(n) for n in text.split()}

        def chain(name, events):
            one, events = sem(name), events.split()
            return {e: Event(one, k + 1, len(events)) for k, e in enumerate(events)}

        L = names("x_in const_in wa_in gk_in wo_in mlp_in cols_in nodew_in scal_in ln_in")
        S = names("wz_ok wa_ok wfirst_ok we_t we_c fold_ps fold_ok be_t be_c "
                  "bias_w w_out_ok am0 eps_ok zero_ok prep_a prep_d")
        A = names("xn_ok h_ok hT_ps hT_ok z_ps b_ps eb_ok q_ps k_ps qe_ok ke_ok qbd_ok "
                  "v_ps v_ok g_ps eg_ok sg_ok keT_ps keT_ok kv_ps am_ok "
                  "n_ok nT_ps nT_ok gate_ps up_ps eg2_ok si_ok hid_ok y_ps y_ok x1_ok xn2_ok "
                  "xT_ps xT_ok")
        B = names("qk_ps v_ps2 hi_ok lo_ok vals_ok s_ps max_ok exp_ok pT_ps pT_act pT_dve pv_ok "
                  "node_ok vones fy_free out_stored")
        A.update(chain("ln1", "bn1 sm1 sd1 mv1 ve_ok rl ra rb rc rstd1_ok"))
        A.update(chain("rms2", "ve2_ok r2l r2a r2b r2c rstd2_ok"))
        A.update(chain("ln2", "bn2 sm2 sd2 mv2 ve3_ok r3l r3a r3b r3c rstd3_ok"))
        B.update(chain("fin", "fin_read fbn fsm fsd fmv fve_ok frl fra frb frc fr_ok fyn_ok fg_ok fb_ok"))
        A.update(chain("logsig", "zb_ok za_ok e_ok l_ok gl_ok"))
        A.update(chain("state", "kvs_ok s2_ok s3_ok"))
        A.update(chain("heads", "o_ps sq_ok ms_ps msl_ok rstd_ok t1_ok u_ok at_ps x2_ok ss_ok"))
        S.update(chain("gk", "gk1_t gk1_c gk_ps"))
        S.update(chain("bias", "bias_ps bias_c bo_ps bo_ok bias_f nb_b nb_ps"))
        B.update(chain("ctx", "raw_ok rawT_ps rec_ok ctxc_ok ctxT_ps ctxT_ok node_ps"))
        a_ps = [sem(f"a_ps{t}") for t in range(TPI)]
        stored = [sem(f"stored{n}") for n in range(2)]
        stacked = [sem(f"stacked{b}") for b in range(LIVE)]
        x0_in = [sem(f"x0_in{b}") for b in range(LIVE)]

        x_d = a["L0_attn_hidden_states"].rearrange("b t d -> (b t) d").rearrange("(n p) d -> p n d", p=P)
        out_d = out.rearrange("b t d -> (b t) d").rearrange("(n t p) d -> n p t d", t=KT, p=P)

        def col(v):
            return v.rearrange("(d a) -> d a", a=1)


        def slots(eng, body):
            body(0, None)
            with eng.Fori(1, ITERS) as i:
                body(i, i - 1)
            body(None, ITERS - 1)


        LAST = STEPS * GROUPS

        def node_slots(eng, body, tail=4):
            def run(base, m):
                def step(off):
                    k = m - off
                    if isinstance(base, int):
                        n = base * STEPS + k
                        if n < 0 or n >= LAST:
                            return None
                        return Step(n // STEPS, n % STEPS)
                    return Step(base + k // STEPS, k % STEPS)
                body(step)

            for m in range(tail):
                run(0, m)
            with eng.Fori(0, GROUPS - 1) as i:
                for m in range(tail, tail + STEPS):
                    run(i, m)
            for m in range(tail, tail + STEPS):
                run(GROUPS - 1, m)

        class Step:
            def __init__(self, it, m):
                self.it, self.m, self.c, self.b = it, m, m // LIVE, m % LIVE
                self.n2 = m % 2

            def count(self, per=1, plus=0):
                return self.it * (STEPS * per) + (self.m * per + plus)

            def number(self):
                return self.count()

            def nodes(self):
                return self.it * ((NODES - 1) * LIVE) + min(self.m + 1, (NODES - 1) * LIVE)

            def finals(self):
                return self.it * LIVE + max(0, self.m + 1 - (NODES - 1) * LIVE)

            def back(self, k):
                if self.m >= k:
                    return Step(self.it, self.m - k)
                if isinstance(self.it, int) and self.it == 0:
                    return None
                return Step(self.it - 1, self.m - k + STEPS)

            def stacks(self):
                return self.it * (16 * STACK_DMAS * NODES) + 16 * STACK_DMAS * (self.c + 1)

        def ahead(step, u):
            return step(2 - u // UNITS), u % UNITS

        def score_bank(s, u):
            return bank[SBANK[(s.m * UNITS + u) % len(SBANK)]]

        def copy_unit(eng, x, u):
            pr, qt = u // KT, u % KT
            eng.wait_ge(B["pT_ps"], x.count(UNITS, u + 1))
            last = x.back(1)
            if last is not None and u in (0, 1, UNITS // 2, UNITS // 2 + 1):
                eng.wait_ge(B["pv_ok"], last.count(2, 2 * u // UNITS + 1))
            to = probT[:, 2 * pr:2 * pr + 2, :].rearrange("p h (k q) -> p h k q", k=KT)[:, :, :, qt * P:(qt + 1) * P]
            src = bank[2 + u % 2][:, :].rearrange("p (h k q) -> p h k q", h=2, k=KT)
            if u in ACT_UNITS:
                eng.activation(to, src, ACT.Copy).then_inc(B["pT_act"], 1)
            else:
                eng.tensor_copy(to, src).then_inc(B["pT_dve"], 1)

        def copies(s, upto, eng):
            mine = [u for u in range(UNITS) if (u in ACT_UNITS) == (eng == "act")]
            return s.count(len(mine), sum(u < upto for u in mine))

        def update(bb, c):
            at = (bb * 2 + c // 2) * D
            return bank[[3, 1][c % 2]][0:QK, at:at + D]

        block = ctx.enter_context(nc.Block())

        @block.sync
        def _(sp):
            sp.dma_start(cst[:, :], consts).then_inc(L["const_in"], 16)
            for half in range(2):
                h = TILES // 2
                sp.dma_start(xall[:, half * h:(half + 1) * h, :], x_d[:, half * h:(half + 1) * h, :]).then_inc(L["x_in"], 16)
            sp.dma_start(wa[:, 0:QK], a["L0_attn_Wq"]).then_inc(L["wa_in"], 16)
            sp.dma_start(wa[:, QK:2 * QK], a["L0_attn_Wk"]).then_inc(L["wa_in"], 16)
            sp.dma_start(wa[:, 2 * QK:2 * QK + D], a["L0_attn_Wv"]).then_inc(L["wa_in"], 16)
            sp.dma_start(wa[:, 2 * QK + D:], a["L0_attn_Wg"]).then_inc(L["wa_in"], 16)
            sp.dma_start(wo[:, :], a["L0_attn_Wo"]).then_inc(L["wo_in"], 16)
            sp.dma_start(wgu[:, 0, :], a["L0_attn_W_gate"]).then_inc(L["mlp_in"], 16)
            sp.dma_start(wgu[:, 1, :], a["L0_attn_W_up"]).then_inc(L["mlp_in"], 16)
            sp.dma_start(wd[:, 0:2, :], a["L0_attn_W_down"][0:256, :].rearrange("(m p) d -> p m d", p=P)).then_inc(L["mlp_in"], 16)
            sp.dma_start(wd[0:MROWS[2], 2, :], a["L0_attn_W_down"][256:MLP, :]).then_inc(L["mlp_in"], 16)

            def phase(step):
                s = step(0)
                if s is None:
                    return
                if isinstance(s.it, int) and s.it == 0 and s.m < LIVE:
                    sp.wait_ge(S["zero_ok"], s.b + 1)
                sp.wait_ge(B["lo_ok"], s.count(1, 1))
                sp.dma_start(parts[s.b], hl[s.n2][:, :, :].bitcast(F32)).then_inc(stored[s.n2], 16)
                sp.wait_ge(stored[s.n2], s.it * (16 * STEPS // 2) + 16 * (s.m // 2 + 1))
                for blk in range(PARTS):
                    kp, qp = [(0, 0), (1, 0), (0, 1)][blk]
                    rows = blk * 32
                    for odd in range(2):
                        src = parts[s.b, :, kp, 0:T].rearrange("(j s r) t -> s r j t", j=PAIRS, s=2)[odd]
                        sp.dma_start(kz[s.b][rows + 16 * odd:rows + 16 * odd + 16, odd::2, :].bitcast(F32), src)\
                            .then_inc(stacked[s.b], 16)
                    src = parts[s.b, :, qp, T:2 * T].rearrange("(j r) t -> r j t", j=PAIRS)
                    sp.dma_start(qs[s.b][rows:rows + 32, :, :].bitcast(F32), src).then_inc(stacked[s.b], 16)

            node_slots(sp, phase)

        @block.gpsimd
        def _(pool):
            pool.dma_start(cols[:, 0:1], col(a["L0_attn_attn_norm_w"])).then_inc(L["cols_in"], 16)
            pool.dma_start(cols[:, 1:2], col(a["L0_attn_mlp_norm_w"])).then_inc(L["cols_in"], 16)
            for h in range(GH):
                pool.dma_start(cols[DV * h:DV * h + DV, 2:3], col(a["L0_attn_gnorm_w"])).then_inc(L["cols_in"], 16)
            pool.dma_start(wgk1, a["L0_attn_Wgk1"]).then_inc(L["gk_in"], 16)
            pool.dma_start(wgk2, a["L0_attn_Wgk2"]).then_inc(L["gk_in"], 16)
            pool.dma_start(bgk[:, :], a["L0_attn_bgk2"].partition_broadcast(P)).then_inc(L["gk_in"], 16)
            pool.dma_start(scal[:, 0:18], a["L0_ffn_ew"].rearrange("a b -> (a b)").partition_broadcast(P)).then_inc(L["scal_in"], 16)
            pool.dma_start(scal[:, 18:24], a["L0_ffn_act_w"].partition_broadcast(P)).then_inc(L["scal_in"], 16)
            pool.dma_start(lng[:, 0, :], a["L0_ffn_ln_g"].partition_broadcast(P)).then_inc(L["ln_in"], 16)
            pool.dma_start(lng[:, 1, :], a["L0_ffn_ln_b"].partition_broadcast(P)).then_inc(L["ln_in"], 16)
            for b in range(LIVE):
                pool.memset(kz[b][:, :, :].bitcast(F32), 0.0).then_inc(S["zero_ok"], 1)
            pool.memset(eps_col[:, :], RMS_EPS).then_inc(S["eps_ok"], 1)
            pool.wait_ge(S["prep_a"], 1)
            pool.wait_ge(S["prep_d"], 1)
            pool.memset(am, 0.0).then_inc(S["am0"], 1)

            def first(i, j):
                if j is None:
                    return
                pool.wait_ge(A["y_ok"], j + 1)
                pool.tensor_tensor(xall[:, ds(TPI * j, TPI), :], nn, xall[:, ds(TPI * j, TPI), :], ALU.add)\
                    .then_inc(A["x1_ok"], 1)
            slots(pool, first)

            pool.wait_ge(A["xT_ok"], ITERS)
            for b in range(LIVE):
                v = vaug[b].rearrange("p k (h w) -> p k h w", w=VW)
                pool.memset(v[:, :, :, DH + 1:], 0.0)
                pool.memset(v[:, :, :, DH:DH + 1], 1.0).then_inc(B["vones"], 1)
            pool.memset(fy, 0.0).then_inc(B["fy_free"], 1)
            for b in range(LIVE):
                pool.dma_start(x0T[:, b, :], xT[:, T * b:T * b + T]).then_inc(x0_in[b], 16)

            def phase(step):
                s = step(1)
                if s is not None and s.c == NODES - 1:
                    pool.wait_ge(B["qk_ps"], s.count(1, 1))
                    if not (isinstance(s.it, int) and s.it == GROUPS - 1):
                        pool.dma_start(x0T[:, s.b, :], xT[:, ds((s.it + 1) * (LIVE * T) + s.b * T, T)])\
                            .then_inc(x0_in[s.b], 16)
                s = step(4)
                if s is not None and s.c == NODES - 1:
                    f = s.it * LIVE + s.b
                    tiles = xall[:, ds(f * KT, KT), :]
                    pool.wait_ge(B["fyn_ok"].sem, B["fyn_ok"].at(f))
                    pool.tensor_tensor(fy, fy, lng[:, 0:1, :].to_broadcast([P, KT, D]), ALU.mult).then_inc(B["fg_ok"].sem, 1)
                    pool.wait_ge(B["fg_ok"].sem, B["fg_ok"].at(f))
                    pool.tensor_tensor(fy, fy, lng[:, 1:2, :].to_broadcast([P, KT, D]), ALU.add).then_inc(B["fb_ok"].sem, 1)
                    pool.wait_ge(B["fb_ok"].sem, B["fb_ok"].at(f))
                    pool.tensor_tensor(tiles, fy, tiles, ALU.add).then_inc(B["fy_free"], 1)
                    pool.wait_ge(B["fy_free"], f + 2)
                    pool.dma_start(out_d[f], tiles).then_inc(B["out_stored"], 16)
            pool.wait_ge(L["ln_in"], 32)
            node_slots(pool, phase)
            pool.wait_ge(B["out_stored"], 16 * BATCH)

        @block.scalar
        def _(act):
            act.dma_start(we_raw, a["L0_ffn_We"].rearrange("e d n -> d e n")).then_inc(L["nodew_in"], 16)
            for j, w in enumerate(("Wq", "Wk", "Wv")):
                act.dma_start(wqkv_raw[:, j, :].rearrange("p (c n) -> p c n", c=NODES),
                              a["L0_ffn_" + w].rearrange("c d n -> d c n")).then_inc(L["nodew_in"], 16)
            act.dma_start(wo_raw, a["L0_ffn_Wo"].rearrange("c d n -> d c n")).then_inc(L["nodew_in"], 16)
            act.dma_start(be_rows, a["L0_ffn_be"]).then_inc(L["nodew_in"], 16)
            act.wait_ge(S["gk1_t"].sem, S["gk1_t"].at(0))
            act.activation(wgk1T, bank[6][0:RANK, 0:P], ACT.Copy).then_inc(S["gk1_c"].sem, 1)
            act.wait_ge(S["be_t"], 1)
            act.activation(beT, bank[7][:, 0:EDGES], ACT.Copy).then_inc(S["be_c"], 1)
            for c in range(NODES):
                act.wait_ge(S["we_t"], c + 1)
                if c >= 2:
                    act.wait_ge(S["fold_ps"], c - 1)
                act.activation(weT[:, c % 2, :], bank[c % 2][:, 0:3 * D], ACT.Copy).then_inc(S["we_c"], 1)
            act.wait_ge(S["prep_d"], 1)
            act.copy(cols[:, 0:1], cols[:, 0:1]).then_inc(S["prep_a"], 1)

            def first(i, j):
                if j is not None:
                    inverse_root(ve2, rr2, j, "ve2_ok", "r2l", "r2a")
                if i is not None:
                    inverse_root(ve, rr, i, "ve_ok", "rl", "ra")
                if j is not None:
                    act.wait_ge(A["nT_ps"], j + 1)
                    act.activation(nT, bank[5][:, :], ACT.Copy).then_inc(A["nT_ok"], 1)
                    gate_tanh(j, 0)
                if i is not None:
                    act.wait_ge(A["hT_ps"], i + 1)
                    act.activation(hT, bank[0][:, :], ACT.Copy).then_inc(A["hT_ok"], 1)
                if j is not None:
                    gate_tanh(j, 1)
                if i is not None:
                    act.wait_ge(A["za_ok"].sem, A["za_ok"].at(i))
                    act.activation(za, za, ACT.Exp).then_inc(A["e_ok"].sem, 1)
                    act.wait_ge(A["e_ok"].sem, A["e_ok"].at(i))
                    act.activation(za, za, ACT.Ln, bias=1.0).then_inc(A["l_ok"].sem, 1)
                    act.wait_ge(A["v_ps"], i + 1)
                    act.activation(vsb, quads(4), ACT.Copy).then_inc(A["v_ok"], 1)
                if j is not None:
                    gate_tanh(j, 2)
                if i is not None:
                    act.wait_ge(A["b_ps"], i + 1)
                    act.activation(ebq, bank[1][0:QK, :], ACT.Exp, scale=1.0 / GATE_NORM)
                    act.activation(ebk, bank[1][0:QK, :], ACT.Exp, scale=-1.0 / GATE_NORM).then_inc(A["eb_ok"], 1)
                    act.wait_ge(A["g_ps"], i + 1)
                    act.activation(sg, bank[0][:, :], ACT.Tanh, scale=0.5).then_inc(A["eg_ok"], 1)
                    act.wait_ge(A["keT_ps"], i + 1)
                    act.activation(keT, bank[2][:, 0:TPI * QK].rearrange("p (t k) -> p t k", t=TPI), ACT.Copy).then_inc(A["keT_ok"], 1)
                if j is not None:
                    inverse_root(ve3, rr3, j, "ve3_ok", "r3l", "r3a")
                    act.wait_ge(A["xT_ps"], j + 1)
                    act.activation(xT[:, ds(j * TOK, TOK)], bank[7][:, :], ACT.Copy).then_inc(A["xT_ok"], 1)
                if i is not None:
                    act.wait_ge(A["o_ps"].sem, A["o_ps"].at(i))
                    act.activation(sq, bank[0][:, :], ACT.Square).then_inc(A["sq_ok"].sem, 1)
                    act.wait_ge(S["eps_ok"], 1)
                    act.wait_ge(A["ms_ps"].sem, A["ms_ps"].at(i))
                    act.activation(sq, bank[3][:, :], ACT.Ln, bias=eps_col[:, 0:1]).then_inc(A["msl_ok"].sem, 1)
                    act.wait_ge(A["msl_ok"].sem, A["msl_ok"].at(i))
                    act.activation(sq, sq, ACT.Exp, scale=-0.5).then_inc(A["rstd_ok"].sem, 1)
                    act.wait_ge(A["x2_ok"].sem, A["x2_ok"].at(i))
                    for t in range(TPI):
                        k = act.activation(nn[:, t, :], x2[:, t, :], ACT.Square, accum_out=ss[:, t:t + 1])
                    k.then_inc(A["ss_ok"].sem, 1)

            def inverse_root(v, r, n, ready, log, done, sems=A):
                act.wait_ge(sems[ready].sem, sems[ready].at(n))
                act.activation(r, v, ACT.Ln).then_inc(sems[log].sem, 1)
                act.wait_ge(sems[log].sem, sems[log].at(n))
                act.activation(r, r, ACT.Exp, scale=-0.5).then_inc(sems[done].sem, 1)

            def gate_tanh(j, m):
                act.wait_ge(A["gate_ps"], j * MT + m + 1)
                if m == 2:
                    act.wait_ge(A["hid_ok"], j * MT + m - 1)
                act.activation(eg[0:MROWS[m], m % 2, :], bank[[6, 5, 7][m]][0:MROWS[m], :], ACT.Tanh, scale=0.5).then_inc(A["eg2_ok"], 1)
            slots(act, first)

            def phase(step):
                d = step(3)
                if d is not None:
                    act.wait_ge(B["pv_ok"], d.count(2, 2))
                    last = d.back(1)
                    if last is not None:
                        act.wait_ge(B["rawT_ps"].sem, B["rawT_ps"].at(last.number()))
                    act.activation(raw, bank[4 + d.n2][:, :], ACT.Copy).then_inc(B["raw_ok"].sem, 1)
                s = step(0)
                if s is not None:
                    act.wait_ge(B["qk_ps"], s.count(1, 1))
                    old = s.back(2)
                    if old is not None:
                        act.wait_ge(stored[s.n2], old.it * (16 * STEPS // 2) + 16 * (old.m // 2 + 1))
                    act.activation(hl[s.n2][:, 0, 0:T], bank[6][:, 0:T], ACT.Identity, bias=bcol[:, s.c, 1:2])
                    act.activation(hl[s.n2][:, 0, T:2 * T], bank[6][:, T:2 * T], ACT.Identity, bias=bcol[:, s.c, 0:1])\
                        .then_inc(B["hi_ok"], 1)
                for u in range(UNITS):
                    exps(*ahead(step, u + 1))
                    x = step(2)
                    if x is not None and u in ACT_UNITS:
                        copy_unit(act, x, u)
                    if u == 2 and s is not None:
                        act.wait_ge(B["v_ps2"], s.count(1, 1))
                        if isinstance(s.it, int) and s.it == 0 and s.m < LIVE:
                            act.wait_ge(B["vones"], s.b + 1)
                        v = vaug[s.b].rearrange("p k (h w) -> p k h w", w=VW)
                        act.activation(v[:, :, :, 0:DH], bank[6][:, 0:T].rearrange("p (k h d) -> p k h d", k=KT, h=H),
                                       ACT.Copy).then_inc(B["vals_ok"], 1)
                    if u == 4 and d is not None:
                        act.wait_ge(B["ctxT_ps"].sem, B["ctxT_ps"].at(d.number()))
                        act.activation(ctxT[d.n2], bank[4 + d.n2][:, 0:T], ACT.Copy).then_inc(B["ctxT_ok"].sem, 1)
                    if u == 6 and d is not None and d.c < NODES - 1:
                        act.wait_ge(B["node_ps"].sem, B["node_ps"].at(d.number()))
                        act.activation(node[:, d.b, d.c, :], bank[4 + d.n2][:, T:2 * T], ACT.Identity, bias=bcol[:, d.c, 2:3])\
                            .then_inc(B["node_ok"], 1)
                    if u == 7 and d is not None and d.c == NODES - 1:
                        inverse_root(fve, fr, d.it * LIVE + d.b, "fve_ok", "frl", "fra", B)

            def exps(s, u):
                if s is None:
                    return
                act.wait_ge(B["max_ok"], s.count(UNITS, u + 1))
                back = s.count(UNITS, u - 1)
                if not (isinstance(back, int) and back < 1):
                    act.wait_ge(B["pT_ps"], back)
                for k in range(2):
                    i = act.activation(prob[u % 2][:, k, :], score_bank(s, u)[:, k * T:(k + 1) * T], ACT.Exp, bias=mx[s.n2][:, u, k:k + 1])
                i.then_inc(B["exp_ok"], 1)
            node_slots(act, phase)

        @block.vector
        def _(dve):
            def scale_q(c):
                return scal[:, 3 * c:3 * c + 1]

            dve.wait_ge(L["cols_in"], 16 * 6)
            dve.wait_ge(L["wa_in"], 64)
            dve.tensor_scalar(wa[:, 0:QK], wa[:, 0:QK], cols[:, 0:1], float(DK) ** -0.5, ALU.mult, ALU.mult)
            dve.tensor_scalar(wa[:, QK:], wa[:, QK:], cols[:, 0:1], None, ALU.mult)
            dve.wait_ge(L["wo_in"], 16)
            dve.tensor_scalar(wo[:, :], wo[:, :], cols[:, 2:3], 0.5, ALU.mult, ALU.mult)
            dve.wait_ge(L["mlp_in"], 64)
            dve.tensor_scalar(wgu[:, 0, :], wgu[:, 0, :], cols[:, 1:2], None, ALU.mult)
            dve.tensor_scalar(wgu[:, 1, :], wgu[:, 1, :], cols[:, 1:2], 0.5, ALU.mult, ALU.mult)
            dve.wait_ge(S["gk_ps"].sem, S["gk_ps"].at(0))
            dve.tensor_scalar(wz[:, :], bank[6][:, 128:128 + QK], cols[:, 0:1], None, ALU.mult).then_inc(S["wa_ok"], 1)
            dve.wait_ge(L["scal_in"], 32)
            dve.wait_ge(L["nodew_in"], 16 * 6)
            for c in range(NODES):
                dve.tensor_scalar(w_res[:, c, :], we_raw[:, GRAPH[c]["e"][0], :], scale_q(c), None, ALU.mult)
                k = dve.tensor_scalar(w_out[:, c, :], wo_raw[:, c, :], scal[:, 18 + c:19 + c], None, ALU.mult)
            k.then_inc(S["w_out_ok"], 1)
            for c in range(NODES):
                dve.wait_ge(S["fold_ps"], c + 1)
                src = bank[2 + c % 2]
                dve.tensor_scalar(w_fold[:, c, 0, :], src[:, 0:D], scale_q(c), float(DH) ** -0.5, ALU.mult, ALU.mult)
                for j in range(1, 3):
                    k = dve.tensor_scalar(w_fold[:, c, j, :], src[:, j * D:(j + 1) * D], scal[:, 3 * c + j:3 * c + j + 1], None, ALU.mult)
                k.then_inc(S["fold_ok"], 1)
            ew = scal[:, 0:18].rearrange("p (c j) -> p c j", j=3)
            dve.wait_ge(S["bias_ps"].sem, S["bias_ps"].at(0))
            bp = bank[4][:, 0:3 * NODES].rearrange("p (c j) -> p c j", j=3)
            dve.tensor_tensor(bprod[:, :, 0:3], bp, ew, ALU.mult).then_inc(S["bias_c"].sem, 1)
            dve.wait_ge(S["bias_c"].sem, S["bias_c"].at(0))
            dve.tensor_scalar(bcol[:, :, 0:1], bprod[:, :, 0:1], float(DH) ** -0.5, None, ALU.mult)
            dve.tensor_copy(bcol[:, :, 1:2], bprod[:, :, 1:2])
            dve.wait_ge(S["be_c"], 1)
            for c in range(NODES):
                e = GRAPH[c]["e"][0]
                k = dve.tensor_tensor(bprod[:, c, 3:4], beT[:, e:e + 1], scale_q(c), ALU.mult)
            k.then_inc(S["bias_w"], 1)
            dve.wait_ge(S["bo_ps"].sem, S["bo_ps"].at(0))
            dve.tensor_tensor(bcol[:, :, 2:3], bank[5][:, 0:NODES].unsqueeze(2), scal[:, 18:24].unsqueeze(2), ALU.mult)\
                .then_inc(S["bo_ok"].sem, 1)
            dve.wait_ge(S["bo_ok"].sem, S["bo_ok"].at(0))
            dve.wait_ge(S["bias_w"], 1)
            dve.tensor_tensor(bcol[:, :, 2:3], bcol[:, :, 2:3], bprod[:, :, 3:4], ALU.add).then_inc(S["bias_f"].sem, 1)
            dve.wait_ge(S["bias_f"].sem, S["bias_f"].at(0))
            dve.tensor_copy(nb5w, bcol[:, NODES - 1, 2:3].to_broadcast([P, D])).then_inc(S["nb_b"].sem, 1)
            dve.wait_ge(S["nb_ps"].sem, S["nb_ps"].at(0))
            dve.tensor_copy(nb5[:, :], bank[6][:, 256:256 + D]).then_inc(S["prep_d"], 1)
            dve.wait_ge(S["prep_a"], 1)

            def first(i, j):
                if j is not None:
                    dve.wait_ge(A["ss_ok"].sem, A["ss_ok"].at(j))
                    dve.tensor_scalar(ve2, ss, 1.0 / D, RMS_EPS, ALU.mult, ALU.add).then_inc(A["ve2_ok"].sem, 1)
                    newton(dve, ve2, rr2, rt2, j, "r2a", "r2b", "r2c", "rstd2_ok")
                    dve.wait_ge(A["rstd2_ok"].sem, A["rstd2_ok"].at(j))
                    for t in range(TPI):
                        k = dve.tensor_scalar(nn[:, t, :], x2[:, t, :], rr2[:, t:t + 1], None, ALU.mult)
                    k.then_inc(A["n_ok"], 1)
                if i is not None:
                    dve.wait_ge(L["x_in"], 32)
                    for t in range(TPI):
                        k = dve.bn_stats(st[:, t, :], xall[:, ds(TPI * i + t, 1), :])
                    k.then_inc(A["bn1"].sem, 1)
                    moments(st, mv, sm, i, "bn1", "sm1", "sd1", "mv1")
                    dve.wait_ge(A["mv1"].sem, A["mv1"].at(i))
                    dve.tensor_scalar(ve[:, 0, :], mv[:, 1, :], LN_EPS, None, ALU.add)
                    dve.tensor_scalar(ve[:, 1, :], mv[:, 1, :], 1.0 + RMS_EPS, RMS_EPS * LN_EPS, ALU.mult, ALU.add).then_inc(A["ve_ok"].sem, 1)
                    newton(dve, ve, rr, rt, i, "ra", "rb", "rc", "rstd1_ok")
                    dve.wait_ge(A["rstd1_ok"].sem, A["rstd1_ok"].at(i))
                    for t in range(TPI):
                        k = dve.tensor_scalar(hh[:, t, :], xall[:, ds(TPI * i + t, 1), :].squeeze(1), mv[:, 0, t:t + 1], rr[:, 1, t:t + 1],
                                              ALU.subtract, ALU.mult)
                    k.then_inc(A["h_ok"], 1)
                    for t in range(TPI):
                        k = dve.tensor_scalar(xn[:, t, :], xall[:, ds(TPI * i + t, 1), :].squeeze(1), mv[:, 0, t:t + 1], rr[:, 0, t:t + 1],
                                              ALU.subtract, ALU.mult)
                    k.then_inc(A["xn_ok"], 1)
                if j is not None:
                    silu_gate(j, 0)
                    times_up(j, 0)
                if i is not None:
                    dve.wait_ge(A["z_ps"], i + 1)
                    zps = bank[1][:, 0:TPI * QK].rearrange("p (t k) -> p t k", t=TPI)
                    dve.tensor_tensor(zb, zps, bgk[:, :].unsqueeze(1).to_broadcast([P, TPI, QK]), ALU.add).then_inc(A["zb_ok"].sem, 1)
                    dve.wait_ge(A["zb_ok"].sem, A["zb_ok"].at(i))
                    dve.scalar_tensor_tensor(za, zb, -1.0, zb, ALU.mult, ALU.min).then_inc(A["za_ok"].sem, 1)
                if j is not None:
                    silu_gate(j, 1)
                if i is not None:
                    dve.wait_ge(A["l_ok"].sem, A["l_ok"].at(i))
                    dve.scalar_tensor_tensor(gl, zb, 0.0, za, ALU.min, ALU.subtract).then_inc(A["gl_ok"].sem, 1)
                if j is not None:
                    times_up(j, 1)
                    silu_gate(j, 2)
                if i is not None:
                    dve.wait_ge(A["eb_ok"], i + 1)
                    dve.wait_ge(A["q_ps"], i + 1)
                    dve.tensor_tensor(qe, bank[2][0:QK, :], ebq, ALU.mult).then_inc(A["qe_ok"], 1)
                    dve.wait_ge(A["k_ps"], i + 1)
                    dve.tensor_tensor(ke, bank[3][0:QK, :], ebk, ALU.mult).then_inc(A["ke_ok"], 1)
                if j is not None:
                    times_up(j, 2)
                if i is not None:
                    dve.wait_ge(A["qe_ok"], i + 1)
                    for h in range(GH):
                        k = dve.tensor_scalar(qbd[:, h, :], qe, head_mask[:, h:h + 1], None, ALU.mult)
                    k.then_inc(A["qbd_ok"], 1)
                    dve.wait_ge(A["eg_ok"], i + 1)
                    dve.scalar_tensor_tensor(sg, sg, 1.0, bank[0][:, :], ALU.add, ALU.mult).then_inc(A["sg_ok"], 1)
                    dve.wait_ge(A["kv_ps"], 2 * i + 2)
                    for bb in range(BPI):
                        for c in range(3):
                            k = dve.scalar_tensor_tensor(kvs[:, bb, c, :], update(bb, c), ends(bb, c), state_mask, ALU.mult, ALU.mult)
                    k.then_inc(A["kvs_ok"].sem, 1)
                    for c, (got, did) in ((1, ("kvs_ok", "s2_ok")), (2, ("s2_ok", "s3_ok"))):
                        dve.wait_ge(A[got].sem, A[got].at(i))
                        for bb in range(BPI):
                            k = dve.scalar_tensor_tensor(kvs[:, bb, c, :], kvs[:, bb, c - 1, :], ends(bb, c), kvs[:, bb, c, :],
                                                         ALU.mult, ALU.add)
                        k.then_inc(A[did].sem, 1)
                if i is not None:
                    scores(i, 0)
                    scores(i, 1)
                if j is not None:
                    dve.wait_ge(A["y_ps"], j + 1)
                    dve.tensor_tensor(nn, quads(6), x2, ALU.add).then_inc(A["y_ok"], 1)
                if i is not None:
                    scores(i, 2)
                    scores(i, 3)
                if j is not None:
                    dve.wait_ge(A["x1_ok"], j + 1)
                    for t in range(TPI):
                        k = dve.bn_stats(st2[:, t, :], xall[:, ds(TPI * j + t, 1), :])
                    k.then_inc(A["bn2"].sem, 1)
                    moments(st2, mv2, sm2, j, "bn2", "sm2", "sd2", "mv2")
                    dve.wait_ge(A["mv2"].sem, A["mv2"].at(j))
                    dve.tensor_scalar(ve3, mv2[:, 1, :], LN_EPS, None, ALU.add).then_inc(A["ve3_ok"].sem, 1)
                    newton(dve, ve3, rr3, rt3, j, "r3a", "r3b", "r3c", "rstd3_ok")
                    dve.wait_ge(A["rstd3_ok"].sem, A["rstd3_ok"].at(j))
                    for t in range(TPI):
                        k = dve.tensor_scalar(nn[:, t, :], xall[:, ds(TPI * j + t, 1), :].squeeze(1), mv2[:, 0, t:t + 1], rr3[:, t:t + 1],
                                              ALU.subtract, ALU.mult)
                    k.then_inc(A["xn2_ok"], 1)
                if i is not None:
                    dve.wait_ge(A["rstd_ok"].sem, A["rstd_ok"].at(i))
                    dve.tensor_tensor(sq, bank[0][:, :], sq, ALU.mult).then_inc(A["t1_ok"].sem, 1)
                    dve.wait_ge(A["t1_ok"].sem, A["t1_ok"].at(i))
                    dve.wait_ge(A["sg_ok"], i + 1)
                    dve.tensor_tensor(uu, sq, sg, ALU.mult).then_inc(A["u_ok"].sem, 1)
                    dve.wait_ge(A["at_ps"].sem, A["at_ps"].at(i))
                    if j is not None:
                        dve.wait_ge(A["xT_ps"], j + 1)
                    dve.tensor_tensor(x2, quads(1), xn, ALU.add).then_inc(A["x2_ok"].sem, 1)

            def moments(stats, mv, t, n, got, first, second, done, A=A):
                dve.wait_ge(A[got].sem, A[got].at(n))
                dve.tensor_tensor(t[:, 0, :], stats[:, :, 1], stats[:, :, 4], ALU.add)
                dve.tensor_tensor(t[:, 1, :], stats[:, :, 1], stats[:, :, 4], ALU.subtract)
                dve.tensor_tensor(t[:, 2, :], stats[:, :, 2], stats[:, :, 5], ALU.add).then_inc(A[first].sem, 1)
                dve.wait_ge(A[first].sem, A[first].at(n))
                dve.tensor_scalar(mv[:, 0, :], t[:, 0, :], 0.5, None, ALU.mult)
                dve.scalar_tensor_tensor(t[:, 1, :], t[:, 1, :], 0.25, t[:, 1, :], ALU.mult, ALU.mult).then_inc(A[second].sem, 1)
                dve.wait_ge(A[second].sem, A[second].at(n))
                dve.scalar_tensor_tensor(mv[:, 1, :], t[:, 2, :], 1.0 / D, t[:, 1, :], ALU.mult, ALU.add).then_inc(A[done].sem, 1)

            def newton(eng, v, r, t, n, first, second, third, done, A=A):
                eng.wait_ge(A[first].sem, A[first].at(n))
                eng.tensor_tensor(t, r, r, ALU.mult).then_inc(A[second].sem, 1)
                eng.wait_ge(A[second].sem, A[second].at(n))
                eng.scalar_tensor_tensor(t, t, -0.5, v, ALU.mult, ALU.mult).then_inc(A[third].sem, 1)
                eng.wait_ge(A[third].sem, A[third].at(n))
                eng.scalar_tensor_tensor(r, t, 1.5, r, ALU.add, ALU.mult).then_inc(A[done].sem, 1)

            def ends(bb, c):
                at = bb * T + (c + 1) * CHUNK - 1
                return ebq[:, at:at + 1]

            def silu_gate(j, m):
                n = MROWS[m]
                dve.wait_ge(A["eg2_ok"], j * MT + m + 1)
                dve.scalar_tensor_tensor(eg[0:n, m % 2, :], eg[0:n, m % 2, :], 1.0, bank[[6, 5, 7][m]][0:n, :], ALU.add, ALU.mult)\
                    .then_inc(A["si_ok"], 1)

            def times_up(j, m):
                n = MROWS[m]
                dve.wait_ge(A["up_ps"], j * MT + m + 1)
                dve.wait_ge(A["si_ok"], j * MT + m + 1)
                dve.tensor_tensor(hid[0:n, m, :], bank[[7, 6, 5][m]][0:n, :], eg[0:n, m % 2, :], ALU.mult).then_inc(A["hid_ok"], 1)

            def scores(i, t):
                dve.wait_ge(S["am0"], 1)
                dve.wait_ge(a_ps[t], i + 1)
                dve.copy_predicated(am[:, t, :], causal, bank[[4, 2][t % 2]][:, :]).then_inc(A["am_ok"], 1)

            slots(dve, first)

            def phase(step):
                d = step(3)
                s = step(0)
                if s is not None:
                    dve.wait_ge(B["hi_ok"], s.count(1, 1))
                    for at, j in ((0, 1), (T, 0)):
                        k = dve.scalar_tensor_tensor(hl[s.n2][:, 1, at:at + T], bank[6][:, at:at + T], bcol[:, s.c, j:j + 1],
                                                     hl[s.n2][:, 0, at:at + T].bitcast(F32), ALU.add, ALU.subtract)
                    k.then_inc(B["lo_ok"], 1)
                x = step(2)
                for u in range(UNITS):
                    maxes(*ahead(step, u + 2))
                    if x is not None and u not in ACT_UNITS:
                        copy_unit(dve, x, u)
                    if u == 1 and d is not None:
                        dve.wait_ge(B["rawT_ps"].sem, B["rawT_ps"].at(d.number()))
                        t = bank[4 + d.n2][:, :].rearrange("p (a w) -> p a w", w=VW)
                        dve.reciprocal(rec, t[:, :, DH]).then_inc(B["rec_ok"].sem, 1)
                        last = d.back(1)
                        if last is not None:
                            dve.wait_ge(B["ctxT_ps"].sem, B["ctxT_ps"].at(last.number()))
                        dve.wait_ge(B["rec_ok"].sem, B["rec_ok"].at(d.number()))
                        dve.tensor_tensor(ctxc.rearrange("p t (h d) -> p (t h) d", h=H), t[:, :, 0:DH],
                                          rec.unsqueeze(2).to_broadcast([P, KT * H, DH]), ALU.mult).then_inc(B["ctxc_ok"].sem, 1)
                    if d is not None and d.c == NODES - 1:
                        f = d.it * LIVE + d.b
                        if u == 5:
                            dve.wait_ge(B["node_ps"].sem, B["node_ps"].at(d.number()))
                            dve.wait_ge(B["fy_free"], f + 1)
                            dve.tensor_tensor(fy, bank[4 + d.n2][:, T:2 * T].rearrange("p (t d) -> p t d", t=KT),
                                              nb5[:, :].unsqueeze(1).to_broadcast([P, KT, D]), ALU.add).then_inc(B["fin_read"].sem, 1)
                            dve.wait_ge(B["fin_read"].sem, B["fin_read"].at(f))
                            for t in range(KT):
                                k = dve.bn_stats(fst[:, t, :], fy[:, t, :])
                            k.then_inc(B["fbn"].sem, 1)
                        if u == 6:
                            moments(fst, fmv, fsm, f, "fbn", "fsm", "fsd", "fmv", B)
                            dve.wait_ge(B["fmv"].sem, B["fmv"].at(f))
                            dve.tensor_scalar(fve, fmv[:, 1, :], FFN_LN_EPS, None, ALU.add).then_inc(B["fve_ok"].sem, 1)
                        if u == 7:
                            newton(dve, fve, fr, frt, f, "fra", "frb", "frc", "fr_ok", B)
                            dve.wait_ge(B["fr_ok"].sem, B["fr_ok"].at(f))
                            for t in range(KT):
                                k = dve.tensor_scalar(fy[:, t, :], fy[:, t, :], fmv[:, 0, t:t + 1], fr[:, t:t + 1], ALU.subtract, ALU.mult)
                            k.then_inc(B["fyn_ok"].sem, 1)

            def maxes(s, u):
                if s is None:
                    return
                dve.wait_ge(B["s_ps"], s.count(UNITS, u + 1))
                dve.tensor_reduce(mx[s.n2][:, u, :], score_bank(s, u)[:, :].rearrange("p (h k) -> p h k", h=2), AX_X, ALU.max,
                                  negate=True).then_inc(B["max_ok"], 1)
            node_slots(dve, phase)

        @block.tensor
        def _(pe):
            def mm(o, w, x, start=True, stop=True, skip=False):
                return pe.matmul(o, w, x, start=start, stop=stop, skip_group_check=skip)

            pe.wait_ge(L["const_in"], 16)
            pe.wait_ge(L["gk_in"], 48)
            pe.transpose(bank[6][0:RANK, 0:P], wgk1, ident).then_inc(S["gk1_t"].sem, 1)
            pe.wait_ge(S["gk1_c"].sem, S["gk1_c"].at(0))
            mm(bank[6][:, 128:128 + QK], wgk1T, wgk2).then_inc(S["gk_ps"].sem, 1)
            pe.wait_ge(L["nodew_in"], 16 * 6)
            pe.transpose(bank[7][:, 0:EDGES], be_rows, ident[0:EDGES, 0:EDGES]).then_inc(S["be_t"], 1)
            w3 = wqkv_raw.rearrange("p j (c n) -> p j c n", c=NODES)
            for c in range(NODES + 1):
                if c < NODES:
                    if c >= 2:
                        pe.wait_ge(S["we_c"], c - 1)
                    for j in range(3):
                        k = pe.transpose(bank[c % 2][:, j * D:(j + 1) * D], we_raw[:, GRAPH[c]["e"][j], :], ident)
                    k.then_inc(S["we_t"], 1)
                if c >= 1:
                    b = c - 1
                    pe.wait_ge(S["we_c"], b + 1)
                    if b >= 2:
                        pe.wait_ge(S["fold_ok"], b - 1)
                    for j in range(3):
                        k = mm(bank[2 + b % 2][:, j * D:(j + 1) * D], weT[:, b % 2, j * D:(j + 1) * D], w3[:, j, b, :])
                    k.then_inc(S["fold_ps"], 1)
            pe.wait_ge(S["be_c"], 1)
            for c in range(NODES):
                for j in range(3):
                    e = GRAPH[c]["e"][j]
                    k = mm(bank[4][:, 3 * c + j:3 * c + j + 1], w3[:, j, c, :], beT[:, e:e + 1])
            k.then_inc(S["bias_ps"].sem, 1)
            pe.wait_ge(S["bias_c"].sem, S["bias_c"].at(0))
            for c in range(NODES):
                k = mm(bank[5][:, c:c + 1], wo_raw[:, c, :], bprod[:, c, 2:3])
            k.then_inc(S["bo_ps"].sem, 1)
            pe.wait_ge(S["nb_b"].sem, S["nb_b"].at(0))
            pe.wait_ge(S["wa_ok"], 1)
            mm(bank[6][:, 256:256 + D], nb5w, ident).then_inc(S["nb_ps"].sem, 1)
            pe.wait_ge(S["prep_d"], 1)

            def first(i, j):
                if j is not None:
                    pe.wait_ge(A["n_ok"], j + 1)
                    for t in range(TPI):
                        k = pe.transpose(bank[5][:, t * P:(t + 1) * P], nn[:, t, :], ident)
                    k.then_inc(A["nT_ps"], 1)
                    pe.wait_ge(A["nT_ok"], j + 1)
                    hidden(j, 0, 0, 6)
                    hidden(j, 1, 0, 7)
                    hidden(j, 0, 1, 5)
                if i is not None:
                    pe.wait_ge(A["h_ok"], i + 1)
                    for t in range(TPI):
                        k = pe.transpose(bank[0][:, t * P:(t + 1) * P], hh[:, t, :], ident)
                    k.then_inc(A["hT_ps"], 1)
                    pe.wait_ge(A["hT_ok"], i + 1)
                    for t in range(TPI):
                        k = mm(bank[1][:, t * QK:(t + 1) * QK], hT[:, t * P:(t + 1) * P], wz[:, :])
                    k.then_inc(A["z_ps"], 1)
                    mm(bank[2][0:QK, :], wa[:, 0:QK], hT).then_inc(A["q_ps"], 1)
                    mm(bank[3][0:QK, :], wa[:, QK:2 * QK], hT).then_inc(A["k_ps"], 1)
                    for t in range(TPI):
                        k = mm(bank[4][:, t * P:(t + 1) * P], hT[:, t * P:(t + 1) * P], wa[:, 2 * QK:2 * QK + D])
                    k.then_inc(A["v_ps"], 1)
                    mm(bank[0][:, :], wa[:, 2 * QK + D:], hT).then_inc(A["g_ps"], 1)
                if j is not None:
                    pe.wait_ge(A["si_ok"], j * MT + 1)
                    hidden(j, 1, 1, 6)
                    pe.wait_ge(A["hid_ok"], j * MT + 1)
                    hidden(j, 0, 2, 7)
                if i is not None:
                    pe.wait_ge(A["gl_ok"].sem, A["gl_ok"].at(i))
                    for t in range(TPI):
                        k = mm(bank[1][0:QK, t * P:(t + 1) * P], gl[:, t, :], cum)
                    k.then_inc(A["b_ps"], 1)
                if j is not None:
                    pe.wait_ge(A["si_ok"], j * MT + 2)
                    hidden(j, 1, 2, 5)
                if i is not None:
                    pe.wait_ge(L["const_in"], 16)
                    pe.wait_ge(A["ke_ok"], i + 1)
                    for t in range(TPI):
                        k = pe.transpose(bank[2][:, t * QK:(t + 1) * QK], ke[:, t * P:(t + 1) * P], ident[0:QK, 0:QK])
                    k.then_inc(A["keT_ps"], 1)
                    pe.wait_ge(L["const_in"], 16)
                    pe.wait_ge(A["keT_ok"], i + 1)
                    pe.wait_ge(A["v_ok"], i + 1)
                    for odd in range(2):
                        r = CHUNK * odd
                        for bb in range(BPI):
                            for c in range(odd, 3, 2):
                                t = bb * KT + c // 2
                                k = mm(update(bb, c), keT[r:r + CHUNK, t, :], vsb[r:r + CHUNK, t, :])
                        k.then_inc(A["kv_ps"], 1)
                if j is not None:
                    pe.wait_ge(A["hid_ok"], j * MT + MT)
                    for t in range(TPI):
                        for m in range(MT):
                            k = mm(bank[6][:, t * P:(t + 1) * P], hid[0:MROWS[m], m, t * P:(t + 1) * P], wd[0:MROWS[m], m, :],
                                   start=(m == 0), stop=(m == MT - 1))
                    k.then_inc(A["y_ps"], 1)
                if i is not None:
                    pe.wait_ge(A["qbd_ok"], i + 1)
                    for t in range(TPI):
                        if t >= 2:
                            pe.wait_ge(A["am_ok"], TPI * i + t - 1)
                        mm(bank[[4, 2][t % 2]][:, :].rearrange("p (h c) -> p h c", h=GH), ke[:, t * P:(t + 1) * P],
                           qbd[:, :, t * P:(t + 1) * P]).then_inc(a_ps[t], 1)
                    pe.wait_ge(A["sg_ok"], i + 1)
                    pe.wait_ge(A["s3_ok"].sem, A["s3_ok"].at(i))
                    for t in range(TPI):
                        pe.wait_ge(A["am_ok"], TPI * i + t + 1)
                        for h in range(GH):
                            mm(bank[0][DV * h:DV * h + DV, t * P:(t + 1) * P], vsb[:, t, DV * h:DV * h + DV],
                               am[:, t, h * P:(h + 1) * P], stop=False, skip=True)
                        for cc in range(2):
                            c = 2 * (t % KT) + cc
                            if c > 0:
                                at = t * P + cc * CHUNK
                                k = mm(bank[0][:, at:at + CHUNK], kvs[:, t // KT, c - 1, :], qe[:, at:at + CHUNK],
                                       start=False, skip=True)
                    k.then_inc(A["o_ps"].sem, 1)
                if j is not None:
                    pe.wait_ge(A["xn2_ok"], j + 1)
                    for t in range(TPI):
                        k = pe.transpose(bank[7][:, t * P:(t + 1) * P], nn[:, t, :], ident)
                    k.then_inc(A["xT_ps"], 1)
                if i is not None:
                    pe.wait_ge(A["sq_ok"].sem, A["sq_ok"].at(i))
                    mm(bank[3][:, :], mean_dv, sq).then_inc(A["ms_ps"].sem, 1)
                    pe.wait_ge(A["u_ok"].sem, A["u_ok"].at(i))
                    for t in range(TPI):
                        k = mm(bank[1][:, t * P:(t + 1) * P], uu[:, t * P:(t + 1) * P], wo[:, :])
                    k.then_inc(A["at_ps"].sem, 1)

            def hidden(j, which, m, to):
                mm(bank[to][0:MROWS[m], :], wgu[:, which, m * P:m * P + MROWS[m]], nT).then_inc(A[["gate_ps", "up_ps"][which]], 1)
            slots(pe, first)

            pe.wait_ge(A["xT_ok"], ITERS)

            def source(s, n):
                return x0T[:, s.b, :] if n < 0 else node[:, s.b, n, :]

            def pv(s, g):
                upto = UNITS // 2 * (g + 1)
                pe.wait_ge(B["pT_dve"], copies(s, upto, "dve"))
                pe.wait_ge(B["pT_act"], copies(s, upto, "act"))
                if g == 0:
                    pe.wait_ge(B["vals_ok"], s.count(1, 1))
                    old = s.back(2)
                    if old is not None:
                        if old.c < NODES - 1:
                            pe.wait_ge(B["node_ok"], old.nodes())
                        else:
                            pe.wait_ge(B["fin_read"].sem, B["fin_read"].at(old.finals() - 1))
                for kt in range(KT):
                    for j in range(GCOL):
                        h = g * GCOL + j
                        k = mm(bank[4 + s.n2][32 * j:32 * j + 32, g * T:(g + 1) * T], vaug[s.b][:, kt, VW * h:VW * h + VW],
                               probT[:, h, kt * T:(kt + 1) * T], start=(kt == 0), stop=(kt == KT - 1), skip=True)
                k.then_inc(B["pv_ok"], 1)

            def phase(step):
                d = step(3)
                if d is not None:
                    pv(d, 1)
                s = step(0)
                if s is not None:
                    g = GRAPH[s.c]["src"]
                    pe.wait_ge(x0_in[s.b], 16 * s.it + 16)
                    if s.c > 0:
                        pe.wait_ge(B["node_ok"], s.back(LIVE).nodes())
                    last = s.back(1)
                    if last is not None:
                        pe.wait_ge(B["vals_ok"], last.count(1, 1))
                    mm(bank[6][:, 0:T], w_fold[:, s.c, 1, :], source(s, g[1]))
                    mm(bank[6][:, T:2 * T], w_fold[:, s.c, 0, :], source(s, g[0])).then_inc(B["qk_ps"], 1)
                x = step(2)
                for u in range(UNITS):
                    if x is not None:
                        pe.wait_ge(B["exp_ok"], x.count(UNITS, u + 1))
                        if u >= 2 or x.back(1) is not None:
                            w, v = (x, u - 2) if u >= 2 else (x.back(1), u + UNITS - 2)
                            e = "act" if v in ACT_UNITS else "dve"
                            pe.wait_ge(B["pT_" + e], copies(w, v + 1, e))
                        for k in range(2):
                            for kt in range(KT):
                                o = (k * KT + kt) * P
                                i = pe.transpose(bank[2 + u % 2][:, o:o + P], prob[u % 2][:, k, kt * P:(kt + 1) * P], ident)
                        i.then_inc(B["pT_ps"], 1)
                    scores(*ahead(step, u + 3))
                    if u == 1 and d is not None:
                        pe.wait_ge(B["raw_ok"].sem, B["raw_ok"].at(d.number()))
                        for qt in range(KT):
                            for g in range(2):
                                a = (qt * 2 + g) * P
                                k = pe.transpose(bank[4 + d.n2][:, a:a + P], raw[:, g * T + qt * P:g * T + (qt + 1) * P], ident)
                        k.then_inc(B["rawT_ps"].sem, 1)
                    if u == 2 and s is not None:
                        pe.wait_ge(B["lo_ok"], s.count(1, 1))
                        for kt in range(KT):
                            k = mm(bank[6][:, kt * P:(kt + 1) * P], source(s, GRAPH[s.c]["src"][2])[:, kt * P:(kt + 1) * P], w_fold[:, s.c, 2, :])
                        k.then_inc(B["v_ps2"], 1)
                    if u == 3 and d is not None:
                        pe.wait_ge(B["ctxc_ok"].sem, B["ctxc_ok"].at(d.number()))
                        for qt in range(KT):
                            k = pe.transpose(bank[4 + d.n2][:, qt * P:(qt + 1) * P], ctxc[:, qt, :], ident)
                        k.then_inc(B["ctxT_ps"].sem, 1)
                    if u == 5 and d is not None:
                        project(d)
                    if u == 6 and x is not None:
                        pv(x, 0)

            def scores(s, u):
                if s is None:
                    return
                pr, qt = u // KT, u % KT
                if u == 0:
                    pe.wait_ge(stacked[s.b], s.stacks())
                back = s.count(UNITS, u - 2)
                if not (isinstance(back, int) and back < 1):
                    pe.wait_ge(B["exp_ok"], back)
                mm(score_bank(s, u)[:, :].rearrange("p (h k) -> p h k", h=2), qs[s.b][:, pr, qt * P:(qt + 1) * P],
                   kz[s.b][:, 2 * pr:2 * pr + 2, :]).then_inc(B["s_ps"], 1)

            def project(d):
                to, prev, ctx_n = bank[4 + d.n2], source(d, GRAPH[d.c]["src"][0]), ctxT[d.n2]
                pe.wait_ge(B["ctxT_ok"].sem, B["ctxT_ok"].at(d.number()))
                if d.c < NODES - 1:
                    mm(to[:, T:2 * T], w_res[:, d.c, :], prev, stop=False)
                    mm(to[:, T:2 * T], w_out[:, d.c, :], ctx_n, start=False).then_inc(B["node_ps"].sem, 1)
                else:
                    for t in range(KT):
                        r, o = slice(t * P, (t + 1) * P), slice(T + t * P, T + (t + 1) * P)
                        mm(to[:, o], prev[:, r], w_res[:, d.c, :], stop=False)
                        k = mm(to[:, o], ctx_n[:, r], w_out[:, d.c, :], start=False)
                    k.then_inc(B["node_ps"].sem, 1)
            node_slots(pe, phase)


_INS = ['L0_attn_hidden_states', 'L0_attn_attn_norm_w', 'L0_attn_Wq', 'L0_attn_Wk', 'L0_attn_Wv', 'L0_attn_Wg', 'L0_attn_Wgk1',
        'L0_attn_Wgk2', 'L0_attn_bgk2', 'L0_attn_gnorm_w', 'L0_attn_Wo', 'L0_attn_mlp_norm_w', 'L0_attn_W_gate', 'L0_attn_W_up',
        'L0_attn_W_down', 'L0_ffn_ew', 'L0_ffn_act_w', 'L0_ffn_We', 'L0_ffn_be', 'L0_ffn_Wq', 'L0_ffn_Wk', 'L0_ffn_Wv',
        'L0_ffn_Wo', 'L0_ffn_ln_g', 'L0_ffn_ln_b']


def kernel(**inputs):
    import concourse.bacc as _bacc
    from concourse.bass_utils import run_bass_kernel_spmd as _run

    nc = _bacc.Bacc("TRN2", target_bir_lowering=False, num_devices=1)
    arrays, aps = {}, {}
    for name in _INS:
        v = np.ascontiguousarray(inputs[name])
        arrays[f"in_{name}"] = v
        aps[name] = nc.dram_tensor(f"in_{name}", v.shape, mybir.dt.from_np(v.dtype), kind="ExternalInput").ap()
    arrays["in_constants"] = constants()
    consts = nc.dram_tensor("in_constants", (P, C_END), F32, kind="ExternalInput").ap()
    out = nc.dram_tensor("out_0", (BATCH, T, D), F32, kind="ExternalOutput").ap()
    build(nc, aps, consts, out)
    r = _run(nc, [arrays], core_ids=[0])
    return r.results[0]["out_0"]
```

```python
from contextlib import ExitStack

import numpy as np

import concourse.bass as bass
from concourse import mybir

ALU = mybir.AluOpType
ACT = mybir.ActivationFunctionType
AX_X = mybir.AxisListType.X
F32 = mybir.dt.float32
F32R = mybir.dt.float32r
U32 = mybir.dt.uint32

P = 128
D = 128
BATCH, T = 16, 256
TILES = BATCH * T // P
LN_EPS, RMS_EPS, FFN_LN_EPS = 1e-5, 1e-6, 1e-6

GH, DK, DV, CHUNK = 4, 16, 32, 64
QK = GH * DK
GATE_NORM = 16.0
RANK = 16
MLP = 352
MT = 3
MROWS = [128, 128, MLP - 256]
TPI = 4
TOK = TPI * P
ITERS = TILES // TPI
BPI = TOK // T

NODES, MAX_PREV, EDGES = 6, 5, 20
H, DH = 8, 16
PAIRS = H // 2
KT = T // P
LIVE = 4
STEPS = NODES * LIVE
GROUPS = BATCH // LIVE
GCOL = 4
VW = 32
PARTS = 3
ROWS = PARTS * 32
UNITS = PAIRS * KT
AT = dict(pv1=2, qk=8, rawT=11, v=14, ctxT=14, proj=17, pv0=23, a_raw=5, a_qk=11, a_v=23, a_ctxT=14, a_node=23, d_ctx=11, f0=23, f1=23, a_f=23, f2=23)
S_LEAD, MAX_LEAD, EXP_LEAD = 3, 2, 1
PROBS = 2
PE_SWAP = 0
SBANK = (0, 1, 7)
ACT_UNITS = (2, 7)
STACK_DMAS = PARTS * 3


def graph():
    out, at = [], 0
    for c in range(NODES):
        n = min(c + 1, MAX_PREV)
        s = c - n
        out.append(dict(e=(at + n - 1, at, at + n // 2), src=(c - 1, s, s + n // 2)))
        at += n
    return out


GRAPH = graph()


LOGS = "natural_log_exp_and_others"
GATE_BANK, UP_BANK = (6, 7, 6), (6, 7, 7)


class Event:

    def __init__(self, sem, place, events):
        self.sem, self.place, self.events = sem, place, events

    def at(self, n):
        return n * self.events + self.place

C_ID, C_CUM, C_MASK, C_MEAN, C_HEAD, C_STATE, C_END = 0, 128, 256, 768, 896, 900, 1028


def constants():
    c = np.zeros((P, C_END), np.float32)
    i = np.arange(P)
    c[:, C_ID:C_ID + P] = np.eye(P)
    causal = (i[:, None] <= i[None, :]) & (i[:, None] // CHUNK == i[None, :] // CHUNK)
    c[:, C_CUM:C_CUM + P] = causal
    c[:, C_MASK:C_MASK + GH * P] = np.tile(causal, (1, GH))
    c[:, C_MEAN:C_MEAN + P] = (i[:, None] // DV == i[None, :] // DV) / DV
    r = np.arange(QK)
    c[:QK, C_HEAD:C_HEAD + GH] = r[:, None] // DK == np.arange(GH)[None, :]
    c[:QK, C_STATE:C_STATE + P] = r[:, None] // DK == i[None, :] // DV
    return c


def build(nc, a, consts, out):
    ds = bass.ds
    with ExitStack() as ctx:
        def sb(name, shape, dt=F32):
            return ctx.enter_context(nc.sbuf_tensor(name, shape, dt))

        def sem(name):
            return ctx.enter_context(nc.semaphore(name))

        bank = [ctx.enter_context(nc.psum_tensor(f"bank{n}", [P, 512], F32)) for n in range(8)]

        def quads(n):
            return bank[n][:, :].rearrange("p (t d) -> p t d", t=4)

        cst = sb("cst", [P, C_END])
        ident = cst[:, C_ID:C_ID + P]
        cum = cst[:, C_CUM:C_CUM + P]
        causal = cst[:, C_MASK:C_MASK + GH * P].bitcast(U32)
        mean_dv = cst[:, C_MEAN:C_MEAN + P]
        head_mask = cst[0:QK, C_HEAD:C_HEAD + GH]
        state_mask = cst[0:QK, C_STATE:C_STATE + P]
        xall = sb("xall", [P, TILES, D])
        xT = sb("xT", [P, TILES * P])
        wa = sb("wa", [P, 2 * QK + 2 * D])
        wz = sb("wz", [P, QK])
        wo = sb("wo", [P, D])
        wgu = sb("wgu", [P, 2, MLP])
        wd = sb("wd", [P, MT, D])
        bgk = sb("bgk", [P, QK])
        eps_col = sb("eps_col", [P, 1])
        one_col = sb("one_col", [P, 1])
        cols = sb("cols", [P, 3])
        w_res = sb("w_res", [P, NODES, D])
        w_fold = sb("w_fold", [P, NODES, 3, D])
        w_out = sb("w_out", [P, NODES, D])
        bcol = sb("bcol", [P, NODES, 3])
        nb5 = sb("nb5", [P, D])
        lng = sb("lng", [P, 2, D])
        scal = sb("scal", [P, NODES * 4])
        kz = [sb(f"kz{b}", [ROWS, H, T], F32R) for b in range(LIVE)]
        qs = [sb(f"qs{b}", [ROWS, PAIRS, T], F32R) for b in range(LIVE)]
        hl = [sb(f"hl{n}", [P, 2, 2 * T], F32R) for n in range(2)]
        parts = nc.dram_tensor("parts", (LIVE, P, 2, 2 * T), F32, kind="Internal").ap()

        UW = 16900
        region = sb("region", [P, UW])

        def carver():
            at = [0]

            def carve(*dims, rows=P):
                n = int(np.prod(dims))
                v = region[0:rows, at[0]:at[0] + n]
                at[0] += n
                assert at[0] <= UW, at[0]
                if len(dims) == 2:
                    v = v.rearrange("p (a b) -> p a b", a=dims[0])
                elif len(dims) == 3:
                    v = v.rearrange("p (a b c) -> p a b c", a=dims[0], b=dims[1])
                return v
            return carve, at

        carve, _ = carver()
        xn = carve(TPI, D)
        hh = carve(TPI, D)
        hT = carve(TOK)
        zb = carve(TPI, QK)
        za = carve(TPI, QK)
        gl = carve(TPI, QK)
        ebq = carve(TOK, rows=QK)
        ebk = carve(TOK, rows=QK)
        qe = carve(TOK, rows=QK)
        ke = carve(TOK, rows=QK)
        qbd = carve(GH, TOK, rows=QK)
        vsb = carve(TPI, D)
        sg = carve(TOK)
        keT = carve(TPI, QK)
        am = carve(TPI, GH * P)
        kvs = carve(BPI, 3, D, rows=QK)
        osb = carve(TOK)
        sq = carve(TOK)
        uu = carve(TOK)
        x2 = carve(TPI, D)
        nn = carve(TPI, D)
        x1n = carve(TPI, D)
        nT = carve(TOK)
        eg = carve(2, TOK)
        hid = carve(MT, TOK)
        st = carve(TPI, 6)
        mv = carve(2, TPI)
        sm = carve(3, TPI)
        ve = carve(2, TPI)
        rr = carve(2, TPI)
        rt = carve(2, TPI)
        st2 = carve(TPI, 6)
        mv2 = carve(2, TPI)
        sm2 = carve(3, TPI)
        ss = carve(TPI)
        ve2 = carve(TPI)
        rr2 = carve(TPI)
        rt2 = carve(TPI)
        ve3 = carve(TPI)
        rr3 = carve(TPI)
        rt3 = carve(TPI)
        carve, at = carver()
        at[0] = 0
        we_raw = carve(EDGES, D)
        wqkv_raw = carve(3, NODES * D)
        wo_raw = carve(NODES, D)
        weT = carve(2, 3 * D)
        be_rows = carve(D, rows=EDGES)
        beT = carve(EDGES)
        bprod = carve(NODES, 4)
        wgk1 = carve(RANK)
        wgk1T = carve(P, rows=RANK)
        wgk2 = carve(QK, rows=RANK)
        nb5w = carve(D)
        carve, _ = carver()
        x0T = carve(LIVE, T)
        node = carve(LIVE, NODES - 1, T)
        vaug = [carve(KT, H * VW) for _ in range(LIVE)]
        prob = [carve(2, T) for _ in range(PROBS)]
        probT = carve(H, KT * T)
        raw = carve(2 * T)
        rec = carve(KT * H)
        ctxc = carve(KT, D)
        qk = [carve(2 * T) for _ in range(2)]
        ctxT = [carve(T) for _ in range(2)]
        mx = [carve(UNITS, 2) for _ in range(2)]
        fy = carve(KT, D)
        fst = carve(KT, 6)
        fmv = carve(2, KT)
        fsm = carve(3, KT)
        fve = carve(KT)
        fr = carve(KT)
        frt = carve(KT)

        def names(text):
            return {n: sem(n) for n in text.split()}

        def chain(name, events):
            one, events = sem(name), events.split()
            return {e: Event(one, k + 1, len(events)) for k, e in enumerate(events)}

        L = names("x_in const_in wa_in gk_in wo_in mlp_in cols_in nodew_in scal_in ln_in")
        S = names("wz_ok wa_ok wfirst_ok we_t we_c fold_ps fold_ok be_t be_c "
                  "bias_w w_out_ok am0 eps_ok one_ok zero_ok prep_a prep_d")
        A = names("xn_ok h_ok hT_ps hT_ok z_ps b_ps eb_ok q_ps k_ps qe_ok ke_ok qbd_ok "
                  "v_ps v_ok g_ps eg_ok sg_ok keT_ps keT_ok kv_ps am_ok "
                  "n_ok nT_ps nT_ok gate_ps up_ps eg2_ok si_ok hid_ok y_ps res_ok x1_ok xn2_ok "
                  "xT_ps xT_ok")
        B = names("qk_ps v_ps2 qk_ok hi_ok lo_ok vals_ok s_ps max_ok exp_ok pT_ps pT_act pT_dve pv_ok "
                  "node_ok vones fy_free out_stored")
        A.update(chain("ln1", "bn1 sm1 sd1 mv1 ve_ok rl ra rb rc rstd1_ok"))
        A.update(chain("rms2", "ve2_ok r2l r2a r2b r2c rstd2_ok"))
        A.update(chain("ln2", "bn2 sm2 sd2 mv2 ve3_ok r3l r3a r3b r3c rstd3_ok"))
        B.update(chain("fin", "fin_read fbn fsm fsd fmv fve_ok frl fra frb frc fr_ok fyn_ok fg_ok fb_ok"))
        A.update(chain("logsig", "zb_ok za_ok e_ok l_ok gl_ok"))
        A.update(chain("state", "kvs_ok s2_ok s3_ok"))
        A.update(chain("outs", "o_ps o_ok"))
        A.update(chain("heads", "sq_ok ms_ps msl_ok rstd_ok t1_ok u_ok at_ps x2_ok ss_ok"))
        S.update(chain("gk", "gk1_t gk1_c gk_ps"))
        S.update(chain("bias", "bias_ps bias_c bo_ps bo_ok bias_f nb_b nb_ps"))
        B.update(chain("ctx", "raw_ok rawT_ps rec_ok ctxc_ok ctxT_ps ctxT_ok node_ps"))
        a_ps = [sem(f"a_ps{t}") for t in range(TPI)]
        stored = [sem(f"stored{n}") for n in range(2)]
        stacked = [sem(f"stacked{b}") for b in range(LIVE)]
        x0_in = [sem(f"x0_in{b}") for b in range(LIVE)]

        x_d = a["L0_attn_hidden_states"].rearrange("b t d -> (b t) d").rearrange("(n p) d -> p n d", p=P)
        out_d = out.rearrange("b t d -> (b t) d").rearrange("(n t p) d -> n p t d", t=KT, p=P)

        def col(v):
            return v.rearrange("(d a) -> d a", a=1)


        def slots(eng, body):
            for n in range(-1, 3):
                body(*(m if m >= 0 else None for m in (n + 1, n, n - 1, n - 2)))
            with eng.Fori(3, ITERS - 1) as n:
                body(n + 1, n, n - 1, n - 2)
            for n in range(ITERS - 1, ITERS + 2):
                body(*(m if m < ITERS else None for m in (n + 1, n, n - 1, n - 2)))


        LAST = STEPS * GROUPS

        def node_slots(eng, body, tail=4):
            def run(base, m):
                def step(off):
                    k = m - off
                    if isinstance(base, int):
                        n = base * STEPS + k
                        if n < 0 or n >= LAST:
                            return None
                        return Step(n // STEPS, n % STEPS)
                    return Step(base + k // STEPS, k % STEPS)
                body(step)

            for m in range(tail):
                run(0, m)
            with eng.Fori(0, GROUPS - 1) as i:
                for m in range(tail, tail + STEPS):
                    run(i, m)
            for m in range(tail, tail + STEPS):
                run(GROUPS - 1, m)

        class Step:
            def __init__(self, it, m):
                self.it, self.m, self.c, self.b = it, m, m // LIVE, m % LIVE
                self.n2 = m % 2

            def count(self, per=1, plus=0):
                return self.it * (STEPS * per) + (self.m * per + plus)

            def number(self):
                return self.count()

            def nodes(self):
                return self.it * ((NODES - 1) * LIVE) + min(self.m + 1, (NODES - 1) * LIVE)

            def finals(self):
                return self.it * LIVE + max(0, self.m + 1 - (NODES - 1) * LIVE)

            def back(self, k):
                if self.m >= k:
                    return Step(self.it, self.m - k)
                if isinstance(self.it, int) and self.it == 0:
                    return None
                return Step(self.it - 1, self.m - k + STEPS)

            def stacks(self):
                return self.it * (16 * STACK_DMAS * NODES) + 16 * STACK_DMAS * (self.c + 1)

        def ahead(step, u):
            return step(2 - u // UNITS), u % UNITS

        def score_bank(s, u):
            return bank[SBANK[(s.m * UNITS + u) % len(SBANK)]]

        def copy_unit(eng, x, u):
            pr, qt = u // KT, u % KT
            eng.wait_ge(B["pT_ps"], x.count(UNITS, u + 1))
            last = x.back(1)
            if last is not None and u in (0, 1, UNITS // 2, UNITS // 2 + 1):
                eng.wait_ge(B["pv_ok"], last.count(2, 2 * u // UNITS + 1))
            to = probT[:, 2 * pr:2 * pr + 2, :].rearrange("p h (k q) -> p h k q", k=KT)[:, :, :, qt * P:(qt + 1) * P]
            src = bank[2 + u % 2][:, :].rearrange("p (h k q) -> p h k q", h=2, k=KT)
            if u in ACT_UNITS:
                eng.activation(to, src, ACT.Copy).then_inc(B["pT_act"], 1)
            else:
                eng.tensor_copy(to, src).then_inc(B["pT_dve"], 1)

        def copies(s, upto, eng):
            mine = [u for u in range(UNITS) if (u in ACT_UNITS) == (eng == "act")]
            return s.count(len(mine), sum(u < upto for u in mine))

        def update(bb, c):
            at = (bb * 2 + c // 2) * D
            return bank[[3, 1][c % 2]][0:QK, at:at + D]

        block = ctx.enter_context(nc.Block())

        @block.sync
        def _(sp):
            sp.dma_start(cst[:, :], consts).then_inc(L["const_in"], 16)
            sp.dma_start(wo_raw, a["L0_ffn_Wo"].rearrange("c d n -> d c n")).then_inc(L["nodew_in"], 16)
            sp.dma_start(be_rows, a["L0_ffn_be"]).then_inc(L["nodew_in"], 16)
            sp.dma_start(cols[:, 0:1], col(a["L0_attn_attn_norm_w"])).then_inc(L["cols_in"], 16)
            sp.dma_start(cols[:, 1:2], col(a["L0_attn_mlp_norm_w"])).then_inc(L["cols_in"], 16)
            for h in range(GH):
                sp.dma_start(cols[DV * h:DV * h + DV, 2:3], col(a["L0_attn_gnorm_w"])).then_inc(L["cols_in"], 16)
            sp.dma_start(wa[:, 0:QK], a["L0_attn_Wq"]).then_inc(L["wa_in"], 16)
            sp.dma_start(wa[:, QK:2 * QK], a["L0_attn_Wk"]).then_inc(L["wa_in"], 16)
            sp.dma_start(wa[:, 2 * QK:2 * QK + D], a["L0_attn_Wv"]).then_inc(L["wa_in"], 16)
            sp.dma_start(wa[:, 2 * QK + D:], a["L0_attn_Wg"]).then_inc(L["wa_in"], 16)
            sp.dma_start(wo[:, :], a["L0_attn_Wo"]).then_inc(L["wo_in"], 16)
            sp.dma_start(wgu[:, 0, :], a["L0_attn_W_gate"]).then_inc(L["mlp_in"], 16)
            sp.dma_start(wgu[:, 1, :], a["L0_attn_W_up"]).then_inc(L["mlp_in"], 16)
            sp.dma_start(wd[:, 0:2, :], a["L0_attn_W_down"][0:256, :].rearrange("(m p) d -> p m d", p=P)).then_inc(L["mlp_in"], 16)
            sp.dma_start(wd[0:MROWS[2], 2, :], a["L0_attn_W_down"][256:MLP, :]).then_inc(L["mlp_in"], 16)
            for half in range(2):
                h = TILES // 2
                sp.dma_start(xall[:, half * h:(half + 1) * h, :], x_d[:, half * h:(half + 1) * h, :]).then_inc(L["x_in"], 16)

            def phase(step):
                s = step(0)
                if s is None:
                    return
                if isinstance(s.it, int) and s.it == 0 and s.m < LIVE:
                    sp.wait_ge(S["zero_ok"], s.b + 1)
                sp.wait_ge(B["lo_ok"], s.count(1, 1))
                sp.dma_start(parts[s.b], hl[s.n2][:, :, :].bitcast(F32)).then_inc(stored[s.n2], 16)
                sp.wait_ge(stored[s.n2], s.it * (16 * STEPS // 2) + 16 * (s.m // 2 + 1))
                for blk in range(PARTS):
                    kp, qp = blk % 2, blk // 2
                    rows = blk * 32
                    for odd in range(2):
                        src = parts[s.b, :, kp, 0:T].rearrange("(j s r) t -> s r j t", j=PAIRS, s=2)[odd]
                        sp.dma_start(kz[s.b][rows + 16 * odd:rows + 16 * odd + 16, odd::2, :].bitcast(F32), src)\
                            .then_inc(stacked[s.b], 16)
                    src = parts[s.b, :, qp, T:2 * T].rearrange("(j r) t -> r j t", j=PAIRS)
                    sp.dma_start(qs[s.b][rows:rows + 32, :, :].bitcast(F32), src).then_inc(stacked[s.b], 16)

            node_slots(sp, phase)

        @block.gpsimd
        def _(pool):
            pool.dma_start(scal[:, 0:18], a["L0_ffn_ew"].rearrange("a b -> (a b)").partition_broadcast(P)).then_inc(L["scal_in"], 16)
            pool.dma_start(scal[:, 18:24], a["L0_ffn_act_w"].partition_broadcast(P)).then_inc(L["scal_in"], 16)
            pool.dma_start(lng[:, 0, :], a["L0_ffn_ln_g"].partition_broadcast(P)).then_inc(L["ln_in"], 16)
            pool.dma_start(lng[:, 1, :], a["L0_ffn_ln_b"].partition_broadcast(P)).then_inc(L["ln_in"], 16)
            for b in range(LIVE):
                pool.memset(kz[b][:, :, :].bitcast(F32), 0.0).then_inc(S["zero_ok"], 1)
            pool.memset(eps_col[:, :], RMS_EPS).then_inc(S["eps_ok"], 1)
            pool.memset(one_col[:, :], 1.0).then_inc(S["one_ok"], 1)
            pool.wait_ge(S["prep_a"], 1)
            pool.wait_ge(S["prep_d"], 1)
            pool.memset(am, 0.0).then_inc(S["am0"], 1)

            def first(f, i, k, j):
                if k is not None:
                    pool.wait_ge(A["x2_ok"].sem, A["x2_ok"].at(k))
                    tiles = xall[:, ds(TPI * k, TPI), :]
                    pool.tensor_tensor(tiles, x2, tiles, ALU.add).then_inc(A["res_ok"], 1)
            slots(pool, first)

            pool.wait_ge(A["xT_ok"], ITERS)
            for b in range(LIVE):
                v = vaug[b].rearrange("p k (h w) -> p k h w", w=VW)
                pool.memset(v[:, :, :, DH + 1:], 0.0)
                pool.memset(v[:, :, :, DH:DH + 1], 1.0).then_inc(B["vones"], 1)
            pool.memset(fy, 0.0).then_inc(B["fy_free"], 1)
            for b in range(LIVE):
                pool.dma_start(x0T[:, b, :], xT[:, T * b:T * b + T]).then_inc(x0_in[b], 16)

            def phase(step):
                s = step(0)
                if s is not None:
                    pool.wait_ge(B["qk_ok"], s.count(1, 1))
                    old = s.back(2)
                    if old is not None:
                        pool.wait_ge(stored[s.n2], old.it * (16 * STEPS // 2) + 16 * (old.m // 2 + 1))
                    pool.tensor_tensor(hl[s.n2][:, 0, :], qk[s.n2], one_col[:, :].to_broadcast([P, 2 * T]), ALU.mult)\
                        .then_inc(B["hi_ok"], 1)
                    pool.wait_ge(B["hi_ok"], s.count(1, 1))
                    pool.tensor_tensor(hl[s.n2][:, 1, :], qk[s.n2], hl[s.n2][:, 0, :].bitcast(F32), ALU.subtract)\
                        .then_inc(B["lo_ok"], 1)
                s = step(1)
                if s is not None and s.c == NODES - 1:
                    pool.wait_ge(B["qk_ps"], s.count(1, 1))
                    if not (isinstance(s.it, int) and s.it == GROUPS - 1):
                        pool.dma_start(x0T[:, s.b, :], xT[:, ds((s.it + 1) * (LIVE * T) + s.b * T, T)])\
                            .then_inc(x0_in[s.b], 16)
                s = step(4)
                if s is not None and s.c == NODES - 1:
                    f = s.it * LIVE + s.b
                    tiles = xall[:, ds(f * KT, KT), :]
                    pool.wait_ge(B["fyn_ok"].sem, B["fyn_ok"].at(f))
                    pool.tensor_tensor(fy, fy, lng[:, 0:1, :].to_broadcast([P, KT, D]), ALU.mult).then_inc(B["fg_ok"].sem, 1)
                    pool.wait_ge(B["fg_ok"].sem, B["fg_ok"].at(f))
                    pool.tensor_tensor(fy, fy, lng[:, 1:2, :].to_broadcast([P, KT, D]), ALU.add).then_inc(B["fb_ok"].sem, 1)
                    pool.wait_ge(B["fb_ok"].sem, B["fb_ok"].at(f))
                    pool.tensor_tensor(tiles, fy, tiles, ALU.add).then_inc(B["fy_free"], 1)
                    pool.wait_ge(B["fy_free"], f + 2)
                    pool.dma_start(out_d[f], tiles).then_inc(B["out_stored"], 16)
            pool.wait_ge(L["ln_in"], 32)
            pool.wait_ge(S["one_ok"], 1)
            node_slots(pool, phase)
            pool.wait_ge(B["out_stored"], 16 * BATCH)

        @block.scalar
        def _(act):
            act.dma_start(wgk1, a["L0_attn_Wgk1"]).then_inc(L["gk_in"], 16)
            act.dma_start(wgk2, a["L0_attn_Wgk2"]).then_inc(L["gk_in"], 16)
            act.dma_start(bgk[:, :], a["L0_attn_bgk2"].partition_broadcast(P)).then_inc(L["gk_in"], 16)
            act.dma_start(we_raw, a["L0_ffn_We"].rearrange("e d n -> d e n")).then_inc(L["nodew_in"], 16)
            for j, w in enumerate(("Wq", "Wk", "Wv")):
                act.dma_start(wqkv_raw[:, j, :].rearrange("p (c n) -> p c n", c=NODES),
                              a["L0_ffn_" + w].rearrange("c d n -> d c n")).then_inc(L["nodew_in"], 16)
            act.wait_ge(S["gk1_t"].sem, S["gk1_t"].at(0))
            act.activation(wgk1T, bank[6][0:RANK, 0:P], ACT.Copy).then_inc(S["gk1_c"].sem, 1)
            act.wait_ge(S["be_t"], 1)
            act.activation(beT, bank[7][:, 0:EDGES], ACT.Copy).then_inc(S["be_c"], 1)
            for c in range(NODES):
                act.wait_ge(S["we_t"], c + 1)
                if c >= 2:
                    act.wait_ge(S["fold_ps"], c - 1)
                act.activation(weT[:, c % 2, :], bank[c % 2][:, 0:3 * D], ACT.Copy).then_inc(S["we_c"], 1)
            act.wait_ge(S["prep_d"], 1)
            act.copy(cols[:, 0:1], cols[:, 0:1]).then_inc(S["prep_a"], 1)

            act.preload_act_table_set(LOGS)

            def first(f, i, k, j):
                if i is not None:
                    act.wait_ge(A["b_ps"], i + 1)
                    act.activation(ebq, bank[1][0:QK, :], ACT.Exp, scale=1.0 / GATE_NORM)
                    act.activation(ebk, bank[1][0:QK, :], ACT.Exp, scale=-1.0 / GATE_NORM).then_inc(A["eb_ok"], 1)
                    act.wait_ge(A["qe_ok"], i + 1)
                    for h in range(GH):
                        n = act.activation(qbd[:, h, :], qe, ACT.Copy, scale=head_mask[:, h:h + 1])
                    n.then_inc(A["qbd_ok"], 1)
                    act.wait_ge(A["keT_ps"], i + 1)
                    act.activation(keT, bank[2][:, 0:TPI * QK].rearrange("p (t k) -> p t k", t=TPI), ACT.Copy).then_inc(A["keT_ok"], 1)
                if k is not None:
                    act.wait_ge(A["x2_ok"].sem, A["x2_ok"].at(k))
                    for t in range(TPI):
                        n = act.activation(nn[:, t, :], x2[:, t, :], ACT.Square, accum_out=ss[:, t:t + 1])
                    n.then_inc(A["ss_ok"].sem, 1)
                    inverse_root(ve2, rr2, k, "ve2_ok", "r2l", "r2a")
                if f is not None:
                    inverse_root(ve, rr, f, "ve_ok", "rl", "ra")
                if j is not None:
                    gate_tanh(j, 0)
                    gate_tanh(j, 1)
                if i is not None:
                    act.wait_ge(A["g_ps"], i + 1)
                    act.activation(sg, bank[0][:, :], ACT.Tanh, scale=0.5).then_inc(A["eg_ok"], 1)
                if j is not None:
                    gate_tanh(j, 2)
                if k is not None:
                    act.wait_ge(A["nT_ps"], k + 1)
                    if j is not None:
                        act.wait_ge(A["up_ps"], j * MT + MT)
                    act.activation(nT, bank[5][:, :], ACT.Copy).then_inc(A["nT_ok"], 1)
                if f is not None:
                    act.wait_ge(A["hT_ps"], f + 1)
                    act.activation(hT, bank[5][:, :], ACT.Copy).then_inc(A["hT_ok"], 1)
                act.preload_act_table_set(LOGS)
                if f is not None:
                    act.wait_ge(A["za_ok"].sem, A["za_ok"].at(f))
                    act.activation(za, za, ACT.Exp).then_inc(A["e_ok"].sem, 1)
                    act.wait_ge(A["e_ok"].sem, A["e_ok"].at(f))
                    act.activation(za, za, ACT.Ln, bias=1.0).then_inc(A["l_ok"].sem, 1)
                if i is not None:
                    act.wait_ge(A["o_ps"].sem, A["o_ps"].at(i))
                    act.activation(osb, bank[0][:, :], ACT.Copy).then_inc(A["o_ok"].sem, 1)
                    act.wait_ge(A["o_ok"].sem, A["o_ok"].at(i))
                    act.activation(sq, osb, ACT.Square).then_inc(A["sq_ok"].sem, 1)
                if j is not None:
                    inverse_root(ve3, rr3, j, "ve3_ok", "r3l", "r3a")
                if i is not None:
                    act.wait_ge(S["eps_ok"], 1)
                    act.wait_ge(A["ms_ps"].sem, A["ms_ps"].at(i))
                    act.activation(sq, bank[5][:, :], ACT.Ln, bias=eps_col[:, 0:1]).then_inc(A["msl_ok"].sem, 1)
                    act.wait_ge(A["msl_ok"].sem, A["msl_ok"].at(i))
                    act.activation(sq, sq, ACT.Exp, scale=-0.5).then_inc(A["rstd_ok"].sem, 1)
                if f is not None:
                    act.wait_ge(A["v_ps"], f + 1)
                    act.activation(vsb, quads(4), ACT.Copy).then_inc(A["v_ok"], 1)
                if j is not None:
                    act.wait_ge(A["xT_ps"], j + 1)
                    act.activation(xT[:, ds(j * TOK, TOK)], bank[7][:, :], ACT.Copy).then_inc(A["xT_ok"], 1)

            def inverse_root(v, r, n, ready, log, done, sems=A):
                act.wait_ge(sems[ready].sem, sems[ready].at(n))
                act.activation(r, v, ACT.Ln).then_inc(sems[log].sem, 1)
                act.wait_ge(sems[log].sem, sems[log].at(n))
                act.activation(r, r, ACT.Exp, scale=-0.5).then_inc(sems[done].sem, 1)

            def gate_tanh(j, m):
                act.wait_ge(A["gate_ps"], j * MT + m + 1)
                if m == 2:
                    act.wait_ge(A["hid_ok"], j * MT + m - 1)
                act.activation(eg[0:MROWS[m], m % 2, :], bank[GATE_BANK[m]][0:MROWS[m], :], ACT.Tanh, scale=0.5).then_inc(A["eg2_ok"], 1)
            slots(act, first)

            act.preload_act_table_set(LOGS)

            def phase(step):
                s, x, d = step(0), step(2), step(3)

                def others(at):
                    if at == AT["a_raw"] and d is not None:
                        act.wait_ge(B["pv_ok"], d.count(2, 2))
                        last = d.back(1)
                        if last is not None:
                            act.wait_ge(B["rawT_ps"].sem, B["rawT_ps"].at(last.number()))
                        act.activation(raw, bank[4 + d.n2][:, :], ACT.Copy).then_inc(B["raw_ok"].sem, 1)
                    if at == AT["a_qk"] and s is not None:
                        act.wait_ge(B["qk_ps"], s.count(1, 1))
                        old = s.back(2)
                        if old is not None:
                            act.wait_ge(B["lo_ok"], old.count(1, 1))
                        act.activation(qk[s.n2][:, 0:T], bank[6][:, 0:T], ACT.Identity, bias=bcol[:, s.c, 1:2])
                        act.activation(qk[s.n2][:, T:2 * T], bank[6][:, T:2 * T], ACT.Identity, bias=bcol[:, s.c, 0:1])\
                            .then_inc(B["qk_ok"], 1)
                    if at == AT["a_v"] and s is not None:
                        act.wait_ge(B["v_ps2"], s.count(1, 1))
                        if isinstance(s.it, int) and s.it == 0 and s.m < LIVE:
                            act.wait_ge(B["vones"], s.b + 1)
                        v = vaug[s.b].rearrange("p k (h w) -> p k h w", w=VW)
                        act.activation(v[:, :, :, 0:DH], bank[6][:, 0:T].rearrange("p (k h d) -> p k h d", k=KT, h=H),
                                       ACT.Copy).then_inc(B["vals_ok"], 1)
                    if at == AT["a_ctxT"] and d is not None:
                        act.wait_ge(B["ctxT_ps"].sem, B["ctxT_ps"].at(d.number()))
                        act.activation(ctxT[d.n2], bank[4 + d.n2][:, 0:T], ACT.Copy).then_inc(B["ctxT_ok"].sem, 1)
                    if at == AT["a_node"] and d is not None and d.c < NODES - 1:
                        act.wait_ge(B["node_ps"].sem, B["node_ps"].at(d.number()))
                        act.activation(node[:, d.b, d.c, :], bank[4 + d.n2][:, T:2 * T], ACT.Identity, bias=bcol[:, d.c, 2:3])\
                            .then_inc(B["node_ok"], 1)
                    if at == AT["a_f"] and d is not None and d.c == NODES - 1:
                        inverse_root(fve, fr, d.it * LIVE + d.b, "fve_ok", "frl", "fra", B)

                for u in range(UNITS):
                    others(3 * u)
                    exps(*ahead(step, u + EXP_LEAD))
                    others(3 * u + 1)
                    if x is not None and u in ACT_UNITS:
                        copy_unit(act, x, u)
                    others(3 * u + 2)

            def exps(s, u):
                if s is None:
                    return
                act.wait_ge(B["max_ok"], s.count(UNITS, u + 1))
                back = s.count(UNITS, u - PROBS + 1)
                if not (isinstance(back, int) and back < 1):
                    act.wait_ge(B["pT_ps"], back)
                for k in range(2):
                    i = act.activation(prob[u % PROBS][:, k, :], score_bank(s, u)[:, k * T:(k + 1) * T], ACT.Exp, bias=mx[s.n2][:, u, k:k + 1])
                i.then_inc(B["exp_ok"], 1)
            node_slots(act, phase)

        @block.vector
        def _(dve):
            def scale_q(c):
                return scal[:, 3 * c:3 * c + 1]

            dve.wait_ge(L["cols_in"], 16 * 6)
            dve.wait_ge(L["wa_in"], 64)
            dve.tensor_scalar(wa[:, 0:QK], wa[:, 0:QK], cols[:, 0:1], float(DK) ** -0.5, ALU.mult, ALU.mult)
            dve.tensor_scalar(wa[:, QK:], wa[:, QK:], cols[:, 0:1], None, ALU.mult)
            dve.wait_ge(L["wo_in"], 16)
            dve.tensor_scalar(wo[:, :], wo[:, :], cols[:, 2:3], 0.5, ALU.mult, ALU.mult)
            dve.wait_ge(L["mlp_in"], 64)
            dve.tensor_scalar(wgu[:, 0, :], wgu[:, 0, :], cols[:, 1:2], None, ALU.mult)
            dve.tensor_scalar(wgu[:, 1, :], wgu[:, 1, :], cols[:, 1:2], 0.5, ALU.mult, ALU.mult)
            dve.wait_ge(S["gk_ps"].sem, S["gk_ps"].at(0))
            dve.tensor_scalar(wz[:, :], bank[6][:, 128:128 + QK], cols[:, 0:1], None, ALU.mult).then_inc(S["wa_ok"], 1)
            dve.wait_ge(L["scal_in"], 32)
            dve.wait_ge(L["nodew_in"], 16 * 6)
            for c in range(NODES):
                dve.tensor_scalar(w_res[:, c, :], we_raw[:, GRAPH[c]["e"][0], :], scale_q(c), None, ALU.mult)
                k = dve.tensor_scalar(w_out[:, c, :], wo_raw[:, c, :], scal[:, 18 + c:19 + c], None, ALU.mult)
            k.then_inc(S["w_out_ok"], 1)
            for c in range(NODES):
                dve.wait_ge(S["fold_ps"], c + 1)
                src = bank[2 + c % 2]
                dve.tensor_scalar(w_fold[:, c, 0, :], src[:, 0:D], scale_q(c), float(DH) ** -0.5, ALU.mult, ALU.mult)
                for j in range(1, 3):
                    k = dve.tensor_scalar(w_fold[:, c, j, :], src[:, j * D:(j + 1) * D], scal[:, 3 * c + j:3 * c + j + 1], None, ALU.mult)
                k.then_inc(S["fold_ok"], 1)
            ew = scal[:, 0:18].rearrange("p (c j) -> p c j", j=3)
            dve.wait_ge(S["bias_ps"].sem, S["bias_ps"].at(0))
            bp = bank[4][:, 0:3 * NODES].rearrange("p (c j) -> p c j", j=3)
            dve.tensor_tensor(bprod[:, :, 0:3], bp, ew, ALU.mult).then_inc(S["bias_c"].sem, 1)
            dve.wait_ge(S["bias_c"].sem, S["bias_c"].at(0))
            dve.tensor_scalar(bcol[:, :, 0:1], bprod[:, :, 0:1], float(DH) ** -0.5, None, ALU.mult)
            dve.tensor_copy(bcol[:, :, 1:2], bprod[:, :, 1:2])
            dve.wait_ge(S["be_c"], 1)
            for c in range(NODES):
                e = GRAPH[c]["e"][0]
                k = dve.tensor_tensor(bprod[:, c, 3:4], beT[:, e:e + 1], scale_q(c), ALU.mult)
            k.then_inc(S["bias_w"], 1)
            dve.wait_ge(S["bo_ps"].sem, S["bo_ps"].at(0))
            dve.tensor_tensor(bcol[:, :, 2:3], bank[5][:, 0:NODES].unsqueeze(2), scal[:, 18:24].unsqueeze(2), ALU.mult)\
                .then_inc(S["bo_ok"].sem, 1)
            dve.wait_ge(S["bo_ok"].sem, S["bo_ok"].at(0))
            dve.wait_ge(S["bias_w"], 1)
            dve.tensor_tensor(bcol[:, :, 2:3], bcol[:, :, 2:3], bprod[:, :, 3:4], ALU.add).then_inc(S["bias_f"].sem, 1)
            dve.wait_ge(S["bias_f"].sem, S["bias_f"].at(0))
            dve.tensor_copy(nb5w, bcol[:, NODES - 1, 2:3].to_broadcast([P, D])).then_inc(S["nb_b"].sem, 1)
            dve.wait_ge(S["nb_ps"].sem, S["nb_ps"].at(0))
            dve.tensor_copy(nb5[:, :], bank[6][:, 256:256 + D]).then_inc(S["prep_d"], 1)
            dve.wait_ge(S["prep_a"], 1)

            def first(f, i, k, j):
                if k is not None:
                    dve.wait_ge(A["rstd_ok"].sem, A["rstd_ok"].at(k))
                    dve.tensor_tensor(sq, osb, sq, ALU.mult).then_inc(A["t1_ok"].sem, 1)
                    dve.wait_ge(A["t1_ok"].sem, A["t1_ok"].at(k))
                    dve.wait_ge(A["sg_ok"], k + 1)
                    dve.tensor_tensor(uu, sq, sg, ALU.mult).then_inc(A["u_ok"].sem, 1)
                if i is not None:
                    dve.wait_ge(A["eb_ok"], i + 1)
                    dve.wait_ge(A["q_ps"], i + 1)
                    dve.tensor_tensor(qe, bank[2][0:QK, :], ebq, ALU.mult).then_inc(A["qe_ok"], 1)
                    dve.wait_ge(A["k_ps"], i + 1)
                    dve.tensor_tensor(ke, bank[3][0:QK, :], ebk, ALU.mult).then_inc(A["ke_ok"], 1)
                if k is not None:
                    dve.wait_ge(A["at_ps"].sem, A["at_ps"].at(k))
                    dve.wait_ge(A["xn_ok"], k + 1)
                    if j is not None:
                        dve.wait_ge(A["res_ok"], j + 1)
                    dve.tensor_tensor(x2, quads(5), xn, ALU.add).then_inc(A["x2_ok"].sem, 1)
                if i is not None:
                    if k is not None:
                        dve.wait_ge(A["x2_ok"].sem, A["x2_ok"].at(k))
                    for t in range(TPI):
                        n = dve.tensor_scalar(xn[:, t, :], xall[:, ds(TPI * i + t, 1), :].squeeze(1), mv[:, 0, t:t + 1], rr[:, 0, t:t + 1],
                                              ALU.subtract, ALU.mult)
                    n.then_inc(A["xn_ok"], 1)
                if f is not None:
                    dve.wait_ge(L["x_in"], 32)
                    for t in range(TPI):
                        n = dve.bn_stats(st[:, t, :], xall[:, ds(TPI * f + t, 1), :])
                    n.then_inc(A["bn1"].sem, 1)
                    if i is not None:
                        dve.wait_ge(A["xn_ok"], i + 1)
                    moments(st, mv, sm, f, "bn1", "sm1", "sd1", "mv1")
                    dve.wait_ge(A["mv1"].sem, A["mv1"].at(f))
                    dve.tensor_scalar(ve[:, 0, :], mv[:, 1, :], LN_EPS, None, ALU.add)
                    dve.tensor_scalar(ve[:, 1, :], mv[:, 1, :], 1.0 + RMS_EPS, RMS_EPS * LN_EPS, ALU.mult, ALU.add).then_inc(A["ve_ok"].sem, 1)
                if k is not None:
                    dve.wait_ge(A["ss_ok"].sem, A["ss_ok"].at(k))
                    dve.tensor_scalar(ve2, ss, 1.0 / D, RMS_EPS, ALU.mult, ALU.add).then_inc(A["ve2_ok"].sem, 1)
                    newton(dve, ve2, rr2, rt2, k, "r2a", "r2b", "r2c", "rstd2_ok")
                    dve.wait_ge(A["rstd2_ok"].sem, A["rstd2_ok"].at(k))
                    for t in range(TPI):
                        n = dve.tensor_scalar(nn[:, t, :], x2[:, t, :], rr2[:, t:t + 1], None, ALU.mult)
                    n.then_inc(A["n_ok"], 1)
                if f is not None:
                    newton(dve, ve, rr, rt, f, "ra", "rb", "rc", "rstd1_ok")
                    dve.wait_ge(A["rstd1_ok"].sem, A["rstd1_ok"].at(f))
                    for t in range(TPI):
                        n = dve.tensor_scalar(hh[:, t, :], xall[:, ds(TPI * f + t, 1), :].squeeze(1), mv[:, 0, t:t + 1], rr[:, 1, t:t + 1],
                                              ALU.subtract, ALU.mult)
                    n.then_inc(A["h_ok"], 1)
                if j is not None:
                    silu_gate(j, 0)
                    silu_gate(j, 1)
                if i is not None:
                    scores(i, 0)
                    scores(i, 1)
                if j is not None:
                    times_up(j, 0)
                    times_up(j, 1)
                if i is not None:
                    dve.wait_ge(A["kv_ps"], 2 * i + 2)
                    for bb in range(BPI):
                        for c in range(3):
                            n = dve.scalar_tensor_tensor(kvs[:, bb, c, :], update(bb, c), ends(bb, c), state_mask, ALU.mult, ALU.mult)
                    n.then_inc(A["kvs_ok"].sem, 1)
                if j is not None:
                    silu_gate(j, 2)
                    times_up(j, 2)
                if i is not None:
                    for c, (got, did) in ((1, ("kvs_ok", "s2_ok")), (2, ("s2_ok", "s3_ok"))):
                        dve.wait_ge(A[got].sem, A[got].at(i))
                        for bb in range(BPI):
                            n = dve.scalar_tensor_tensor(kvs[:, bb, c, :], kvs[:, bb, c - 1, :], ends(bb, c), kvs[:, bb, c, :],
                                                         ALU.mult, ALU.add)
                        n.then_inc(A[did].sem, 1)
                    dve.wait_ge(A["eg_ok"], i + 1)
                    dve.scalar_tensor_tensor(sg, sg, 1.0, bank[0][:, :], ALU.add, ALU.mult).then_inc(A["sg_ok"], 1)
                if i is not None:
                    scores(i, 2)
                    scores(i, 3)
                if j is not None:
                    dve.wait_ge(A["y_ps"], j + 1)
                    dve.wait_ge(A["res_ok"], j + 1)
                    tiles = xall[:, ds(TPI * j, TPI), :]
                    dve.tensor_tensor(tiles, quads(6), tiles, ALU.add).then_inc(A["x1_ok"], 1)
                    dve.wait_ge(L["x_in"], 32)
                    dve.wait_ge(A["x1_ok"], j + 1)
                    for t in range(TPI):
                        n = dve.bn_stats(st2[:, t, :], xall[:, ds(TPI * j + t, 1), :])
                    n.then_inc(A["bn2"].sem, 1)
                if f is not None:
                    dve.wait_ge(A["z_ps"], f + 1)
                    zps = bank[1][:, 0:TPI * QK].rearrange("p (t k) -> p t k", t=TPI)
                    dve.tensor_tensor(zb, zps, bgk[:, :].unsqueeze(1).to_broadcast([P, TPI, QK]), ALU.add).then_inc(A["zb_ok"].sem, 1)
                    dve.wait_ge(A["zb_ok"].sem, A["zb_ok"].at(f))
                    dve.scalar_tensor_tensor(za, zb, -1.0, zb, ALU.mult, ALU.min).then_inc(A["za_ok"].sem, 1)
                if j is not None:
                    moments(st2, mv2, sm2, j, "bn2", "sm2", "sd2", "mv2")
                    dve.wait_ge(A["mv2"].sem, A["mv2"].at(j))
                    dve.tensor_scalar(ve3, mv2[:, 1, :], LN_EPS, None, ALU.add).then_inc(A["ve3_ok"].sem, 1)
                if f is not None:
                    dve.wait_ge(A["l_ok"].sem, A["l_ok"].at(f))
                    dve.scalar_tensor_tensor(gl, zb, 0.0, za, ALU.min, ALU.subtract).then_inc(A["gl_ok"].sem, 1)
                if j is not None:
                    newton(dve, ve3, rr3, rt3, j, "r3a", "r3b", "r3c", "rstd3_ok")
                    dve.wait_ge(A["rstd3_ok"].sem, A["rstd3_ok"].at(j))
                    for t in range(TPI):
                        n = dve.tensor_scalar(x1n[:, t, :], xall[:, ds(TPI * j + t, 1), :].squeeze(1), mv2[:, 0, t:t + 1], rr3[:, t:t + 1],
                                              ALU.subtract, ALU.mult)
                    n.then_inc(A["xn2_ok"], 1)

            def moments(stats, mv, t, n, got, first, second, done, A=A):
                dve.wait_ge(A[got].sem, A[got].at(n))
                dve.tensor_tensor(t[:, 0, :], stats[:, :, 1], stats[:, :, 4], ALU.add)
                dve.tensor_tensor(t[:, 1, :], stats[:, :, 1], stats[:, :, 4], ALU.subtract)
                dve.tensor_tensor(t[:, 2, :], stats[:, :, 2], stats[:, :, 5], ALU.add).then_inc(A[first].sem, 1)
                dve.wait_ge(A[first].sem, A[first].at(n))
                dve.tensor_scalar(mv[:, 0, :], t[:, 0, :], 0.5, None, ALU.mult)
                dve.scalar_tensor_tensor(t[:, 1, :], t[:, 1, :], 0.25, t[:, 1, :], ALU.mult, ALU.mult).then_inc(A[second].sem, 1)
                dve.wait_ge(A[second].sem, A[second].at(n))
                dve.scalar_tensor_tensor(mv[:, 1, :], t[:, 2, :], 1.0 / D, t[:, 1, :], ALU.mult, ALU.add).then_inc(A[done].sem, 1)

            def newton(eng, v, r, t, n, first, second, third, done, A=A):
                eng.wait_ge(A[first].sem, A[first].at(n))
                eng.tensor_tensor(t, r, r, ALU.mult).then_inc(A[second].sem, 1)
                eng.wait_ge(A[second].sem, A[second].at(n))
                eng.scalar_tensor_tensor(t, t, -0.5, v, ALU.mult, ALU.mult).then_inc(A[third].sem, 1)
                eng.wait_ge(A[third].sem, A[third].at(n))
                eng.scalar_tensor_tensor(r, t, 1.5, r, ALU.add, ALU.mult).then_inc(A[done].sem, 1)

            def ends(bb, c):
                at = bb * T + (c + 1) * CHUNK - 1
                return ebq[:, at:at + 1]

            def silu_gate(j, m):
                n = MROWS[m]
                dve.wait_ge(A["eg2_ok"], j * MT + m + 1)
                dve.scalar_tensor_tensor(eg[0:n, m % 2, :], eg[0:n, m % 2, :], 1.0, bank[GATE_BANK[m]][0:n, :], ALU.add, ALU.mult)\
                    .then_inc(A["si_ok"], 1)

            def times_up(j, m):
                n = MROWS[m]
                dve.wait_ge(A["up_ps"], j * MT + m + 1)
                dve.wait_ge(A["si_ok"], j * MT + m + 1)
                dve.tensor_tensor(hid[0:n, m, :], bank[UP_BANK[m]][0:n, :], eg[0:n, m % 2, :], ALU.mult).then_inc(A["hid_ok"], 1)

            def scores(i, t):
                dve.wait_ge(S["am0"], 1)
                dve.wait_ge(a_ps[t], i + 1)
                dve.copy_predicated(am[:, t, :], causal, bank[[4, 2][t % 2]][:, :]).then_inc(A["am_ok"], 1)

            slots(dve, first)

            def phase(step):
                s, x, d = step(0), step(2), step(3)

                def others(at):
                    if at == AT["d_ctx"] and d is not None:
                        dve.wait_ge(B["rawT_ps"].sem, B["rawT_ps"].at(d.number()))
                        t = bank[4 + d.n2][:, :].rearrange("p (a w) -> p a w", w=VW)
                        dve.reciprocal(rec, t[:, :, DH]).then_inc(B["rec_ok"].sem, 1)
                        last = d.back(1)
                        if last is not None:
                            dve.wait_ge(B["ctxT_ps"].sem, B["ctxT_ps"].at(last.number()))
                        dve.wait_ge(B["rec_ok"].sem, B["rec_ok"].at(d.number()))
                        dve.tensor_tensor(ctxc.rearrange("p t (h d) -> p (t h) d", h=H), t[:, :, 0:DH],
                                          rec.unsqueeze(2).to_broadcast([P, KT * H, DH]), ALU.mult).then_inc(B["ctxc_ok"].sem, 1)
                    if d is not None and d.c == NODES - 1:
                        f = d.it * LIVE + d.b
                        if at == AT["f0"]:
                            dve.wait_ge(B["node_ps"].sem, B["node_ps"].at(d.number()))
                            dve.wait_ge(B["fy_free"], f + 1)
                            dve.tensor_tensor(fy, bank[4 + d.n2][:, T:2 * T].rearrange("p (t d) -> p t d", t=KT),
                                              nb5[:, :].unsqueeze(1).to_broadcast([P, KT, D]), ALU.add).then_inc(B["fin_read"].sem, 1)
                            dve.wait_ge(B["fin_read"].sem, B["fin_read"].at(f))
                            for t in range(KT):
                                k = dve.bn_stats(fst[:, t, :], fy[:, t, :])
                            k.then_inc(B["fbn"].sem, 1)
                        if at == AT["f1"]:
                            moments(fst, fmv, fsm, f, "fbn", "fsm", "fsd", "fmv", B)
                            dve.wait_ge(B["fmv"].sem, B["fmv"].at(f))
                            dve.tensor_scalar(fve, fmv[:, 1, :], FFN_LN_EPS, None, ALU.add).then_inc(B["fve_ok"].sem, 1)
                        if at == AT["f2"]:
                            newton(dve, fve, fr, frt, f, "fra", "frb", "frc", "fr_ok", B)
                            dve.wait_ge(B["fr_ok"].sem, B["fr_ok"].at(f))
                            for t in range(KT):
                                k = dve.tensor_scalar(fy[:, t, :], fy[:, t, :], fmv[:, 0, t:t + 1], fr[:, t:t + 1], ALU.subtract, ALU.mult)
                            k.then_inc(B["fyn_ok"].sem, 1)

                for u in range(UNITS):
                    others(3 * u)
                    maxes(*ahead(step, u + MAX_LEAD))
                    others(3 * u + 1)
                    if x is not None and u not in ACT_UNITS:
                        copy_unit(dve, x, u)
                    others(3 * u + 2)

            def maxes(s, u):
                if s is None:
                    return
                dve.wait_ge(B["s_ps"], s.count(UNITS, u + 1))
                dve.tensor_reduce(mx[s.n2][:, u, :], score_bank(s, u)[:, :].rearrange("p (h k) -> p h k", h=2), AX_X, ALU.max,
                                  negate=True).then_inc(B["max_ok"], 1)
            node_slots(dve, phase)

        @block.tensor
        def _(pe):
            def mm(o, w, x, start=True, stop=True, skip=False):
                return pe.matmul(o, w, x, start=start, stop=stop, skip_group_check=skip)

            pe.wait_ge(L["const_in"], 16)
            pe.wait_ge(L["gk_in"], 48)
            pe.transpose(bank[6][0:RANK, 0:P], wgk1, ident).then_inc(S["gk1_t"].sem, 1)
            pe.wait_ge(S["gk1_c"].sem, S["gk1_c"].at(0))
            mm(bank[6][:, 128:128 + QK], wgk1T, wgk2).then_inc(S["gk_ps"].sem, 1)
            pe.wait_ge(L["nodew_in"], 16 * 6)
            pe.transpose(bank[7][:, 0:EDGES], be_rows, ident[0:EDGES, 0:EDGES]).then_inc(S["be_t"], 1)
            w3 = wqkv_raw.rearrange("p j (c n) -> p j c n", c=NODES)
            for c in range(NODES + 1):
                if c < NODES:
                    if c >= 2:
                        pe.wait_ge(S["we_c"], c - 1)
                    for j in range(3):
                        k = pe.transpose(bank[c % 2][:, j * D:(j + 1) * D], we_raw[:, GRAPH[c]["e"][j], :], ident)
                    k.then_inc(S["we_t"], 1)
                if c >= 1:
                    b = c - 1
                    pe.wait_ge(S["we_c"], b + 1)
                    if b >= 2:
                        pe.wait_ge(S["fold_ok"], b - 1)
                    for j in range(3):
                        k = mm(bank[2 + b % 2][:, j * D:(j + 1) * D], weT[:, b % 2, j * D:(j + 1) * D], w3[:, j, b, :])
                    k.then_inc(S["fold_ps"], 1)
            pe.wait_ge(S["be_c"], 1)
            for c in range(NODES):
                for j in range(3):
                    e = GRAPH[c]["e"][j]
                    k = mm(bank[4][:, 3 * c + j:3 * c + j + 1], w3[:, j, c, :], beT[:, e:e + 1])
            k.then_inc(S["bias_ps"].sem, 1)
            pe.wait_ge(S["bias_c"].sem, S["bias_c"].at(0))
            for c in range(NODES):
                k = mm(bank[5][:, c:c + 1], wo_raw[:, c, :], bprod[:, c, 2:3])
            k.then_inc(S["bo_ps"].sem, 1)
            pe.wait_ge(S["nb_b"].sem, S["nb_b"].at(0))
            pe.wait_ge(S["wa_ok"], 1)
            mm(bank[6][:, 256:256 + D], nb5w, ident).then_inc(S["nb_ps"].sem, 1)
            pe.wait_ge(S["prep_d"], 1)

            def first(f, i, k, j):
                if j is not None:
                    pe.wait_ge(A["nT_ok"], j + 1)
                    gate(j, 0)
                if k is not None:
                    pe.wait_ge(A["u_ok"].sem, A["u_ok"].at(k))
                    for t in range(TPI):
                        n = mm(bank[5][:, t * P:(t + 1) * P], uu[:, t * P:(t + 1) * P], wo[:, :])
                    n.then_inc(A["at_ps"].sem, 1)
                if i is not None:
                    pe.wait_ge(A["ke_ok"], i + 1)
                    mm(bank[0][:, :], wa[:, 2 * QK + D:], hT).then_inc(A["g_ps"], 1)
                    for t in range(TPI):
                        n = pe.transpose(bank[2][:, t * QK:(t + 1) * QK], ke[:, t * P:(t + 1) * P], ident[0:QK, 0:QK])
                    n.then_inc(A["keT_ps"], 1)
                if j is not None:
                    if not (isinstance(j, int) and j == 0):
                        pe.wait_ge(A["xT_ok"], j)
                    gate(j, 1)
                if i is not None:
                    pe.wait_ge(L["const_in"], 16)
                    pe.wait_ge(A["keT_ok"], i + 1)
                    pe.wait_ge(A["v_ok"], i + 1)
                    for odd in range(2):
                        r = CHUNK * odd
                        for bb in range(BPI):
                            for c in range(odd, 3, 2):
                                t = bb * KT + c // 2
                                n = mm(update(bb, c), keT[r:r + CHUNK, t, :], vsb[r:r + CHUNK, t, :])
                        n.then_inc(A["kv_ps"], 1)
                    pe.wait_ge(A["qbd_ok"], i + 1)
                    for t in range(2):
                        heads_scores(i, t)
                if k is not None:
                    pe.wait_ge(A["n_ok"], k + 1)
                    for t in range(TPI):
                        n = pe.transpose(bank[5][:, t * P:(t + 1) * P], nn[:, t, :], ident)
                    n.then_inc(A["nT_ps"], 1)
                if j is not None:
                    for m in range(2):
                        pe.wait_ge(A["si_ok"], j * MT + m + 1)
                        up(j, m)
                    pe.wait_ge(A["hid_ok"], j * MT + 1)
                    gate(j, 2)
                    pe.wait_ge(A["hid_ok"], j * MT + 2)
                    up(j, 2)
                if i is not None:
                    for t in range(2, TPI):
                        pe.wait_ge(A["am_ok"], TPI * i + t - 1)
                        heads_scores(i, t)
                if f is not None:
                    pe.wait_ge(A["h_ok"], f + 1)
                    if k is not None:
                        pe.wait_ge(A["nT_ok"], k + 1)
                    for t in range(TPI):
                        n = pe.transpose(bank[5][:, t * P:(t + 1) * P], hh[:, t, :], ident)
                    n.then_inc(A["hT_ps"], 1)
                if j is not None:
                    pe.wait_ge(A["si_ok"], j * MT + MT)
                    for m in range(MT):
                        if m == MT - 1:
                            pe.wait_ge(A["hid_ok"], j * MT + MT)
                        for t in range(TPI):
                            n = mm(bank[6][:, t * P:(t + 1) * P], hid[0:MROWS[m], m, t * P:(t + 1) * P], wd[0:MROWS[m], m, :],
                                   start=(m == 0 and t == 0), stop=(m == MT - 1), skip=True)
                    n.then_inc(A["y_ps"], 1)
                if f is not None:
                    pe.wait_ge(A["hT_ok"], f + 1)
                    if i is not None:
                        pe.wait_ge(A["kvs_ok"].sem, A["kvs_ok"].at(i))
                    for t in range(TPI):
                        n = mm(bank[1][:, t * QK:(t + 1) * QK], hT[:, t * P:(t + 1) * P], wz[:, :])
                    n.then_inc(A["z_ps"], 1)
                if i is not None:
                    pe.wait_ge(A["sg_ok"], i + 1)
                    pe.wait_ge(A["s3_ok"].sem, A["s3_ok"].at(i))
                    for t in range(TPI):
                        pe.wait_ge(A["am_ok"], TPI * i + t + 1)
                        for h in range(GH):
                            mm(bank[0][DV * h:DV * h + DV, t * P:(t + 1) * P], vsb[:, t, DV * h:DV * h + DV],
                               am[:, t, h * P:(h + 1) * P], stop=False, skip=True)
                        for cc in range(2):
                            c = 2 * (t % KT) + cc
                            if c > 0:
                                at = t * P + cc * CHUNK
                                n = mm(bank[0][:, at:at + CHUNK], kvs[:, t // KT, c - 1, :], qe[:, at:at + CHUNK],
                                       start=False, skip=True)
                    n.then_inc(A["o_ps"].sem, 1)
                if f is not None:
                    mm(bank[2][0:QK, :], wa[:, 0:QK], hT).then_inc(A["q_ps"], 1)
                    mm(bank[3][0:QK, :], wa[:, QK:2 * QK], hT).then_inc(A["k_ps"], 1)
                if i is not None:
                    pe.wait_ge(A["sq_ok"].sem, A["sq_ok"].at(i))
                    mm(bank[5][:, :], mean_dv, sq).then_inc(A["ms_ps"].sem, 1)
                if f is not None:
                    pe.wait_ge(A["gl_ok"].sem, A["gl_ok"].at(f))
                    for t in range(TPI):
                        n = mm(bank[1][0:QK, t * P:(t + 1) * P], gl[:, t, :], cum)
                    n.then_inc(A["b_ps"], 1)
                    for t in range(TPI):
                        n = mm(bank[4][:, t * P:(t + 1) * P], hT[:, t * P:(t + 1) * P], wa[:, 2 * QK:2 * QK + D])
                    n.then_inc(A["v_ps"], 1)
                if j is not None:
                    pe.wait_ge(A["xn2_ok"], j + 1)
                    for t in range(TPI):
                        n = pe.transpose(bank[7][:, t * P:(t + 1) * P], x1n[:, t, :], ident)
                    n.then_inc(A["xT_ps"], 1)

            def heads_scores(i, t):
                mm(bank[[4, 2][t % 2]][:, :].rearrange("p (h c) -> p h c", h=GH), ke[:, t * P:(t + 1) * P],
                   qbd[:, :, t * P:(t + 1) * P]).then_inc(a_ps[t], 1)

            def gate(j, m):
                mm(bank[GATE_BANK[m]][0:MROWS[m], :], wgu[:, 0, m * P:m * P + MROWS[m]], nT).then_inc(A["gate_ps"], 1)

            def up(j, m):
                mm(bank[UP_BANK[m]][0:MROWS[m], :], wgu[:, 1, m * P:m * P + MROWS[m]], nT).then_inc(A["up_ps"], 1)
            slots(pe, first)

            pe.wait_ge(A["xT_ok"], ITERS)

            def source(s, n):
                return x0T[:, s.b, :] if n < 0 else node[:, s.b, n, :]

            def pv(s, g):
                upto = UNITS // 2 * (g + 1)
                pe.wait_ge(B["pT_dve"], copies(s, upto, "dve"))
                pe.wait_ge(B["pT_act"], copies(s, upto, "act"))
                if g == 0:
                    pe.wait_ge(B["vals_ok"], s.count(1, 1))
                    old = s.back(2)
                    if old is not None:
                        if old.c < NODES - 1:
                            pe.wait_ge(B["node_ok"], old.nodes())
                        else:
                            pe.wait_ge(B["fin_read"].sem, B["fin_read"].at(old.finals() - 1))
                for kt in range(KT):
                    for j in range(GCOL):
                        h = g * GCOL + j
                        k = mm(bank[4 + s.n2][32 * j:32 * j + 32, g * T:(g + 1) * T], vaug[s.b][:, kt, VW * h:VW * h + VW],
                               probT[:, h, kt * T:(kt + 1) * T], start=(kt == 0), stop=(kt == KT - 1), skip=True)
                k.then_inc(B["pv_ok"], 1)

            def phase(step):
                s, x, d = step(0), step(2), step(3)

                def others(at):
                    if at == AT["pv1"] and d is not None:
                        pv(d, 1)
                    if at == AT["qk"] and s is not None:
                        g = GRAPH[s.c]["src"]
                        pe.wait_ge(x0_in[s.b], 16 * s.it + 16)
                        if s.c > 0:
                            pe.wait_ge(B["node_ok"], s.back(LIVE).nodes())
                        last = s.back(1)
                        if last is not None:
                            pe.wait_ge(B["vals_ok"], last.count(1, 1))
                        mm(bank[6][:, 0:T], w_fold[:, s.c, 1, :], source(s, g[1]))
                        mm(bank[6][:, T:2 * T], w_fold[:, s.c, 0, :], source(s, g[0])).then_inc(B["qk_ps"], 1)
                    if at == AT["rawT"] and d is not None:
                        pe.wait_ge(B["raw_ok"].sem, B["raw_ok"].at(d.number()))
                        for qt in range(KT):
                            for g in range(2):
                                a = (qt * 2 + g) * P
                                k = pe.transpose(bank[4 + d.n2][:, a:a + P], raw[:, g * T + qt * P:g * T + (qt + 1) * P], ident)
                        k.then_inc(B["rawT_ps"].sem, 1)
                    if at == AT["v"] and s is not None:
                        pe.wait_ge(B["qk_ok"], s.count(1, 1))
                        for kt in range(KT):
                            k = mm(bank[6][:, kt * P:(kt + 1) * P], source(s, GRAPH[s.c]["src"][2])[:, kt * P:(kt + 1) * P], w_fold[:, s.c, 2, :])
                        k.then_inc(B["v_ps2"], 1)
                    if at == AT["ctxT"] and d is not None:
                        pe.wait_ge(B["ctxc_ok"].sem, B["ctxc_ok"].at(d.number()))
                        for qt in range(KT):
                            k = pe.transpose(bank[4 + d.n2][:, qt * P:(qt + 1) * P], ctxc[:, qt, :], ident)
                        k.then_inc(B["ctxT_ps"].sem, 1)
                    if at == AT["proj"] and d is not None:
                        project(d)
                    if at == AT["pv0"] and x is not None:
                        pv(x, 0)

                for u in range(UNITS):
                    others(3 * u)
                    if PE_SWAP:
                        scores(*ahead(step, u + S_LEAD))
                    else:
                        transposes(x, u)
                    others(3 * u + 1)
                    if PE_SWAP:
                        transposes(x, u)
                    else:
                        scores(*ahead(step, u + S_LEAD))
                    others(3 * u + 2)

            def transposes(x, u):
                if x is None:
                    return
                pe.wait_ge(B["exp_ok"], x.count(UNITS, u + 1))
                if u >= 2 or x.back(1) is not None:
                    w, v = (x, u - 2) if u >= 2 else (x.back(1), u + UNITS - 2)
                    e = "act" if v in ACT_UNITS else "dve"
                    pe.wait_ge(B["pT_" + e], copies(w, v + 1, e))
                for k in range(2):
                    for kt in range(KT):
                        o = (k * KT + kt) * P
                        i = pe.transpose(bank[2 + u % 2][:, o:o + P], prob[u % PROBS][:, k, kt * P:(kt + 1) * P], ident)
                i.then_inc(B["pT_ps"], 1)

            def scores(s, u):
                if s is None:
                    return
                pr, qt = u // KT, u % KT
                if u == 0:
                    pe.wait_ge(stacked[s.b], s.stacks())
                back = s.count(UNITS, u - len(SBANK) + 1)
                if not (isinstance(back, int) and back < 1):
                    pe.wait_ge(B["exp_ok"], back)
                mm(score_bank(s, u)[:, :].rearrange("p (h k) -> p h k", h=2), qs[s.b][:, pr, qt * P:(qt + 1) * P],
                   kz[s.b][:, 2 * pr:2 * pr + 2, :]).then_inc(B["s_ps"], 1)

            def project(d):
                to, prev, ctx_n = bank[4 + d.n2], source(d, GRAPH[d.c]["src"][0]), ctxT[d.n2]
                pe.wait_ge(B["ctxT_ok"].sem, B["ctxT_ok"].at(d.number()))
                if d.c < NODES - 1:
                    mm(to[:, T:2 * T], w_res[:, d.c, :], prev, stop=False)
                    mm(to[:, T:2 * T], w_out[:, d.c, :], ctx_n, start=False).then_inc(B["node_ps"].sem, 1)
                else:
                    for t in range(KT):
                        r, o = slice(t * P, (t + 1) * P), slice(T + t * P, T + (t + 1) * P)
                        mm(to[:, o], prev[:, r], w_res[:, d.c, :], stop=False)
                        k = mm(to[:, o], ctx_n[:, r], w_out[:, d.c, :], start=False)
                    k.then_inc(B["node_ps"].sem, 1)
            node_slots(pe, phase)


_INS = ['L0_attn_hidden_states', 'L0_attn_attn_norm_w', 'L0_attn_Wq', 'L0_attn_Wk', 'L0_attn_Wv', 'L0_attn_Wg', 'L0_attn_Wgk1',
        'L0_attn_Wgk2', 'L0_attn_bgk2', 'L0_attn_gnorm_w', 'L0_attn_Wo', 'L0_attn_mlp_norm_w', 'L0_attn_W_gate', 'L0_attn_W_up',
        'L0_attn_W_down', 'L0_ffn_ew', 'L0_ffn_act_w', 'L0_ffn_We', 'L0_ffn_be', 'L0_ffn_Wq', 'L0_ffn_Wk', 'L0_ffn_Wv',
        'L0_ffn_Wo', 'L0_ffn_ln_g', 'L0_ffn_ln_b']


def kernel(**inputs):
    import concourse.bacc as _bacc
    from concourse.bass_utils import run_bass_kernel_spmd as _run

    nc = _bacc.Bacc("TRN2", target_bir_lowering=False, num_devices=1)
    arrays, aps = {}, {}
    for name in _INS:
        v = np.ascontiguousarray(inputs[name])
        arrays[f"in_{name}"] = v
        aps[name] = nc.dram_tensor(f"in_{name}", v.shape, mybir.dt.from_np(v.dtype), kind="ExternalInput").ap()
    arrays["in_constants"] = constants()
    consts = nc.dram_tensor("in_constants", (P, C_END), F32, kind="ExternalInput").ap()
    out = nc.dram_tensor("out_0", (BATCH, T, D), F32, kind="ExternalOutput").ap()
    build(nc, aps, consts, out)
    r = _run(nc, [arrays], core_ids=[0])
    return r.results[0]["out_0"]
```

```python
from contextlib import ExitStack

import numpy as np

import concourse.bass as bass
from concourse import mybir

ALU = mybir.AluOpType
ACT = mybir.ActivationFunctionType
AX_X = mybir.AxisListType.X
F32 = mybir.dt.float32
F32R = mybir.dt.float32r
U32 = mybir.dt.uint32

P = 128
D = 128
BATCH, T = 16, 256
TILES = BATCH * T // P
LN_EPS, RMS_EPS, FFN_LN_EPS = 1e-5, 1e-6, 1e-6

GH, DK, DV, CHUNK = 4, 16, 32, 64
QK = GH * DK
GATE_NORM = 16.0
RANK = 16
MLP = 352
MT = 3
MROWS = [128, 128, MLP - 256]
TPI = 4
TOK = TPI * P
ITERS = TILES // TPI
BPI = TOK // T

NODES, MAX_PREV, EDGES = 6, 5, 20
H, DH = 8, 16
PAIRS = H // 2
KT = T // P
LIVE = 4
STEPS = NODES * LIVE
GROUPS = BATCH // LIVE
GCOL = 4
VW = 32
PARTS = 3
ROWS = PARTS * 32
UNITS = PAIRS * KT
AT = dict(pv1=3, qk=5, rawT=9, v=12, ctxT=15, proj=17, pv0=20, a_raw=6, a_qk=9, a_v=20,
          a_ctxT=15, a_node=20, d_ctx=12, f0=22, a_f=5)
MLP_AT = dict(g01=2, t01=3, s01=4, u01=5, h01=8, g2=14, t2=15, s2=16, y=19, x1=20, mom=28, inv=28, x1n=35, xT=40, c=40)
S_LEAD, MAX_LEAD, EXP_LEAD = 3, 2, 1
LEADING = 2
EARLY = 2
CLOSING = 1
PROBS = 2
SBANK = (0, 1, 7)
ACT_UNITS = (3, 7)
STACK_DMAS = PARTS * 3


def graph():
    out, at = [], 0
    for c in range(NODES):
        n = min(c + 1, MAX_PREV)
        s = c - n
        out.append(dict(e=(at + n - 1, at, at + n // 2), src=(c - 1, s, s + n // 2)))
        at += n
    return out


GRAPH = graph()
LOGS = "natural_log_exp_and_others"


def mlp_bank(j, m):
    last = isinstance(j, int) and (j == ITERS - 1 or j == ITERS - 2 and m == 7)
    return (4 if last else 6) + (0, 1, 0, 0, 1, 1, 0, 1)[m]


class Event:

    def __init__(self, sem, place, events):
        self.sem, self.place, self.events = sem, place, events

    def at(self, n):
        return n * self.events + self.place


C_ID, C_CUM, C_MASK, C_MEAN, C_HEAD, C_STATE, C_SIGN, C_END = 0, 128, 256, 768, 896, 900, 1028, 1029


def constants():
    c = np.zeros((P, C_END), np.float32)
    i = np.arange(P)
    c[:, C_ID:C_ID + P] = np.eye(P)
    causal = (i[:, None] <= i[None, :]) & (i[:, None] // CHUNK == i[None, :] // CHUNK)
    c[:, C_CUM:C_CUM + P] = causal
    c[:, C_MASK:C_MASK + GH * P] = np.tile(causal, (1, GH))
    c[:, C_MEAN:C_MEAN + P] = (i[:, None] // DV == i[None, :] // DV) / DV
    r = np.arange(QK)
    c[:QK, C_HEAD:C_HEAD + GH] = r[:, None] // DK == np.arange(GH)[None, :]
    c[:QK, C_STATE:C_STATE + P] = r[:, None] // DK == i[None, :] // DV
    c[:, C_SIGN] = np.where(i < QK, 1.0, -1.0) / GATE_NORM
    return c


def build(nc, a, consts, out):
    ds = bass.ds
    with ExitStack() as ctx:
        def sb(name, shape, dt=F32):
            return ctx.enter_context(nc.sbuf_tensor(name, shape, dt))

        def sem(name):
            return ctx.enter_context(nc.semaphore(name))

        bank = [ctx.enter_context(nc.psum_tensor(f"bank{n}", [P, 512], F32)) for n in range(8)]

        def quads(n):
            return bank[n][:, :].rearrange("p (t d) -> p t d", t=4)

        cst = sb("cst", [P, C_END])
        ident = cst[:, C_ID:C_ID + P]
        cum = cst[:, C_CUM:C_CUM + P]
        causal = cst[:, C_MASK:C_MASK + GH * P].bitcast(U32)
        mean_dv = cst[:, C_MEAN:C_MEAN + P]
        head_mask = cst[0:QK, C_HEAD:C_HEAD + GH]
        sign_col = cst[:, C_SIGN:C_SIGN + 1]
        state_mask = cst[0:QK, C_STATE:C_STATE + P]
        xall = sb("xall", [P, TILES, D])
        xT = sb("xT", [P, TILES * P])
        wa = sb("wa", [P, 2 * QK + 2 * D])
        wz = sb("wz", [P, QK])
        wo = sb("wo", [P, D])
        wgu = sb("wgu", [P, 2, MLP])
        wd = sb("wd", [P, MT, D])
        bgk = sb("bgk", [P, QK])
        eps_col = sb("eps_col", [P, 1])
        one_col = sb("one_col", [P, 1])
        cols = sb("cols", [P, 3])
        w_res = sb("w_res", [P, NODES, D])
        w_fold = sb("w_fold", [P, NODES, 3, D])
        w_out = sb("w_out", [P, NODES, D])
        bcol = sb("bcol", [P, NODES, 3])
        nb5 = sb("nb5", [P, D])
        lng = sb("lng", [P, 2, D])
        scal = sb("scal", [P, NODES * 4])
        beT = sb("beT", [P, EDGES])[:, :]
        bprod = sb("bprod", [P, NODES, 4])[:, :, :]
        nb5w = sb("nb5w", [P, D])[:, :]
        kz = [sb(f"kz{b}", [ROWS, H, T], F32R) for b in range(LIVE)]
        qs = [sb(f"qs{b}", [ROWS, PAIRS, T], F32R) for b in range(LIVE)]
        hl = [sb(f"hl{n}", [P, 2, 2 * T], F32R) for n in range(2)]
        x0T = sb("x0T", [P, LIVE, T])
        qk = [sb(f"qk{n}", [P, 2 * T])[:, :] for n in range(2)]
        parts = nc.dram_tensor("parts", (LIVE, P, 2, 2 * T), F32, kind="Internal").ap()

        UW = 17000
        region = sb("region", [P, UW])

        def carver():
            at = [0]

            def carve(*dims, rows=P):
                n = int(np.prod(dims))
                v = region[0:rows, at[0]:at[0] + n]
                at[0] += n
                assert at[0] <= UW, at[0]
                if len(dims) == 2:
                    v = v.rearrange("p (a b) -> p a b", a=dims[0])
                elif len(dims) == 3:
                    v = v.rearrange("p (a b c) -> p a b c", a=dims[0], b=dims[1])
                return v
            return carve, at

        carve, used = carver()
        xn = carve(TPI, D)
        xs = carve(TPI)
        hh = carve(TPI, D)
        hT = carve(TOK)
        zb = carve(TPI, QK)
        za = carve(TPI, QK)
        gl = carve(TPI, 2 * QK)
        eb = carve(TOK)
        qke = carve(TOK)
        qe, ke = qke[0:QK, :], qke[QK:2 * QK, :]
        qbd = carve(GH, TOK)[QK:2 * QK]
        vsb = carve(TPI, D)
        sg = carve(TOK)
        keT = carve(TPI, QK)
        am = carve(TPI, GH * P)
        kvs = carve(BPI, 3, D, rows=QK)
        osb = carve(TOK)
        sq = carve(TOK)
        later = used[0]
        uu = carve(TOK)
        x2 = carve(TPI, D)
        nn = carve(TPI, D)
        x1n = carve(TPI, D)
        nT = carve(TOK)
        eg = carve(2, TOK)
        hid = carve(MT, TOK)
        until = used[0]
        st = carve(TPI, 6)
        mv = carve(2, TPI)
        sm = carve(3, TPI)
        ve = carve(2, TPI)
        rr = carve(2, TPI)
        rt = carve(2, TPI)
        st2 = carve(TPI, 6)
        mv2 = carve(2, TPI)
        sm2 = carve(3, TPI)
        ss = carve(TPI)
        ve2 = carve(TPI)
        rr2 = carve(TPI)
        rt2 = carve(TPI)
        ve3 = carve(TPI)
        rr3 = carve(TPI)
        rt3 = carve(TPI)
        carve, used = carver()
        used[0] = later
        we_raw = carve(EDGES, D)
        wgk1 = carve(RANK)
        wgk1T = carve(P, rows=RANK)
        wgk2 = carve(QK, rows=RANK)
        assert used[0] <= until
        wqkv_raw = xT[:, 0:3 * NODES * D].rearrange("p (j n) -> p j n", j=3)
        wo_raw = xT[:, 18 * D:24 * D].rearrange("p (c n) -> p c n", c=NODES)
        weT = xT[:, 24 * D:30 * D].rearrange("p (b n) -> p b n", b=2)
        be_rows = xT[0:EDGES, 30 * D:31 * D]
        carve, used = carver()
        vaug = [carve(KT, H * VW) for _ in range(LIVE)]
        prob = [carve(2, T) for _ in range(PROBS)]
        probT = carve(H, KT * T)
        raw = carve(2 * T)
        rec = carve(KT * H)
        ctxc = carve(KT, D)
        ctxT = [carve(T) for _ in range(2)]
        mx = [carve(UNITS, 2) for _ in range(2)]
        fy = carve(KT, D)
        fst = carve(KT, 6)
        fmv = carve(KT)
        fsm = carve(3, KT)
        fve = carve(KT)
        fr = carve(KT)
        frt = carve(3, KT)
        assert used[0] <= later
        node = carve(LIVE, NODES - 1, T)

        def names(text):
            return {n: sem(n) for n in text.split()}

        def chain(name, events):
            one, events = sem(name), events.split()
            return {e: Event(one, k + 1, len(events)) for k, e in enumerate(events)}

        L = names("x_first x_half x_in const_in wa_in gk_in wo_in mlp_in cols_in nodew_in scal_in ln_in")
        S = names("wa_ok we_t we_c fold_ps fold_ok be_t be_c "
                  "bias_w am0 eps_ok one_ok zero_ok prep_d")
        A = names("xn_ok h_ok hT_ps hT_ok z_ps b_ps eb_ok qkp_ps qke_ok qbd_ok "
                  "v_ps v_ok g_ps eg_ok sg_ok keT_ps keT_ok kv_ps am_ok "
                  "n_ok nT_ps nT_ok gate_ps up_ps eg2_ok si_ok hid_ok y_ps res_ok x1_ok xn2_ok "
                  "xT_ps xT_ok t1_ok xa_ok")
        B = names("qk_ps v_ps2 qk_ok hi_ok lo_ok vals_ok s_ps max_ok exp_ok pT_ps pT_act pT_dve pv_ok "
                  "node_ok vones fy_free out_stored last_stored")
        A.update(chain("ln1", "bn1 sm1 sd1 mv1 ve_ok rl ra rb rc rstd1_ok"))
        A.update(chain("rms2", "ve2_ok r2l r2a r2b r2c rstd2_ok"))
        A.update(chain("ln2", "bn2 sm2 sd2 mv2 ve3_ok r3l r3a r3b r3c rstd3_ok"))
        B.update(chain("fin", "fin_read fbn fsm fsd fve_ok frl fra frb frc frd fr_ok fc_ok fyn_ok fg_ok fb_ok"))
        A.update(chain("logsig", "zb_ok za_ok e_ok l_ok gl_ok"))
        A.update(chain("state", "kvs_ok s2_ok s3_ok"))
        A.update(chain("outs", "o_ps o_ok"))
        A.update(chain("heads", "sq_ok ms_ps msl_ok rstd_ok u_ok at_ps x2_ok ss_ok"))
        S.update(chain("gk", "gk1_t gk1_c gk_ps"))
        S.update(chain("bias", "bias_ps bias_c bo_ps bo_ok bias_f nb_b nb_ps"))
        B.update(chain("ctx", "raw_ok rawT_ps rec_ok ctxc_ok ctxT_ps ctxT_ok node_ps"))
        a_ps = [sem(f"a_ps{t}") for t in range(TPI)]
        stored = [sem(f"stored{n}") for n in range(2)]
        stacked = [sem(f"stacked{b}") for b in range(LIVE)]
        x0_in = [sem(f"x0_in{b}") for b in range(LIVE)]

        x_d = a["L0_attn_hidden_states"].rearrange("b t d -> (b t) d").rearrange("(n p) d -> p n d", p=P)
        out_d = out.rearrange("b t d -> (b t) d").rearrange("(n t p) d -> n p t d", t=KT, p=P)

        def col(v):
            return v.rearrange("(d a) -> d a", a=1)


        def slots(eng, body, prepare={}):
            for n in range(-1, 3):
                body(*(m if m >= 0 else None for m in (n + 1, n, n - 1, n - 2)))
                if n in prepare:
                    prepare[n]()
            with eng.Fori(3, ITERS - 1) as n:
                body(n + 1, n, n - 1, n - 2)
            for n in range(ITERS - 1, ITERS + 1):
                body(*(m if m < ITERS else None for m in (n + 1, n, n - 1, n - 2)))


        LAST = STEPS * GROUPS

        def node_slot(body, base, m):
            def step(off):
                k = m - off
                if isinstance(base, int):
                    n = base * STEPS + k
                    if n < 0 or n >= LAST:
                        return None
                    return Step(n // STEPS, n % STEPS)
                return Step(base + k // STEPS, k % STEPS)
            body(step)

        def leading_slots(body):
            for m in range(LEADING):
                node_slot(body, 0, m)

        def node_slots(eng, body, tail=4):
            for m in range(LEADING, tail):
                node_slot(body, 0, m)
            with eng.Fori(0, GROUPS - 1) as i:
                for m in range(tail, tail + STEPS):
                    node_slot(body, i, m)
            for m in range(tail, tail + STEPS):
                node_slot(body, GROUPS - 1, m)

        class Step:
            def __init__(self, it, m):
                self.it, self.m, self.c, self.b = it, m, m // LIVE, m % LIVE
                self.n2 = m % 2

            def count(self, per=1, plus=0):
                return self.it * (STEPS * per) + (self.m * per + plus)

            def number(self):
                return self.count()

            def mlp_at(self, at):
                if isinstance(self.it, int) and self.it == 0 and LEADING <= self.m < LEADING + 2:
                    return at + (self.m - LEADING) * 3 * UNITS

            def closing(self):
                return isinstance(self.it, int) and self.it == GROUPS - 1 and self.b >= LIVE - CLOSING

            def early(self):
                return isinstance(self.it, int) and self.it == 0 and self.m < EARLY

            def nodes(self):
                return self.it * ((NODES - 1) * LIVE) + min(self.m + 1, (NODES - 1) * LIVE)

            def finals(self):
                return self.it * LIVE + max(0, self.m + 1 - (NODES - 1) * LIVE)

            def back(self, k):
                if self.m >= k:
                    return Step(self.it, self.m - k)
                if isinstance(self.it, int) and self.it == 0:
                    return None
                return Step(self.it - 1, self.m - k + STEPS)

            def stacks(self):
                return self.it * (16 * STACK_DMAS * NODES) + 16 * STACK_DMAS * (self.c + 1)

        def last_but_one(i, k):
            return i is None and k is not None and isinstance(k, int) and k == ITERS - 1

        def early_steps(i, k):
            return [Step(0, m) for m in range(EARLY)] if last_but_one(i, k) else []

        def ahead(step, u):
            return step(2 - u // UNITS), u % UNITS

        def score_bank(s, u):
            return bank[SBANK[(s.m * UNITS + u) % len(SBANK)]]

        def copy_unit(eng, x, u):
            pr, qt = u // KT, u % KT
            eng.wait_ge(B["pT_ps"], x.count(UNITS, u + 1))
            last = x.back(1)
            if last is not None and u in (0, 1, UNITS // 2, UNITS // 2 + 1):
                eng.wait_ge(B["pv_ok"], last.count(2, 2 * u // UNITS + 1))
            to = probT[:, 2 * pr:2 * pr + 2, :].rearrange("p h (k q) -> p h k q", k=KT)[:, :, :, qt * P:(qt + 1) * P]
            src = bank[2 + u % 2][:, :].rearrange("p (h k q) -> p h k q", h=2, k=KT)
            if u in ACT_UNITS:
                eng.activation(to, src, ACT.Copy).then_inc(B["pT_act"], 1)
            else:
                eng.tensor_copy(to, src).then_inc(B["pT_dve"], 1)

        def copies(s, upto, eng):
            mine = [u for u in range(UNITS) if (u in ACT_UNITS) == (eng == "act")]
            return s.count(len(mine), sum(u < upto for u in mine))

        def update(bb, c):
            at = (bb * 2 + c // 2) * D
            return bank[[3, 1][c % 2]][0:QK, at:at + D]

        def final_norm(eng, z):
            f = z.it * LIVE + z.b
            eng.wait_ge(B["fbn"].sem, B["fbn"].at(f))
            eng.tensor_tensor(fsm[:, 0, :], fst[:, :, 1], fst[:, :, 4], ALU.add)
            eng.tensor_tensor(fsm[:, 1, :], fst[:, :, 1], fst[:, :, 4], ALU.subtract)
            eng.tensor_tensor(fsm[:, 2, :], fst[:, :, 2], fst[:, :, 5], ALU.add).then_inc(B["fsm"].sem, 1)
            eng.wait_ge(B["fsm"].sem, B["fsm"].at(f))
            eng.tensor_tensor(fsm[:, 1, :], fsm[:, 1, :], fsm[:, 1, :], ALU.mult)
            eng.tensor_scalar(fmv, fsm[:, 0, :], 0.5, None, ALU.mult)
            eng.tensor_scalar(fsm[:, 2, :], fsm[:, 2, :], 4.0 / D, 4.0 * FFN_LN_EPS, ALU.mult, ALU.add).then_inc(B["fsd"].sem, 1)
            eng.wait_ge(B["fsd"].sem, B["fsd"].at(f))
            eng.tensor_tensor(fve, fsm[:, 2, :], fsm[:, 1, :], ALU.add).then_inc(B["fve_ok"].sem, 1)
            eng.wait_ge(B["fra"].sem, B["fra"].at(f))
            eng.tensor_tensor(frt[:, 0, :], fr, fr, ALU.mult)
            eng.tensor_scalar(frt[:, 1, :], fr, 1.5, None, ALU.mult)
            eng.tensor_scalar(frt[:, 2, :], fve, -0.125, None, ALU.mult).then_inc(B["frb"].sem, 1)
            eng.wait_ge(B["frb"].sem, B["frb"].at(f))
            eng.tensor_tensor(frt[:, 0, :], frt[:, 0, :], frt[:, 2, :], ALU.mult).then_inc(B["frc"].sem, 1)
            eng.wait_ge(B["frc"].sem, B["frc"].at(f))
            eng.tensor_tensor(frt[:, 0, :], frt[:, 0, :], fr, ALU.mult).then_inc(B["frd"].sem, 1)
            eng.wait_ge(B["frd"].sem, B["frd"].at(f))
            eng.tensor_tensor(fr, frt[:, 0, :], frt[:, 1, :], ALU.add).then_inc(B["fr_ok"].sem, 1)
            eng.wait_ge(B["fr_ok"].sem, B["fr_ok"].at(f))
            eng.tensor_tensor(fy, fy, fmv.unsqueeze(2).to_broadcast([P, KT, D]), ALU.subtract).then_inc(B["fc_ok"].sem, 1)
            eng.wait_ge(B["fc_ok"].sem, B["fc_ok"].at(f))
            eng.tensor_tensor(fy, fy, fr.unsqueeze(2).to_broadcast([P, KT, D]), ALU.mult).then_inc(B["fyn_ok"].sem, 1)

        def final_scale(eng, z):
            f = z.it * LIVE + z.b
            tiles = xall[:, ds(f * KT, KT), :]
            eng.wait_ge(B["fyn_ok"].sem, B["fyn_ok"].at(f))
            eng.tensor_tensor(fy, fy, lng[:, 0:1, :].to_broadcast([P, KT, D]), ALU.mult).then_inc(B["fg_ok"].sem, 1)
            eng.wait_ge(B["fg_ok"].sem, B["fg_ok"].at(f))
            eng.tensor_tensor(fy, fy, lng[:, 1:2, :].to_broadcast([P, KT, D]), ALU.add).then_inc(B["fb_ok"].sem, 1)
            eng.wait_ge(B["fb_ok"].sem, B["fb_ok"].at(f))
            eng.tensor_tensor(tiles, fy, tiles, ALU.add).then_inc(B["fy_free"], 1)

        block = ctx.enter_context(nc.Block())

        @block.sync
        def _(sp):
            sp.dma_start(cst[:, :], consts).then_inc(L["const_in"], 16)
            sp.dma_start(xall[:, 0:TPI, :], x_d[:, 0:TPI, :]).then_inc(L["x_first"], 16)
            sp.dma_start(cols[:, 0:1], col(a["L0_attn_attn_norm_w"])).then_inc(L["cols_in"], 16)
            sp.dma_start(cols[:, 1:2], col(a["L0_attn_mlp_norm_w"])).then_inc(L["cols_in"], 16)
            for h in range(GH):
                sp.dma_start(cols[DV * h:DV * h + DV, 2:3], col(a["L0_attn_gnorm_w"])).then_inc(L["cols_in"], 16)
            sp.dma_start(wa[:, 0:QK], a["L0_attn_Wq"]).then_inc(L["wa_in"], 16)
            sp.dma_start(wa[:, QK:2 * QK], a["L0_attn_Wk"]).then_inc(L["wa_in"], 16)
            sp.dma_start(wa[:, 2 * QK:2 * QK + D], a["L0_attn_Wv"]).then_inc(L["wa_in"], 16)
            sp.dma_start(wa[:, 2 * QK + D:], a["L0_attn_Wg"]).then_inc(L["wa_in"], 16)
            sp.dma_start(wo[:, :], a["L0_attn_Wo"]).then_inc(L["wo_in"], 16)
            sp.dma_start(wgu[:, 0, :], a["L0_attn_W_gate"]).then_inc(L["mlp_in"], 16)
            sp.dma_start(wgu[:, 1, :], a["L0_attn_W_up"]).then_inc(L["mlp_in"], 16)
            sp.dma_start(wd[:, 0:2, :], a["L0_attn_W_down"][0:256, :].rearrange("(m p) d -> p m d", p=P)).then_inc(L["mlp_in"], 16)
            sp.dma_start(wd[0:MROWS[2], 2, :], a["L0_attn_W_down"][256:MLP, :]).then_inc(L["mlp_in"], 16)
            sp.dma_start(xall[:, TPI:TILES // 2, :], x_d[:, TPI:TILES // 2, :]).then_inc(L["x_half"], 16)
            sp.dma_start(be_rows, a["L0_ffn_be"]).then_inc(L["nodew_in"], 16)
            sp.dma_start(we_raw, a["L0_ffn_We"].rearrange("e d n -> d e n")).then_inc(L["nodew_in"], 16)
            for j, w in enumerate(("Wq", "Wk", "Wv")):
                sp.dma_start(wqkv_raw[:, j, :].rearrange("p (c n) -> p c n", c=NODES),
                             a["L0_ffn_" + w].rearrange("c d n -> d c n")).then_inc(L["nodew_in"], 16)
            sp.dma_start(wo_raw, a["L0_ffn_Wo"].rearrange("c d n -> d c n")).then_inc(L["nodew_in"], 16)
            sp.dma_start(xall[:, TILES // 2:, :], x_d[:, TILES // 2:, :]).then_inc(L["x_in"], 16)

            def phase(step):
                s = step(0)
                if s is None:
                    return
                if isinstance(s.it, int) and s.it == 0 and s.m < LIVE:
                    sp.wait_ge(S["zero_ok"], s.b + 1)
                sp.wait_ge(B["lo_ok"], s.count(1, 1))
                sp.dma_start(parts[s.b], hl[s.n2][:, :, :].bitcast(F32)).then_inc(stored[s.n2], 16)
                sp.wait_ge(stored[s.n2], s.it * (16 * STEPS // 2) + 16 * (s.m // 2 + 1))
                for blk in range(PARTS):
                    kp, qp = blk % 2, blk // 2
                    rows = blk * 32
                    for odd in range(2):
                        src = parts[s.b, :, kp, 0:T].rearrange("(j s r) t -> s r j t", j=PAIRS, s=2)[odd]
                        sp.dma_start(kz[s.b][rows + 16 * odd:rows + 16 * odd + 16, odd::2, :].bitcast(F32), src)\
                            .then_inc(stacked[s.b], 16)
                    src = parts[s.b, :, qp, T:2 * T].rearrange("(j r) t -> r j t", j=PAIRS)
                    sp.dma_start(qs[s.b][rows:rows + 32, :, :].bitcast(F32), src).then_inc(stacked[s.b], 16)

            leading_slots(phase)
            node_slots(sp, phase)
            for f in range(BATCH - CLOSING, BATCH):
                sp.wait_ge(B["fy_free"], f + 2)
                sp.dma_start(out_d[f], xall[:, f * KT:(f + 1) * KT, :]).then_inc(B["last_stored"], 16)
            sp.wait_ge(B["last_stored"], 16 * CLOSING)

        @block.gpsimd
        def _(pool):
            pool.dma_start(scal[:, 0:18], a["L0_ffn_ew"].rearrange("a b -> (a b)").partition_broadcast(P)).then_inc(L["scal_in"], 16)
            pool.dma_start(scal[:, 18:24], a["L0_ffn_act_w"].partition_broadcast(P)).then_inc(L["scal_in"], 16)
            pool.dma_start(lng[:, 0, :], a["L0_ffn_ln_g"].partition_broadcast(P)).then_inc(L["ln_in"], 16)
            pool.dma_start(lng[:, 1, :], a["L0_ffn_ln_b"].partition_broadcast(P)).then_inc(L["ln_in"], 16)
            for b in range(LIVE):
                pool.memset(kz[b][:, :, :].bitcast(F32), 0.0).then_inc(S["zero_ok"], 1)
            pool.memset(eps_col[:, :], RMS_EPS).then_inc(S["eps_ok"], 1)
            pool.memset(one_col[:, :], 1.0).then_inc(S["one_ok"], 1)
            pool.memset(am, 0.0).then_inc(S["am0"], 1)

            def first(f, i, k, j):
                if k is not None:
                    pool.wait_ge(A["sg_ok"], k + 1)
                    pool.wait_ge(A["sq_ok"].sem, A["sq_ok"].at(k))
                    pool.tensor_tensor(osb, osb, sg, ALU.mult).then_inc(A["t1_ok"], 1)
                if i is not None:
                    if k is not None:
                        pool.wait_ge(A["x2_ok"].sem, A["x2_ok"].at(k))
                    pool.wait_ge(A["h_ok"], i + 1)
                    pool.tensor_tensor(xn, hh, xs.unsqueeze(2).to_broadcast([P, TPI, D]), ALU.mult).then_inc(A["xn_ok"], 1)
                if k is not None:
                    pool.wait_ge(A["rstd2_ok"].sem, A["rstd2_ok"].at(k))
                    pool.tensor_tensor(nn, x2, rr2.unsqueeze(2).to_broadcast([P, TPI, D]), ALU.mult).then_inc(A["n_ok"], 1)
                if k is not None:
                    tiles = xall[:, ds(TPI * k, TPI), :]
                    pool.tensor_tensor(tiles, x2, tiles, ALU.add).then_inc(A["res_ok"], 1)
                if f is None and i is not None:
                    pool.wait_ge(A["xT_ok"], -(-LIVE // BPI))
                    for b in range(LIVE):
                        pool.dma_start(x0T[:, b, :], xT[:, T * b:T * b + T]).then_inc(x0_in[b], 16)
                for s in early_steps(i, k):
                    split(s)
                if last_but_one(i, k):
                    for b in range(LIVE):
                        v = vaug[b].rearrange("p k (h w) -> p k h w", w=VW)
                        pool.memset(v[:, :, :, DH + 1:], 0.0)
                        pool.memset(v[:, :, :, DH:DH + 1], 1.0).then_inc(B["vones"], 1)

            def split(s):
                pool.wait_ge(B["qk_ok"], s.count(1, 1))
                old = s.back(2)
                if old is not None:
                    pool.wait_ge(stored[s.n2], old.it * (16 * STEPS // 2) + 16 * (old.m // 2 + 1))
                pool.tensor_tensor(hl[s.n2][:, 0, :], qk[s.n2], one_col[:, :].to_broadcast([P, 2 * T]), ALU.mult)\
                    .then_inc(B["hi_ok"], 1)
                pool.wait_ge(B["hi_ok"], s.count(1, 1))
                pool.tensor_tensor(hl[s.n2][:, 1, :], qk[s.n2], hl[s.n2][:, 0, :].bitcast(F32), ALU.subtract)\
                    .then_inc(B["lo_ok"], 1)
            pool.wait_ge(S["one_ok"], 1)
            slots(pool, first)

            pool.memset(fy, 0.0).then_inc(B["fy_free"], 1)

            def phase(step):
                z = step(4)
                here = z is not None and z.c == NODES - 1 and not z.closing()
                if here:
                    final_norm(pool, z)
                s = step(0)
                if s is not None and not s.early():
                    split(s)
                if s is not None and s.mlp_at(0) == 3 * UNITS:
                    pool.wait_ge(A["xT_ok"], ITERS)
                s = step(1)
                if s is not None and s.c == NODES - 1:
                    pool.wait_ge(B["qk_ps"], s.count(1, 1))
                    if not (isinstance(s.it, int) and s.it == GROUPS - 1):
                        pool.dma_start(x0T[:, s.b, :], xT[:, ds((s.it + 1) * (LIVE * T) + s.b * T, T)])\
                            .then_inc(x0_in[s.b], 16)
                if here:
                    f = z.it * LIVE + z.b
                    final_scale(pool, z)
                    pool.wait_ge(B["fy_free"], f + 2)
                    pool.dma_start(out_d[f], xall[:, ds(f * KT, KT), :]).then_inc(B["out_stored"], 16)
            pool.wait_ge(L["ln_in"], 32)
            node_slots(pool, phase)
            pool.wait_ge(B["out_stored"], 16 * (BATCH - CLOSING))

        @block.scalar
        def _(act):
            act.dma_start(wgk1, a["L0_attn_Wgk1"]).then_inc(L["gk_in"], 16)
            act.dma_start(wgk2, a["L0_attn_Wgk2"]).then_inc(L["gk_in"], 16)
            act.dma_start(bgk[:, :], a["L0_attn_bgk2"].partition_broadcast(P)).then_inc(L["gk_in"], 16)
            act.wait_ge(S["gk1_t"].sem, S["gk1_t"].at(0))
            act.activation(wgk1T, bank[6][0:RANK, 0:P], ACT.Copy).then_inc(S["gk1_c"].sem, 1)

            act.preload_act_table_set(LOGS)

            def first(f, i, k, j):
                if i is not None:
                    act.wait_ge(A["qke_ok"], i + 1)
                    for h in range(GH):
                        n = act.activation(qbd[:, h, :], qe, ACT.Copy, scale=head_mask[:, h:h + 1])
                    n.then_inc(A["qbd_ok"], 1)
                    act.wait_ge(A["keT_ps"], i + 1)
                    act.activation(keT, bank[2][:, 0:TPI * QK].rearrange("p (t k) -> p t k", t=TPI), ACT.Copy).then_inc(A["keT_ok"], 1)
                if k is not None:
                    act.wait_ge(A["x2_ok"].sem, A["x2_ok"].at(k))
                    for t in range(TPI):
                        n = act.activation(nn[:, t, :], x2[:, t, :], ACT.Square, accum_out=ss[:, t:t + 1])
                    n.then_inc(A["ss_ok"].sem, 1)
                    inverse_root(ve2, rr2, k, "ve2_ok", "r2l", "r2a")
                if f is not None:
                    inverse_root(ve, rr, f, "ve_ok", "rl", "ra")
                for s in early_steps(i, k):
                    copy_qk(s, bank[2 + s.m])
                if isinstance(i, int) and i == 0:
                    transposed_weights()
                if j is not None:
                    gate_tanh(j, 0)
                    gate_tanh(j, 1)
                if i is not None:
                    act.wait_ge(A["g_ps"], i + 1)
                    act.activation(sg, bank[0][:, :], ACT.Tanh, scale=0.5).then_inc(A["eg_ok"], 1)
                if j is not None:
                    gate_tanh(j, 2)
                if k is not None:
                    act.wait_ge(A["nT_ps"], k + 1)
                    if j is not None:
                        act.wait_ge(A["up_ps"], j * MT + MT)
                    act.activation(nT, bank[5][:, :], ACT.Copy).then_inc(A["nT_ok"], 1)
                if f is not None:
                    act.wait_ge(A["hT_ps"], f + 1)
                    act.activation(hT, bank[5][:, :], ACT.Copy).then_inc(A["hT_ok"], 1)
                act.preload_act_table_set(LOGS)
                if f is not None:
                    act.wait_ge(A["za_ok"].sem, A["za_ok"].at(f))
                    act.activation(za, za, ACT.Exp).then_inc(A["e_ok"].sem, 1)
                    act.wait_ge(A["e_ok"].sem, A["e_ok"].at(f))
                    act.activation(za, za, ACT.Ln, bias=1.0).then_inc(A["l_ok"].sem, 1)
                if i is not None:
                    act.wait_ge(A["o_ps"].sem, A["o_ps"].at(i))
                    act.activation(osb, bank[0][:, :], ACT.Copy).then_inc(A["o_ok"].sem, 1)
                    act.wait_ge(A["o_ok"].sem, A["o_ok"].at(i))
                    act.activation(sq, osb, ACT.Square).then_inc(A["sq_ok"].sem, 1)
                if j is not None:
                    inverse_root(ve3, rr3, j, "ve3_ok", "r3l", "r3a")
                if i is not None:
                    act.wait_ge(S["eps_ok"], 1)
                    act.wait_ge(A["ms_ps"].sem, A["ms_ps"].at(i))
                    act.activation(sq, bank[5][:, :], ACT.Ln, bias=eps_col[:, 0:1]).then_inc(A["msl_ok"].sem, 1)
                    act.wait_ge(A["msl_ok"].sem, A["msl_ok"].at(i))
                    act.activation(sq, sq, ACT.Exp, scale=-0.5).then_inc(A["rstd_ok"].sem, 1)
                if f is not None:
                    act.wait_ge(A["b_ps"], f + 1)
                    act.activation(eb, bank[1][:, :], ACT.Exp, scale=sign_col).then_inc(A["eb_ok"], 1)
                    act.wait_ge(A["v_ps"], f + 1)
                    act.activation(vsb, quads(4), ACT.Copy).then_inc(A["v_ok"], 1)
                if last_but_one(i, k):
                    leading_slots(phase)
                if j is not None:
                    copy_xT(j)

            def inverse_root(v, r, n, ready, log, done, sems=A, scale=1.0):
                act.wait_ge(sems[ready].sem, sems[ready].at(n))
                act.activation(r, v, ACT.Ln, scale=scale).then_inc(sems[log].sem, 1)
                act.wait_ge(sems[log].sem, sems[log].at(n))
                act.activation(r, r, ACT.Exp, scale=-0.5).then_inc(sems[done].sem, 1)

            def copy_qk(s, src):
                act.wait_ge(B["qk_ps"], s.count(1, 1))
                old = s.back(2)
                if old is not None:
                    act.wait_ge(B["lo_ok"], old.count(1, 1))
                act.activation(qk[s.n2][:, 0:T], src[:, 0:T], ACT.Identity, bias=bcol[:, s.c, 1:2])
                act.activation(qk[s.n2][:, T:2 * T], src[:, T:2 * T], ACT.Identity, bias=bcol[:, s.c, 0:1]).then_inc(B["qk_ok"], 1)

            def copy_xT(j):
                act.wait_ge(A["xT_ps"], j + 1)
                act.activation(xT[:, ds(j * TOK, TOK)], bank[mlp_bank(j, 7)][:, :], ACT.Copy).then_inc(A["xT_ok"], 1)

            def gate_tanh(j, m):
                act.wait_ge(A["gate_ps"], j * MT + m + 1)
                if m == 2:
                    act.wait_ge(A["hid_ok"], j * MT + m - 1)
                act.activation(eg[0:MROWS[m], m % 2, :], bank[mlp_bank(j, m)][0:MROWS[m], :], ACT.Tanh, scale=0.5).then_inc(A["eg2_ok"], 1)

            def transposed_weights():
                act.wait_ge(S["be_t"], 1)
                act.activation(beT, bank[5][:, 0:EDGES], ACT.Copy).then_inc(S["be_c"], 1)
                for c in range(NODES):
                    act.wait_ge(S["we_t"], c + 1)
                    if c >= 2:
                        act.wait_ge(S["fold_ps"], c - 1)
                    act.activation(weT[:, c % 2, :], bank[6 + c % 2][:, 0:3 * D], ACT.Copy).then_inc(S["we_c"], 1)

            def phase(step):
                s, x, d, z = step(0), step(2), step(3), step(4)

                def others(at):
                    place = s.mlp_at(at) if s is not None else None
                    if place is not None:
                        j = ITERS - 1
                        if place == MLP_AT["t01"]:
                            gate_tanh(j, 0)
                            gate_tanh(j, 1)
                        if place == MLP_AT["t2"]:
                            gate_tanh(j, 2)
                        if place == MLP_AT["inv"]:
                            act.preload_act_table_set(LOGS)
                            inverse_root(ve3, rr3, j, "ve3_ok", "r3l", "r3a")
                        if place == MLP_AT["c"]:
                            copy_xT(j)
                    if at == AT["a_raw"] and d is not None:
                        act.wait_ge(B["pv_ok"], d.count(2, 2))
                        last = d.back(1)
                        if last is not None:
                            act.wait_ge(B["rawT_ps"].sem, B["rawT_ps"].at(last.number()))
                        act.activation(raw, bank[4 + d.n2][:, :], ACT.Copy).then_inc(B["raw_ok"].sem, 1)
                    if at == AT["a_qk"] and s is not None and not s.early():
                        copy_qk(s, bank[6])
                    if at == AT["a_v"] and s is not None:
                        act.wait_ge(B["v_ps2"], s.count(1, 1))
                        if isinstance(s.it, int) and s.it == 0 and s.m < LIVE:
                            act.wait_ge(B["vones"], s.b + 1)
                        v = vaug[s.b].rearrange("p k (h w) -> p k h w", w=VW)
                        act.activation(v[:, :, :, 0:DH], bank[6][:, 0:T].rearrange("p (k h d) -> p k h d", k=KT, h=H),
                                       ACT.Copy).then_inc(B["vals_ok"], 1)
                    if at == AT["a_ctxT"] and d is not None:
                        act.wait_ge(B["ctxT_ps"].sem, B["ctxT_ps"].at(d.number()))
                        act.activation(ctxT[d.n2], bank[4 + d.n2][:, 0:T], ACT.Copy).then_inc(B["ctxT_ok"].sem, 1)
                    if at == AT["a_node"] and d is not None and d.c < NODES - 1:
                        act.wait_ge(B["node_ps"].sem, B["node_ps"].at(d.number()))
                        act.activation(node[:, d.b, d.c, :], bank[4 + d.n2][:, T:2 * T], ACT.Identity, bias=bcol[:, d.c, 2:3])\
                            .then_inc(B["node_ok"], 1)
                    if at == AT["a_f"] and z is not None and z.c == NODES - 1:
                        inverse_root(fve, fr, z.it * LIVE + z.b, "fve_ok", "frl", "fra", B, 0.25)

                for u in range(UNITS):
                    others(3 * u)
                    exps(*ahead(step, u + EXP_LEAD))
                    others(3 * u + 1)
                    if x is not None and u in ACT_UNITS:
                        copy_unit(act, x, u)
                    others(3 * u + 2)

            def exps(s, u):
                if s is None:
                    return
                act.wait_ge(B["max_ok"], s.count(UNITS, u + 1))
                back = s.count(UNITS, u - PROBS + 1)
                if not (isinstance(back, int) and back < 1):
                    act.wait_ge(B["pT_ps"], back)
                for k in range(2):
                    i = act.activation(prob[u % PROBS][:, k, :], score_bank(s, u)[:, k * T:(k + 1) * T], ACT.Exp, bias=mx[s.n2][:, u, k:k + 1])
                i.then_inc(B["exp_ok"], 1)
            slots(act, first)
            node_slots(act, phase)

        @block.vector
        def _(dve):
            def scale_q(c):
                return scal[:, 3 * c:3 * c + 1]

            def first(f, i, k, j):
                if k is not None:
                    dve.wait_ge(A["t1_ok"], k + 1)
                    dve.wait_ge(A["rstd_ok"].sem, A["rstd_ok"].at(k))
                    dve.tensor_tensor(uu, osb, sq, ALU.mult).then_inc(A["u_ok"].sem, 1)
                if i is not None:
                    dve.wait_ge(A["eb_ok"], i + 1)
                    dve.wait_ge(A["qkp_ps"], i + 1)
                    dve.tensor_tensor(qke, bank[2][:, :], eb, ALU.mult).then_inc(A["qke_ok"], 1)
                if k is not None:
                    dve.wait_ge(A["at_ps"].sem, A["at_ps"].at(k))
                    dve.wait_ge(A["xn_ok"], k + 1)
                    if j is not None:
                        dve.wait_ge(A["res_ok"], j + 1)
                    dve.tensor_tensor(x2, quads(5), xn, ALU.add).then_inc(A["x2_ok"].sem, 1)
                if f is not None:
                    if i is None:
                        dve.wait_ge(L["x_first"], 16)
                    elif isinstance(f, int) and f < ITERS // 2:
                        dve.wait_ge(L["x_half"], 16)
                    else:
                        dve.wait_ge(L["x_in"], 16)
                    for t in range(TPI):
                        n = dve.bn_stats(st[:, t, :], xall[:, ds(TPI * f + t, 1), :])
                    n.then_inc(A["bn1"].sem, 1)
                    moments(st, mv, sm, f, "bn1", "sm1", "sd1", "mv1")
                    dve.wait_ge(A["mv1"].sem, A["mv1"].at(f))
                    dve.tensor_scalar(ve[:, 0, :], mv[:, 1, :], LN_EPS, None, ALU.add)
                    dve.tensor_scalar(ve[:, 1, :], mv[:, 1, :], 1.0 + RMS_EPS, RMS_EPS * LN_EPS, ALU.mult, ALU.add).then_inc(A["ve_ok"].sem, 1)
                if k is not None:
                    dve.wait_ge(A["ss_ok"].sem, A["ss_ok"].at(k))
                    dve.tensor_scalar(ve2, ss, 1.0 / D, RMS_EPS, ALU.mult, ALU.add).then_inc(A["ve2_ok"].sem, 1)
                    newton(dve, ve2, rr2, rt2, k, "r2a", "r2b", "r2c", "rstd2_ok")
                if f is not None:
                    newton(dve, ve, rr, rt, f, "ra", "rb", "rc", "rstd1_ok")
                    dve.wait_ge(A["rstd1_ok"].sem, A["rstd1_ok"].at(f))
                    if i is not None:
                        dve.wait_ge(A["xn_ok"], i + 1)
                    dve.tensor_tensor(xs, rr[:, 0, :], ve[:, 1, :], ALU.mult).then_inc(A["xa_ok"], 1)
                    dve.wait_ge(A["xa_ok"], f + 1)
                    dve.tensor_tensor(xs, xs, rr[:, 1, :], ALU.mult)
                    for t in range(TPI):
                        n = dve.tensor_scalar(hh[:, t, :], xall[:, ds(TPI * f + t, 1), :].squeeze(1), mv[:, 0, t:t + 1], rr[:, 1, t:t + 1],
                                              ALU.subtract, ALU.mult)
                    n.then_inc(A["h_ok"], 1)
                    if i is None:
                        scale_first()
                if isinstance(i, int) and i == 0:
                    scale_weights()
                if j is not None:
                    silu_gate(j, 0)
                    silu_gate(j, 1)
                if i is not None:
                    scores(i, 0)
                    scores(i, 1)
                if j is not None:
                    times_up(j, 0)
                    times_up(j, 1)
                if i is not None:
                    dve.wait_ge(A["kv_ps"], 2 * i + 2)
                    for bb in range(BPI):
                        for c in range(3):
                            n = dve.scalar_tensor_tensor(kvs[:, bb, c, :], update(bb, c), ends(bb, c), state_mask, ALU.mult, ALU.mult)
                    n.then_inc(A["kvs_ok"].sem, 1)
                if j is not None:
                    silu_gate(j, 2)
                    times_up(j, 2)
                if i is not None:
                    for c, (got, did) in ((1, ("kvs_ok", "s2_ok")), (2, ("s2_ok", "s3_ok"))):
                        dve.wait_ge(A[got].sem, A[got].at(i))
                        for bb in range(BPI):
                            n = dve.scalar_tensor_tensor(kvs[:, bb, c, :], kvs[:, bb, c - 1, :], ends(bb, c), kvs[:, bb, c, :],
                                                         ALU.mult, ALU.add)
                        n.then_inc(A[did].sem, 1)
                    dve.wait_ge(A["eg_ok"], i + 1)
                    dve.scalar_tensor_tensor(sg, sg, 1.0, bank[0][:, :], ALU.add, ALU.mult).then_inc(A["sg_ok"], 1)
                if i is not None:
                    scores(i, 2)
                    scores(i, 3)
                if j is not None:
                    add_mlp(j)
                if f is not None:
                    dve.wait_ge(A["z_ps"], f + 1)
                    zps = bank[1][:, 0:TPI * QK].rearrange("p (t k) -> p t k", t=TPI)
                    dve.tensor_tensor(zb, zps, bgk[:, :].unsqueeze(1).to_broadcast([P, TPI, QK]), ALU.add).then_inc(A["zb_ok"].sem, 1)
                    dve.wait_ge(A["zb_ok"].sem, A["zb_ok"].at(f))
                    dve.scalar_tensor_tensor(za, zb, -1.0, zb, ALU.mult, ALU.min).then_inc(A["za_ok"].sem, 1)
                if j is not None:
                    x1_moments(j)
                if f is not None:
                    dve.wait_ge(A["l_ok"].sem, A["l_ok"].at(f))
                    for c in range(2):
                        n = dve.scalar_tensor_tensor(gl[:, :, c * QK:(c + 1) * QK], zb, 0.0, za, ALU.min, ALU.subtract)
                    n.then_inc(A["gl_ok"].sem, 1)
                if j is not None:
                    x1_norm(j)
                if last_but_one(i, k):
                    leading_slots(phase)

            def moments(stats, mv, t, n, got, first, second, done, A=A):
                dve.wait_ge(A[got].sem, A[got].at(n))
                dve.tensor_tensor(t[:, 0, :], stats[:, :, 1], stats[:, :, 4], ALU.add)
                dve.tensor_tensor(t[:, 1, :], stats[:, :, 1], stats[:, :, 4], ALU.subtract)
                dve.tensor_tensor(t[:, 2, :], stats[:, :, 2], stats[:, :, 5], ALU.add).then_inc(A[first].sem, 1)
                dve.wait_ge(A[first].sem, A[first].at(n))
                dve.tensor_scalar(mv[:, 0, :], t[:, 0, :], 0.5, None, ALU.mult)
                dve.scalar_tensor_tensor(t[:, 1, :], t[:, 1, :], 0.25, t[:, 1, :], ALU.mult, ALU.mult).then_inc(A[second].sem, 1)
                dve.wait_ge(A[second].sem, A[second].at(n))
                dve.scalar_tensor_tensor(mv[:, 1, :], t[:, 2, :], 1.0 / D, t[:, 1, :], ALU.mult, ALU.add).then_inc(A[done].sem, 1)

            def newton(eng, v, r, t, n, first, second, third, done, A=A):
                eng.wait_ge(A[first].sem, A[first].at(n))
                eng.tensor_tensor(t, r, r, ALU.mult).then_inc(A[second].sem, 1)
                eng.wait_ge(A[second].sem, A[second].at(n))
                eng.scalar_tensor_tensor(t, t, -0.5, v, ALU.mult, ALU.mult).then_inc(A[third].sem, 1)
                eng.wait_ge(A[third].sem, A[third].at(n))
                eng.scalar_tensor_tensor(r, t, 1.5, r, ALU.add, ALU.mult).then_inc(A[done].sem, 1)

            def ends(bb, c):
                at = bb * T + (c + 1) * CHUNK - 1
                return eb[0:QK, at:at + 1]

            def add_mlp(j):
                dve.wait_ge(A["y_ps"], j + 1)
                dve.wait_ge(A["res_ok"], j + 1)
                tiles = xall[:, ds(TPI * j, TPI), :]
                dve.tensor_tensor(tiles, quads(mlp_bank(j, 6)), tiles, ALU.add).then_inc(A["x1_ok"], 1)
                dve.wait_ge(L["x_in"], 16)
                dve.wait_ge(A["x1_ok"], j + 1)
                for t in range(TPI):
                    n = dve.bn_stats(st2[:, t, :], xall[:, ds(TPI * j + t, 1), :])
                n.then_inc(A["bn2"].sem, 1)

            def x1_moments(j):
                moments(st2, mv2, sm2, j, "bn2", "sm2", "sd2", "mv2")
                dve.wait_ge(A["mv2"].sem, A["mv2"].at(j))
                dve.tensor_scalar(ve3, mv2[:, 1, :], LN_EPS, None, ALU.add).then_inc(A["ve3_ok"].sem, 1)

            def x1_norm(j):
                newton(dve, ve3, rr3, rt3, j, "r3a", "r3b", "r3c", "rstd3_ok")
                dve.wait_ge(A["rstd3_ok"].sem, A["rstd3_ok"].at(j))
                for t in range(TPI):
                    n = dve.tensor_scalar(x1n[:, t, :], xall[:, ds(TPI * j + t, 1), :].squeeze(1), mv2[:, 0, t:t + 1], rr3[:, t:t + 1],
                                          ALU.subtract, ALU.mult)
                n.then_inc(A["xn2_ok"], 1)

            def silu_gate(j, m):
                n = MROWS[m]
                dve.wait_ge(A["eg2_ok"], j * MT + m + 1)
                dve.scalar_tensor_tensor(eg[0:n, m % 2, :], eg[0:n, m % 2, :], 1.0, bank[mlp_bank(j, m)][0:n, :], ALU.add, ALU.mult)\
                    .then_inc(A["si_ok"], 1)

            def times_up(j, m):
                n = MROWS[m]
                dve.wait_ge(A["up_ps"], j * MT + m + 1)
                dve.wait_ge(A["si_ok"], j * MT + m + 1)
                dve.tensor_tensor(hid[0:n, m, :], bank[mlp_bank(j, MT + m)][0:n, :], eg[0:n, m % 2, :], ALU.mult).then_inc(A["hid_ok"], 1)

            def scores(i, t):
                dve.wait_ge(S["am0"], 1)
                dve.wait_ge(a_ps[t], i + 1)
                dve.copy_predicated(am[:, t, :], causal, bank[[4, 2][t % 2]][:, :]).then_inc(A["am_ok"], 1)

            def scale_first():
                dve.wait_ge(L["cols_in"], 16 * 6)
                dve.wait_ge(L["wa_in"], 64)
                dve.tensor_scalar(wa[:, 0:QK], wa[:, 0:QK], cols[:, 0:1], float(DK) ** -0.5, ALU.mult, ALU.mult)
                dve.tensor_scalar(wa[:, QK:], wa[:, QK:], cols[:, 0:1], None, ALU.mult)
                dve.wait_ge(S["gk_ps"].sem, S["gk_ps"].at(0))
                dve.tensor_scalar(wz[:, :], bank[6][:, 128:128 + QK], cols[:, 0:1], None, ALU.mult).then_inc(S["wa_ok"], 1)

            def scale_weights():
                dve.wait_ge(L["wo_in"], 16)
                dve.tensor_scalar(wo[:, :], wo[:, :], cols[:, 2:3], 0.5, ALU.mult, ALU.mult)
                dve.wait_ge(L["mlp_in"], 64)
                dve.tensor_scalar(wgu[:, 0, :], wgu[:, 0, :], cols[:, 1:2], None, ALU.mult)
                dve.tensor_scalar(wgu[:, 1, :], wgu[:, 1, :], cols[:, 1:2], 0.5, ALU.mult, ALU.mult)
                dve.wait_ge(L["scal_in"], 32)
                dve.wait_ge(L["nodew_in"], 16 * 6)
                for c in range(NODES):
                    dve.tensor_scalar(w_res[:, c, :], we_raw[:, GRAPH[c]["e"][0], :], scale_q(c), None, ALU.mult)
                    dve.tensor_scalar(w_out[:, c, :], wo_raw[:, c, :], scal[:, 18 + c:19 + c], None, ALU.mult)
                for c in range(NODES):
                    dve.wait_ge(S["fold_ps"], c + 1)
                    src = bank[3 + c % 2]
                    dve.tensor_scalar(w_fold[:, c, 0, :], src[:, 0:D], scale_q(c), float(DH) ** -0.5, ALU.mult, ALU.mult)
                    for j in range(1, 3):
                        k = dve.tensor_scalar(w_fold[:, c, j, :], src[:, j * D:(j + 1) * D], scal[:, 3 * c + j:3 * c + j + 1], None, ALU.mult)
                    k.then_inc(S["fold_ok"], 1)

            def biases():
                ew = scal[:, 0:18].rearrange("p (c j) -> p c j", j=3)
                dve.wait_ge(S["bias_ps"].sem, S["bias_ps"].at(0))
                bp = bank[6][:, 0:3 * NODES].rearrange("p (c j) -> p c j", j=3)
                dve.tensor_tensor(bprod[:, :, 0:3], bp, ew, ALU.mult).then_inc(S["bias_c"].sem, 1)
                dve.wait_ge(S["bias_c"].sem, S["bias_c"].at(0))
                dve.tensor_scalar(bcol[:, :, 0:1], bprod[:, :, 0:1], float(DH) ** -0.5, None, ALU.mult)
                dve.tensor_copy(bcol[:, :, 1:2], bprod[:, :, 1:2])
                dve.wait_ge(S["be_c"], 1)
                for c in range(NODES):
                    e = GRAPH[c]["e"][0]
                    k = dve.tensor_tensor(bprod[:, c, 3:4], beT[:, e:e + 1], scale_q(c), ALU.mult)
                k.then_inc(S["bias_w"], 1)

            def node_biases():
                dve.wait_ge(S["bo_ps"].sem, S["bo_ps"].at(0))
                dve.tensor_tensor(bcol[:, :, 2:3], bank[7][:, 0:NODES].unsqueeze(2), scal[:, 18:24].unsqueeze(2), ALU.mult)\
                    .then_inc(S["bo_ok"].sem, 1)
                dve.wait_ge(S["bo_ok"].sem, S["bo_ok"].at(0))
                dve.wait_ge(S["bias_w"], 1)
                dve.tensor_tensor(bcol[:, :, 2:3], bcol[:, :, 2:3], bprod[:, :, 3:4], ALU.add).then_inc(S["bias_f"].sem, 1)
                dve.wait_ge(S["bias_f"].sem, S["bias_f"].at(0))
                dve.tensor_copy(nb5w, bcol[:, NODES - 1, 2:3].to_broadcast([P, D])).then_inc(S["nb_b"].sem, 1)

            def last_bias():
                dve.wait_ge(S["nb_ps"].sem, S["nb_ps"].at(0))
                dve.tensor_copy(nb5[:, :], bank[6][:, 256:256 + D]).then_inc(S["prep_d"], 1)

            def phase(step):
                s, x, d, z = step(0), step(2), step(3), step(4)
                if z is not None and z.c == NODES - 1 and z.closing():
                    dve.wait_ge(L["ln_in"], 32)
                    final_norm(dve, z)
                    final_scale(dve, z)

                def others(at):
                    place = s.mlp_at(at) if s is not None else None
                    if place is not None:
                        j = ITERS - 1
                        if place == MLP_AT["s01"]:
                            silu_gate(j, 0)
                            silu_gate(j, 1)
                        if place == MLP_AT["h01"]:
                            times_up(j, 0)
                            times_up(j, 1)
                        if place == MLP_AT["s2"]:
                            silu_gate(j, 2)
                            times_up(j, 2)
                        if place == MLP_AT["x1"]:
                            add_mlp(j)
                        if place == MLP_AT["mom"]:
                            x1_moments(j)
                        if place == MLP_AT["x1n"]:
                            x1_norm(j)
                    if at == AT["d_ctx"] and d is not None:
                        dve.wait_ge(B["rawT_ps"].sem, B["rawT_ps"].at(d.number()))
                        t = bank[4 + d.n2][:, :].rearrange("p (a w) -> p a w", w=VW)
                        dve.reciprocal(rec, t[:, :, DH]).then_inc(B["rec_ok"].sem, 1)
                        last = d.back(1)
                        if last is not None:
                            dve.wait_ge(B["ctxT_ps"].sem, B["ctxT_ps"].at(last.number()))
                        dve.wait_ge(B["rec_ok"].sem, B["rec_ok"].at(d.number()))
                        dve.tensor_tensor(ctxc.rearrange("p t (h d) -> p (t h) d", h=H), t[:, :, 0:DH],
                                          rec.unsqueeze(2).to_broadcast([P, KT * H, DH]), ALU.mult).then_inc(B["ctxc_ok"].sem, 1)
                    if d is not None and d.c == NODES - 1:
                        f = d.it * LIVE + d.b
                        if at == AT["f0"]:
                            dve.wait_ge(B["node_ps"].sem, B["node_ps"].at(d.number()))
                            dve.wait_ge(B["fy_free"], f + 1)
                            dve.tensor_tensor(fy, bank[4 + d.n2][:, T:2 * T].rearrange("p (t d) -> p t d", t=KT),
                                              nb5[:, :].unsqueeze(1).to_broadcast([P, KT, D]), ALU.add).then_inc(B["fin_read"].sem, 1)
                            dve.wait_ge(B["fin_read"].sem, B["fin_read"].at(f))
                            for t in range(KT):
                                k = dve.bn_stats(fst[:, t, :], fy[:, t, :])
                            k.then_inc(B["fbn"].sem, 1)

                for u in range(UNITS):
                    others(3 * u)
                    maxes(*ahead(step, u + MAX_LEAD))
                    others(3 * u + 1)
                    if x is not None and u not in ACT_UNITS:
                        copy_unit(dve, x, u)
                    others(3 * u + 2)

            def maxes(s, u):
                if s is None:
                    return
                dve.wait_ge(B["s_ps"], s.count(UNITS, u + 1))
                dve.tensor_reduce(mx[s.n2][:, u, :], score_bank(s, u)[:, :].rearrange("p (h k) -> p h k", h=2), AX_X, ALU.max,
                                  negate=True).then_inc(B["max_ok"], 1)
            slots(dve, first, {0: biases, 1: node_biases, 2: last_bias})
            node_slots(dve, phase)

        @block.tensor
        def _(pe):
            def mm(o, w, x, start=True, stop=True, skip=False):
                return pe.matmul(o, w, x, start=start, stop=stop, skip_group_check=skip)

            pe.wait_ge(L["const_in"], 16)
            pe.wait_ge(L["gk_in"], 48)
            pe.transpose(bank[6][0:RANK, 0:P], wgk1, ident).then_inc(S["gk1_t"].sem, 1)
            pe.wait_ge(S["gk1_c"].sem, S["gk1_c"].at(0))
            mm(bank[6][:, 128:128 + QK], wgk1T, wgk2).then_inc(S["gk_ps"].sem, 1)

            def first(f, i, k, j):
                if j is not None:
                    pe.wait_ge(A["nT_ok"], j + 1)
                    gate(j, 0)
                if k is not None:
                    pe.wait_ge(A["u_ok"].sem, A["u_ok"].at(k))
                    for t in range(TPI):
                        n = mm(bank[5][:, t * P:(t + 1) * P], uu[:, t * P:(t + 1) * P], wo[:, :])
                    n.then_inc(A["at_ps"].sem, 1)
                for s in early_steps(i, k):
                    project_qk(s, bank[2 + s.m])
                if i is not None:
                    pe.wait_ge(A["qke_ok"], i + 1)
                    mm(bank[0][:, :], wa[:, 2 * QK + D:], hT).then_inc(A["g_ps"], 1)
                    for t in range(TPI):
                        n = pe.transpose(bank[2][:, t * QK:(t + 1) * QK], ke[:, t * P:(t + 1) * P], ident[QK:2 * QK, QK:2 * QK])
                    n.then_inc(A["keT_ps"], 1)
                if j is not None:
                    if not (isinstance(j, int) and j == 0):
                        pe.wait_ge(A["xT_ok"], j)
                    gate(j, 1)
                if isinstance(i, int) and i == 0:
                    fold_weights()
                if i is not None:
                    pe.wait_ge(L["const_in"], 16)
                    pe.wait_ge(A["keT_ok"], i + 1)
                    pe.wait_ge(A["v_ok"], i + 1)
                    for odd in range(2):
                        r = CHUNK * odd
                        for bb in range(BPI):
                            for c in range(odd, 3, 2):
                                t = bb * KT + c // 2
                                n = mm(update(bb, c), keT[r:r + CHUNK, t, :], vsb[r:r + CHUNK, t, :])
                        n.then_inc(A["kv_ps"], 1)
                    pe.wait_ge(A["qbd_ok"], i + 1)
                    for t in range(2):
                        heads_scores(i, t)
                if k is not None:
                    pe.wait_ge(A["n_ok"], k + 1)
                    for t in range(TPI):
                        n = pe.transpose(bank[5][:, t * P:(t + 1) * P], nn[:, t, :], ident)
                    n.then_inc(A["nT_ps"], 1)
                if j is not None:
                    for m in range(2):
                        pe.wait_ge(A["si_ok"], j * MT + m + 1)
                        up(j, m)
                    pe.wait_ge(A["hid_ok"], j * MT + 1)
                    gate(j, 2)
                    pe.wait_ge(A["hid_ok"], j * MT + 2)
                    up(j, 2)
                if i is not None:
                    for t in range(2, TPI):
                        pe.wait_ge(A["am_ok"], TPI * i + t - 1)
                        heads_scores(i, t)
                if f is not None:
                    pe.wait_ge(A["h_ok"], f + 1)
                    if k is not None:
                        pe.wait_ge(A["nT_ok"], k + 1)
                    for t in range(TPI):
                        n = pe.transpose(bank[5][:, t * P:(t + 1) * P], hh[:, t, :], ident)
                    n.then_inc(A["hT_ps"], 1)
                if j is not None:
                    mlp_out(j)
                if f is not None:
                    pe.wait_ge(A["hT_ok"], f + 1)
                    if i is not None:
                        pe.wait_ge(A["kvs_ok"].sem, A["kvs_ok"].at(i))
                    if i is None:
                        pe.wait_ge(S["wa_ok"], 1)
                    for t in range(TPI):
                        n = mm(bank[1][:, t * QK:(t + 1) * QK], hT[:, t * P:(t + 1) * P], wz[:, :])
                    n.then_inc(A["z_ps"], 1)
                if i is not None:
                    pe.wait_ge(A["sg_ok"], i + 1)
                    pe.wait_ge(A["s3_ok"].sem, A["s3_ok"].at(i))
                    for t in range(TPI):
                        pe.wait_ge(A["am_ok"], TPI * i + t + 1)
                        for h in range(GH):
                            mm(bank[0][DV * h:DV * h + DV, t * P:(t + 1) * P], vsb[:, t, DV * h:DV * h + DV],
                               am[:, t, h * P:(h + 1) * P], stop=False, skip=True)
                        for cc in range(2):
                            c = 2 * (t % KT) + cc
                            if c > 0:
                                at = t * P + cc * CHUNK
                                n = mm(bank[0][:, at:at + CHUNK], kvs[:, t // KT, c - 1, :], qe[:, at:at + CHUNK],
                                       start=False, skip=True)
                    n.then_inc(A["o_ps"].sem, 1)
                if f is not None:
                    mm(bank[2][:, :], wa[:, 0:2 * QK], hT).then_inc(A["qkp_ps"], 1)
                    for t in range(TPI):
                        n = mm(bank[4][:, t * P:(t + 1) * P], hT[:, t * P:(t + 1) * P], wa[:, 2 * QK:2 * QK + D])
                    n.then_inc(A["v_ps"], 1)
                if i is not None:
                    pe.wait_ge(A["sq_ok"].sem, A["sq_ok"].at(i))
                    mm(bank[5][:, :], mean_dv, sq).then_inc(A["ms_ps"].sem, 1)
                if f is not None:
                    pe.wait_ge(A["gl_ok"].sem, A["gl_ok"].at(f))
                    for t in range(TPI):
                        n = mm(bank[1][:, t * P:(t + 1) * P], gl[:, t, :], cum)
                    n.then_inc(A["b_ps"], 1)
                if last_but_one(i, k):
                    pe.wait_ge(A["x1_ok"], j + 1)
                    leading_slots(phase)
                if j is not None:
                    transpose_x1(j)

            def mlp_out(j):
                pe.wait_ge(A["si_ok"], j * MT + MT)
                for m in range(MT):
                    if m == MT - 1:
                        pe.wait_ge(A["hid_ok"], j * MT + MT)
                    for t in range(TPI):
                        n = mm(bank[mlp_bank(j, 6)][:, t * P:(t + 1) * P], hid[0:MROWS[m], m, t * P:(t + 1) * P], wd[0:MROWS[m], m, :],
                               start=(m == 0 and t == 0), stop=(m == MT - 1), skip=True)
                n.then_inc(A["y_ps"], 1)

            def transpose_x1(j):
                pe.wait_ge(A["xn2_ok"], j + 1)
                for t in range(TPI):
                    n = pe.transpose(bank[mlp_bank(j, 7)][:, t * P:(t + 1) * P], x1n[:, t, :], ident)
                n.then_inc(A["xT_ps"], 1)

            def source(s, n):
                return x0T[:, s.b, :] if n < 0 else node[:, s.b, n, :]

            def project_qk(s, to):
                g = GRAPH[s.c]["src"]
                pe.wait_ge(x0_in[s.b], 16 * s.it + 16)
                if s.c > 0:
                    pe.wait_ge(B["node_ok"], s.back(LIVE).nodes())
                mm(to[:, 0:T], w_fold[:, s.c, 1, :], source(s, g[1]))
                mm(to[:, T:2 * T], w_fold[:, s.c, 0, :], source(s, g[0])).then_inc(B["qk_ps"], 1)

            def heads_scores(i, t):
                mm(bank[[4, 2][t % 2]][:, :].rearrange("p (h c) -> p h c", h=GH), ke[:, t * P:(t + 1) * P],
                   qbd[:, :, t * P:(t + 1) * P]).then_inc(a_ps[t], 1)

            def gate(j, m):
                mm(bank[mlp_bank(j, m)][0:MROWS[m], :], wgu[:, 0, m * P:m * P + MROWS[m]], nT).then_inc(A["gate_ps"], 1)

            def up(j, m):
                mm(bank[mlp_bank(j, MT + m)][0:MROWS[m], :], wgu[:, 1, m * P:m * P + MROWS[m]], nT).then_inc(A["up_ps"], 1)

            w3 = wqkv_raw.rearrange("p j (c n) -> p j c n", c=NODES)

            def fold_weights():
                pe.wait_ge(L["nodew_in"], 16 * 6)
                pe.transpose(bank[5][:, 0:EDGES], be_rows, ident[0:EDGES, 0:EDGES]).then_inc(S["be_t"], 1)
                for c in range(NODES + 1):
                    if c < NODES:
                        if c >= 2:
                            pe.wait_ge(S["we_c"], c - 1)
                        for j in range(3):
                            k = pe.transpose(bank[6 + c % 2][:, j * D:(j + 1) * D], we_raw[:, GRAPH[c]["e"][j], :], ident)
                        k.then_inc(S["we_t"], 1)
                    if c >= 1:
                        b = c - 1
                        pe.wait_ge(S["we_c"], b + 1)
                        if b >= 2:
                            pe.wait_ge(S["fold_ok"], b - 1)
                        for j in range(3):
                            k = mm(bank[3 + b % 2][:, j * D:(j + 1) * D], weT[:, b % 2, j * D:(j + 1) * D], w3[:, j, b, :])
                        k.then_inc(S["fold_ps"], 1)
                pe.wait_ge(S["fold_ok"], NODES)
                pe.wait_ge(S["be_c"], 1)

            def biases():
                for c in range(NODES):
                    for j in range(3):
                        e = GRAPH[c]["e"][j]
                        k = mm(bank[6][:, 3 * c + j:3 * c + j + 1], w3[:, j, c, :], beT[:, e:e + 1])
                k.then_inc(S["bias_ps"].sem, 1)

            def node_biases():
                pe.wait_ge(S["bias_c"].sem, S["bias_c"].at(0))
                for c in range(NODES):
                    k = mm(bank[7][:, c:c + 1], wo_raw[:, c, :], bprod[:, c, 2:3])
                k.then_inc(S["bo_ps"].sem, 1)

            def last_bias():
                pe.wait_ge(S["nb_b"].sem, S["nb_b"].at(0))
                mm(bank[6][:, 256:256 + D], nb5w, ident).then_inc(S["nb_ps"].sem, 1)
                pe.wait_ge(S["prep_d"], 1)

            def pv(s, g):
                upto = UNITS // 2 * (g + 1)
                pe.wait_ge(B["pT_dve"], copies(s, upto, "dve"))
                pe.wait_ge(B["pT_act"], copies(s, upto, "act"))
                if g == 0:
                    pe.wait_ge(B["vals_ok"], s.count(1, 1))
                    old = s.back(2)
                    if old is None and s.m == 0:
                        pe.wait_ge(A["x1_ok"], ITERS)
                    elif old is None:
                        pe.wait_ge(A["xT_ok"], ITERS)
                    elif old.c < NODES - 1:
                        pe.wait_ge(B["node_ok"], old.nodes())
                    else:
                        pe.wait_ge(B["fin_read"].sem, B["fin_read"].at(old.finals() - 1))
                for kt in range(KT):
                    for j in range(GCOL):
                        h = g * GCOL + j
                        k = mm(bank[4 + s.n2][32 * j:32 * j + 32, g * T:(g + 1) * T], vaug[s.b][:, kt, VW * h:VW * h + VW],
                               probT[:, h, kt * T:(kt + 1) * T], start=(kt == 0), stop=(kt == KT - 1), skip=True)
                k.then_inc(B["pv_ok"], 1)

            def phase(step):
                s, x, d = step(0), step(2), step(3)

                def others(at):
                    place = s.mlp_at(at) if s is not None else None
                    if place is not None:
                        j = ITERS - 1
                        if place == MLP_AT["g01"]:
                            pe.wait_ge(A["nT_ok"], j + 1)
                            pe.wait_ge(A["xT_ok"], j)
                            gate(j, 0)
                            gate(j, 1)
                        if place == MLP_AT["u01"]:
                            for m in range(2):
                                pe.wait_ge(A["si_ok"], j * MT + m + 1)
                                up(j, m)
                        if place == MLP_AT["g2"]:
                            pe.wait_ge(A["hid_ok"], j * MT + 1)
                            gate(j, 2)
                            pe.wait_ge(A["hid_ok"], j * MT + 2)
                            up(j, 2)
                        if place == MLP_AT["y"]:
                            mlp_out(j)
                        if place == MLP_AT["xT"]:
                            transpose_x1(j)
                    if at == AT["pv1"] and d is not None:
                        pv(d, 1)
                    if at == AT["qk"] and s is not None and not s.early():
                        pe.wait_ge(B["vals_ok"], s.back(1).count(1, 1))
                        project_qk(s, bank[6])
                    if at == AT["rawT"] and d is not None:
                        pe.wait_ge(B["raw_ok"].sem, B["raw_ok"].at(d.number()))
                        for qt in range(KT):
                            for g in range(2):
                                a = (qt * 2 + g) * P
                                k = pe.transpose(bank[4 + d.n2][:, a:a + P], raw[:, g * T + qt * P:g * T + (qt + 1) * P], ident)
                        k.then_inc(B["rawT_ps"].sem, 1)
                    if at == AT["v"] and s is not None:
                        pe.wait_ge(B["qk_ok"], s.count(1, 1))
                        if s.early() and s.m > 0:
                            pe.wait_ge(B["vals_ok"], s.back(1).count(1, 1))
                        for kt in range(KT):
                            k = mm(bank[6][:, kt * P:(kt + 1) * P], source(s, GRAPH[s.c]["src"][2])[:, kt * P:(kt + 1) * P], w_fold[:, s.c, 2, :])
                        k.then_inc(B["v_ps2"], 1)
                    if at == AT["ctxT"] and d is not None:
                        pe.wait_ge(B["ctxc_ok"].sem, B["ctxc_ok"].at(d.number()))
                        for qt in range(KT):
                            k = pe.transpose(bank[4 + d.n2][:, qt * P:(qt + 1) * P], ctxc[:, qt, :], ident)
                        k.then_inc(B["ctxT_ps"].sem, 1)
                    if at == AT["proj"] and d is not None:
                        project(d)
                    if at == AT["pv0"] and x is not None:
                        pv(x, 0)

                for u in range(UNITS):
                    others(3 * u)
                    transposes(x, u)
                    others(3 * u + 1)
                    scores(*ahead(step, u + S_LEAD))
                    others(3 * u + 2)

            def transposes(x, u):
                if x is None:
                    return
                pe.wait_ge(B["exp_ok"], x.count(UNITS, u + 1))
                if u >= 2 or x.back(1) is not None:
                    w, v = (x, u - 2) if u >= 2 else (x.back(1), u + UNITS - 2)
                    e = "act" if v in ACT_UNITS else "dve"
                    pe.wait_ge(B["pT_" + e], copies(w, v + 1, e))
                for k in range(2):
                    for kt in range(KT):
                        o = (k * KT + kt) * P
                        i = pe.transpose(bank[2 + u % 2][:, o:o + P], prob[u % PROBS][:, k, kt * P:(kt + 1) * P], ident)
                i.then_inc(B["pT_ps"], 1)

            def scores(s, u):
                if s is None:
                    return
                pr, qt = u // KT, u % KT
                if u == 0:
                    pe.wait_ge(stacked[s.b], s.stacks())
                back = s.count(UNITS, u - len(SBANK) + 1)
                if not (isinstance(back, int) and back < 1):
                    pe.wait_ge(B["exp_ok"], back)
                mm(score_bank(s, u)[:, :].rearrange("p (h k) -> p h k", h=2), qs[s.b][:, pr, qt * P:(qt + 1) * P],
                   kz[s.b][:, 2 * pr:2 * pr + 2, :]).then_inc(B["s_ps"], 1)

            def project(d):
                to, prev, ctx_n = bank[4 + d.n2], source(d, GRAPH[d.c]["src"][0]), ctxT[d.n2]
                pe.wait_ge(B["ctxT_ok"].sem, B["ctxT_ok"].at(d.number()))
                if d.c < NODES - 1:
                    mm(to[:, T:2 * T], w_res[:, d.c, :], prev, stop=False)
                    mm(to[:, T:2 * T], w_out[:, d.c, :], ctx_n, start=False).then_inc(B["node_ps"].sem, 1)
                else:
                    for t in range(KT):
                        r, o = slice(t * P, (t + 1) * P), slice(T + t * P, T + (t + 1) * P)
                        mm(to[:, o], prev[:, r], w_res[:, d.c, :], stop=False)
                        k = mm(to[:, o], ctx_n[:, r], w_out[:, d.c, :], start=False)
                    k.then_inc(B["node_ps"].sem, 1)

            slots(pe, first, {0: biases, 1: node_biases, 2: last_bias})
            node_slots(pe, phase)


_INS = ['L0_attn_hidden_states', 'L0_attn_attn_norm_w', 'L0_attn_Wq', 'L0_attn_Wk', 'L0_attn_Wv', 'L0_attn_Wg', 'L0_attn_Wgk1',
        'L0_attn_Wgk2', 'L0_attn_bgk2', 'L0_attn_gnorm_w', 'L0_attn_Wo', 'L0_attn_mlp_norm_w', 'L0_attn_W_gate', 'L0_attn_W_up',
        'L0_attn_W_down', 'L0_ffn_ew', 'L0_ffn_act_w', 'L0_ffn_We', 'L0_ffn_be', 'L0_ffn_Wq', 'L0_ffn_Wk', 'L0_ffn_Wv',
        'L0_ffn_Wo', 'L0_ffn_ln_g', 'L0_ffn_ln_b']


def kernel(**inputs):
    import concourse.bacc as _bacc
    from concourse.bass_utils import run_bass_kernel_spmd as _run

    nc = _bacc.Bacc("TRN2", target_bir_lowering=False, num_devices=1)
    arrays, aps = {}, {}
    for name in _INS:
        v = np.ascontiguousarray(inputs[name])
        arrays[f"in_{name}"] = v
        aps[name] = nc.dram_tensor(f"in_{name}", v.shape, mybir.dt.from_np(v.dtype), kind="ExternalInput").ap()
    arrays["in_constants"] = constants()
    consts = nc.dram_tensor("in_constants", (P, C_END), F32, kind="ExternalInput").ap()
    out = nc.dram_tensor("out_0", (BATCH, T, D), F32, kind="ExternalOutput").ap()
    build(nc, aps, consts, out)
    r = _run(nc, [arrays], core_ids=[0])
    return r.results[0]["out_0"]
```
